# Optimizing a Trainium2 kernel written in Bass

```python
import numpy as np
import jax
import jax.numpy as jnp

def _softmax(x, axis=-1):
    return jax.nn.softmax(x, axis=axis)

def _gelu(x):
    return jax.nn.gelu(x, approximate=True)

def _silu(x):
    return jax.nn.silu(x)

def _sigmoid(x):
    return jax.nn.sigmoid(x)

def _layernorm(x, axis=-1, eps=1e-05):
    m = jnp.mean(x, axis=axis, keepdims=True)
    v = jnp.var(x, axis=axis, keepdims=True)
    return (x - m) / jnp.sqrt(v + eps)

def _scatter_add(tgt, idx, src, axis=0):
    return tgt.at[idx].add(src)

def _segment_sum(src, seg, n):
    return jax.ops.segment_sum(src, seg, n)
kernel_name = 'mk_adj_ffn_d1_adj_r2_0b26ac'

def setup_inputs(seed: int=0):
    np.random.seed(seed)
    _w = jnp.asarray

    def _rec_inputs():
        import jax
        import jax.numpy as jnp
        _gk = jax.random.key(seed)
        x = -0.0002928 + 1 * jax.random.normal(jax.random.fold_in(_gk, 1), (8, 1024, 128), jnp.float32)
        _w = (1.0 + jnp.arange(1024, dtype=jnp.float32)) ** (-0.5)
        _w = _w / _w.mean()
        _pij = jnp.clip(0.0078125 * _w[:, None] * _w[None, :], 0.0, 1.0)
        _a = jax.random.uniform(jax.random.fold_in(_gk, 2), (8, 1024, 1024)) < _pij
        adj = _a.astype(jnp.int32)
        return (x, adj)
    x, adj = _rec_inputs()

    def _L0_gnn_setup():
        import jax, jax.numpy as jnp
        import numpy as np
        B, N, DIN, DOUT = (16, 512, 128, 128)
        NEG_SLOPE = 0.2
        key = jax.random.key(seed)
        k1, k2, k3, k4 = jax.random.split(key, 4)
        h = jax.random.normal(k1, (B, N, DIN), dtype=jnp.float32)
        adj_mask = jax.random.randint(k2, (B, N, N), 0, 2, dtype=jnp.int32)
        W = jax.random.normal(k3, (DOUT, DIN), dtype=jnp.float32) * (1.0 / np.sqrt(DIN))
        a = jax.random.normal(k4, (2 * DOUT,), dtype=jnp.float32) * (1.0 / np.sqrt(2 * DOUT))
        return {'h': h, 'adj_mask': adj_mask, 'W': W, 'a': a}
    _L0_gnn_all = _L0_gnn_setup()
    _L0_gnn_in = {k: v for k, v in _L0_gnn_all.items() if k in ('W', 'a')}
    del _L0_gnn_all

    def _L0_ffn_setup():
        import jax, jax.numpy as jnp
        import numpy as np
        B, S, D, F, E, K = (8, 1024, 128, 512, 8, 2)
        key = jax.random.key(seed)
        ks = jax.random.split(key, 10)
        s = 0.02
        return {'x': jax.random.normal(ks[0], (B, S, D), dtype=jnp.float32), 'Wr': jax.random.normal(ks[1], (D, E), dtype=jnp.float32) * s, 'W1s': jax.random.normal(ks[2], (D, F), dtype=jnp.float32) * s, 'b1s': jnp.zeros((F,), dtype=jnp.float32), 'W2s': jax.random.normal(ks[3], (F, D), dtype=jnp.float32) * s, 'b2s': jnp.zeros((D,), dtype=jnp.float32), 'W1p': jax.random.normal(ks[4], (E, D, F), dtype=jnp.float32) * s, 'b1p': jnp.zeros((E, F), dtype=jnp.float32), 'W2p': jax.random.normal(ks[5], (E, F, D), dtype=jnp.float32) * s, 'b2p': jnp.zeros((E, D), dtype=jnp.float32)}
    _L0_ffn_all = _L0_ffn_setup()
    _L0_ffn_in = {k: v for k, v in _L0_ffn_all.items() if k in ('Wr', 'W1s', 'b1s', 'W2s', 'b2s', 'W1p', 'b1p', 'W2p', 'b2p')}
    del _L0_ffn_all
    return {'x': x, 'adj': adj, 'L0_gnn_W': _L0_gnn_in['W'], 'L0_gnn_a': _L0_gnn_in['a'], 'L0_ffn_Wr': _L0_ffn_in['Wr'], 'L0_ffn_W1s': _L0_ffn_in['W1s'], 'L0_ffn_b1s': _L0_ffn_in['b1s'], 'L0_ffn_W2s': _L0_ffn_in['W2s'], 'L0_ffn_b2s': _L0_ffn_in['b2s'], 'L0_ffn_W1p': _L0_ffn_in['W1p'], 'L0_ffn_b1p': _L0_ffn_in['b1p'], 'L0_ffn_W2p': _L0_ffn_in['W2p'], 'L0_ffn_b2p': _L0_ffn_in['b2p']}

def reference(x, adj, L0_gnn_W, L0_gnn_a, L0_ffn_Wr, L0_ffn_W1s, L0_ffn_b1s, L0_ffn_W2s, L0_ffn_b2s, L0_ffn_W1p, L0_ffn_b1p, L0_ffn_W2p, L0_ffn_b2p):
    import jax
    import jax.numpy as jnp

    def _L0_gnn_ref(h, adj_mask, W, a):
        import jax, jax.numpy as jnp
        import numpy as np
        B, N, DIN, DOUT = (16, 512, 128, 128)
        NEG_SLOPE = 0.2
        Wh = jnp.einsum('bnd,od->bno', h, W)
        d = Wh.shape[-1]
        a1, a2 = (a[:d], a[d:])
        ei = Wh @ a1
        ej = Wh @ a2
        e = ei[:, :, None] + ej[:, None, :]
        e = jnp.where(e > 0, e, NEG_SLOPE * e)
        e = jnp.where(adj_mask == 0, -jnp.inf, e)
        alpha = jax.nn.softmax(e, axis=-1)
        alpha = jnp.where(jnp.isnan(alpha), 0.0, alpha)
        h_out = jnp.einsum('bij,bjo->bio', alpha, Wh)
        return h_out

    def _L0_ffn_ref(x, Wr, W1s, b1s, W2s, b2s, W1p, b1p, W2p, b2p):
        import jax, jax.numpy as jnp
        import numpy as np
        B, S, D, F, E, K = (8, 1024, 128, 512, 8, 2)
        gelu = lambda t: jax.nn.gelu(t, approximate=False)
        shared = gelu(x @ W1s + b1s) @ W2s + b2s
        rw = jax.nn.softmax(x @ Wr, axis=-1)
        topw, topi = jax.lax.top_k(rw, K)
        topw = topw / jnp.sum(topw, axis=-1, keepdims=True)
        mask = jnp.sum(jax.nn.one_hot(topi, E, dtype=topw.dtype) * topw[..., None], axis=-2)
        h = gelu(jnp.einsum('bsd,edf->bsef', x, W1p) + b1p)
        priv = jnp.einsum('bsef,efd->bsed', h, W2p) + b2p
        routed = jnp.einsum('bsed,bse->bsd', priv, mask)
        return shared + routed
    x = x + _L0_gnn_ref(_layernorm(x, axis=-1), adj, L0_gnn_W, L0_gnn_a)
    x = x + _L0_ffn_ref(_layernorm(x, axis=-1), L0_ffn_Wr, L0_ffn_W1s, L0_ffn_b1s, L0_ffn_W2s, L0_ffn_b2s, L0_ffn_W1p, L0_ffn_b1p, L0_ffn_W2p, L0_ffn_b2p)
    return x

_drawn_inputs = setup_inputs


def setup_inputs(seed=0):
    import zlib

    import numpy as np

    out = dict(_drawn_inputs(seed))
    spreads = {'L0_ffn_b1s': (0.0, 0.376),
     'L0_ffn_b2s': (0.0, 0.1),
     'L0_ffn_b1p': (0.0, 0.513),
     'L0_ffn_b2p': (0.0, 0.1)}
    factors = {}
    for name, (base, spread) in spreads.items():
        noise = np.random.default_rng([zlib.crc32(name.encode()), seed]).standard_normal(out[name].shape)
        drawn = base * np.exp(spread * noise) if base else spread * noise
        out[name] = jnp.asarray(drawn.astype(out[name].dtype))
    for name, factor in factors.items():
        out[name] = (out[name] * factor).astype(out[name].dtype)
    return out
```

```python
from contextlib import ExitStack

import concourse.bass as bass
from concourse import mybir

F32 = mybir.dt.float32
F32R = mybir.dt.float32r
BF16 = mybir.dt.bfloat16
I32 = mybir.dt.int32
U32 = mybir.dt.uint32
ALU = mybir.AluOpType
ACT = mybir.ActivationFunctionType
AX = mybir.AxisListType.X
RMAX = bass.bass_isa.ReduceOp.max

P = 128
SLOPE = 0.2
EPS = 1e-5
TINY = 1e-30
HUGE = 3.0e38


def gnn_moe_layer(nc, x, adj, gnn_W, gnn_a, Wr, W1s, b1s, W2s, b2s, W1p, b1p, W2p, b2p, out):
    NB, N, D = x.shape
    F = W1s.shape[1]
    E = Wr.shape[1]
    NT = N // P
    NC = F // P
    H = 512
    NH = N // H
    T = 512
    TB = T // P
    TSH = T.bit_length() - 1
    GROUPS = [NB - 2, 2]
    assert D == P and N % H == 0 and sum(GROUPS) == NB and 2 * D + 2 * D <= H

    GT = [(2 * g * N - E) // T + E for g in GROUPS]
    REG = [g * N + T for g in GROUPS]
    GBASE = [0, E * REG[0] + T]
    SHARED = GBASE[1] + E * REG[1] + T
    ROWS = SHARED + NB * N
    ST = NB * N // T
    TILE0 = [0, GT[0] + ST]
    NTILES = GT[0] + ST + GT[1]
    COMB = T // P
    ROUNDS = NB * NT // COMB
    ROUNDS_A = GROUPS[0] * NT // COMB
    PAIRS = NTILES // 2 - 2
    COMB_PAIR = PAIRS - ROUNDS_A
    B_PAIR = (TILE0[1] - 4) // 2
    PART0 = [0, GT[0], TILE0[1], NTILES]
    assert NTILES % 2 == 0 and 2 * COMB_PAIR > GT[0] + 2
    GM = max(GT)

    ctx = ExitStack()
    with ctx:
        def sb(name, shape, dt):
            return ctx.enter_context(nc.sbuf_tensor(name, shape, dt))

        def sem(name):
            return ctx.enter_context(nc.semaphore(name))

        def sems(name, n=2):
            return [sem(f"{name}{i}") for i in range(n)]

        bank = [ctx.enter_context(nc.psum_tensor(f"bank{i}", [P, H], F32)) for i in range(8)]

        wsplit = nc.dram_tensor("wsplit", [E + 1, P, 2, 2 * F], F32, kind="Internal").ap()
        xrows = nc.dram_tensor("xrows", [ROWS, D], F32, kind="Internal").ap()
        yrows = [nc.dram_tensor(f"yrows{i}", [n * T, D], F32, kind="Internal").ap()
                 for i, n in enumerate((GT[0], ST, GT[1]))]

        ident = sb("ident", [P, P], F32)
        identb = sb("identb", [P, P], BF16)
        before = sb("before", [P, P], BF16)
        onesb = sb("onesb", [P, P], BF16)
        onesf = sb("onesf", [P, P], F32)
        coefM = sb("coefM", [P, 3], F32)
        minus_half = sb("minus_half", [P, NT], F32)
        iota_i = sb("iota_i", [P, NT, E], I32)
        iota_e = sb("iota_e", [P, NT, E], F32)
        base_i = sb("base_i", [P, 2, E], I32)
        base = sb("base", [P, 2, E], F32)
        iota_ti = sb("iota_ti", [P, GM, E], I32)
        iota_t = sb("iota_t", [P, GM, E], F32)
        zero_e = sb("zero_e", [P, E], F32)
        zrow = sb("zrow", [P, TB, D], F32)
        Wg = sb("Wg", [P, D], F32)
        acol = sb("acol", [P, 2], F32)
        WTa = sb("WTa", [P, D + 1], F32)
        wi = sb("wi", [P, 1], F32)
        wirep = sb("wirep", [P, P], F32)
        Wr_sb = sb("Wr_sb", [P, E], F32)
        NBR = (E + 1) * (NC + 1)
        brow = sb("brow", [NBR, P], F32)
        b1t = sb("b1t", [P, E + 1, NC], F32)
        b2t = sb("b2t", [P, E + 1], F32)
        wraw = sb("wraw", [P, 2, 2, F], F32)
        wst = sb("wst", [P, 2, 2, 2 * F], F32R)

        res = sb("res", [P, NB * NT, D], F32)
        adjm = sb("adjm", [P, 2, NT, N], BF16)
        stat = sb("stat", [P, 2, NT, 6], F32)
        lnt = sb("lnt", [P, 2, 8, NT], F32)
        xn = sb("xn", [P, NT, D], F32)
        xnT = sb("xnT", [P, N], F32)
        WhA = sb("WhA", [P, 2, NT, D + 1], F32)
        ejc = sb("ejc", [P, 2, NT], F32)
        mx = sb("mx", [P, 1], F32)
        Mb = sb("Mb", [P, 1], F32)
        cM = sb("cM", [P, 3], F32)
        Bc = sb("Bc", [P, 2, NT], F32)
        Dc = sb("Dc", [P, 2, NT], F32)
        nBc = sb("nBc", [P, 2, NT], F32)
        crow = sb("crow", [P, 2, N], F32)
        R = sb("R", [P, 2, N], F32)
        PT = sb("PT", [P, 2, N], F32)
        dens = sb("dens", [P, 3, 3], F32)
        rden = sb("rden", [P, 3, 3], F32)
        xn2 = sb("xn2", [P, 2, NT, D], F32)
        x2T = sb("x2T", [P, N], F32)
        Ls = sb("Ls", [P, 2, NT, E], F32)
        m12 = sb("m12", [P, 2, NT], F32)
        eq = sb("eq", [P, NT, E], F32)
        cand = sb("cand", [P, NT, E], F32)
        first = sb("first", [P, NT], F32)
        oh = sb("oh", [P, 2, NT, E], F32)
        mm = sb("mm", [P, NT, E], BF16)
        dm = sb("dm", [P, NT], F32)
        ed = sb("ed", [P, NT], F32)
        ed1 = sb("ed1", [P, NT], F32)
        gates = sb("gates", [P, 2, NB * NT], F32)
        pos = sb("pos", [P, NT, E], F32)
        hit = sb("hit", [P, 2, NT, E], F32)
        slotf = sb("slotf", [P, 2, NT], F32)
        choice = sb("choice", [P, 2, NB * NT], F32)
        slotall = sb("slotall", [P, 2, NB * NT], F32)
        slotmv = sb("slotmv", [P, 2, 2, NB * NT], F32)
        slots = sb("slots", [P, 2, NB * NT], U32)
        sslot = sb("sslot", [P, 2, 2, NT], U32)
        gslot = sb("gslot", [P, 2, COMB], U32)
        carry = sb("carry", [P, E], F32)

        nti = sb("nti", [P, 2, E], I32)
        cnt = sb("cnt", [P, 5, E], F32)
        tge = sb("tge", [P, 2, GM, E], F32)
        tv = sb("tv", [P, 5, GM], F32)
        tab_x = sb("tab_x", [P, NTILES], I32)
        tab_e = sb("tab_e", [P, NTILES], I32)
        tab_tail = sb("tab_tail", [P, 2, E], I32)

        w1, w2 = wst[:, :, 0, :], wst[:, :, 1, :]
        b1 = sb("b1", [P, 2, NC], F32)
        b2 = sb("b2", [P, 2, 1], F32)
        xh = sb("xh", [P, 2, T], F32R)
        xl = sb("xl", [P, 2, T], F32R)
        spare = adjm[:, :, :, :].rearrange("p q t n -> p (q t n)").bitcast(F32)
        taken = [0]

        def over_masks(*dims):
            size = 1
            for d in dims:
                size *= d
            v = spare[:, taken[0]:taken[0] + size]
            taken[0] += size
            if len(dims) == 2:
                v = v.rearrange("p (a b) -> p a b", a=dims[0])
            if len(dims) == 3:
                v = v.rearrange("p (a b c) -> p a b c", a=dims[0], b=dims[1])
            return v

        xs = over_masks(2, TB, D)
        hf = over_masks(2, T)
        yTs = over_masks(T)
        ys = over_masks(2, TB, D)
        g12 = over_masks(COMB, 2, D)
        gsh, oa, ob, ot = (over_masks(COMB, D) for _ in range(4))
        hh = sb("hh", [P, 2, NC, T], F32R)
        hl = sb("hl", [P, 2, NC, T], F32R)

        mT = [bank[i][:, :].bitcast(BF16) for i in (0, 1)]
        at = [bank[2 + i][:, 0:3 * (D + 1)].rearrange("p (t c) -> p t c", t=3) for i in range(3)]
        tp = [bank[5], bank[6]]
        ws = bank[7]
        whp = ws[:, 0:3 * (D + 1)].rearrange("p (t c) -> p t c", t=3)
        lgp = ws[:, 400:400 + NT * E].rearrange("p (t e) -> p t e", e=E)
        cntp = ws[:, 480:480 + E]
        hps = bank[0:4]
        yTp, xTp, yRp = (bank[4], bank[7]), bank[5], bank[6]

        s_zero, s_iota, s_const = sem("s_zero"), sem("s_iota"), sem("s_const")
        s_par, s_wt, s_wcopy, s_wirep = sem("s_par"), sem("s_wt"), sem("s_wcopy"), sem("s_wirep")
        s_brow, s_bT, s_btab = sem("s_brow"), sem("s_bT"), sem("s_btab")
        s_wraw, s_whi, s_wlo, s_wst = sems("s_wraw"), sem("s_whi"), sem("s_wlo"), sems("s_wst")
        s_x, s_adj, s_msk = sems("s_x"), sems("s_adj"), sem("s_msk")
        s_stat, s_lnsum, s_lnsq, s_var = sems("s_stat"), sems("s_lnsum"), sems("s_lnsq"), sems("s_var")
        s_vareps, s_rstd = sems("s_vareps"), sems("s_rstd")
        s_xn, s_xnt, s_xnT, s_Whp, s_Whc, s_ei = (sem(n) for n in ("s_xn", "s_xnt", "s_xnT", "s_Whp", "s_Whc", "s_ei"))
        s_mx, s_M, s_cM, s_BD, s_nB, s_E1, s_crow = (sem(n) for n in ("s_mx", "s_M", "s_cM", "s_BD", "s_nB", "s_E1", "s_crow"))
        s_mT, s_R, s_PT, s_at = sem("s_mT"), sem("s_R"), sem("s_PT"), sem("s_at")
        s_den, s_rden, s_res = sem("s_den"), sem("s_rden"), sem("s_res")
        s_xn2, s_xn2t, s_x2T, s_lg, s_route, s_mm = (sem(n) for n in ("s_xn2", "s_xn2t", "s_x2T", "s_lg", "s_route", "s_mm"))
        s_yslot = sem("s_yslot")
        s_oh, s_hit, s_gslot = sem("s_oh"), sem("s_hit"), sem("s_gslot")
        s_dm, s_ed, s_gate, s_rank, s_pos, s_slot = (sem(n) for n in ("s_dm", "s_ed", "s_gate", "s_rank", "s_pos", "s_slot"))
        s_carry, s_scat, s_shx = sem("s_carry"), sems("s_scat"), sems("s_shx")
        s_tstep, s_tab, s_tabS, s_tail = sem("s_tstep"), sem("s_tab"), sem("s_tabS"), sem("s_tail")
        s_xin, s_w1, s_w2 = sems("s_xin"), sems("s_w1"), sems("s_w2")
        s_xT, s_xh, s_xl, s_hp, s_hf, s_hh, s_hl = (sem(n) for n in ("s_xT", "s_xh", "s_xl", "s_hp", "s_hf", "s_hh", "s_hl"))
        s_yT, s_yTs, s_yR, s_ys, s_yst = sem("s_yT"), sem("s_yTs"), sem("s_yR"), sem("s_ys"), sems("s_yst")
        s_g, s_gsh, s_oa, s_ob, s_ot, s_out = sems("s_g", COMB), sem("s_gsh"), sem("s_oa"), sem("s_ob"), sem("s_ot"), sem("s_out")

        s_alone = sem("s_alone")
        block = ctx.enter_context(nc.Block())

        def stage1(eng, ahead, attend):
            def at(b):
                return b, b % 2, b // 2
            ahead(at(0))
            attend(at(0), None, at(1))
            attend(at(1), at(0), at(2))
            attend(at(2), at(1), at(3))
            with eng.Fori(1, NB // 2 - 1) as p:
                attend((2 * p + 1, 1, p), (2 * p, 0, p), (2 * p + 2, 0, p + 1))
                attend((2 * p + 2, 0, p + 1), (2 * p + 1, 1, p), (2 * p + 3, 1, p + 1))
            attend(at(NB - 1), at(NB - 2), None)
            attend(None, at(NB - 1), None)

        def stage2(step, loop):
            for k in range(4):
                step(k, k % 2)
            loop()
            for k in range(NTILES - 2, NTILES + 2):
                step(k, k % 2)

        def alone(eng):
            eng.sem_inc(s_alone, 1)

        def isint(v):
            return isinstance(v, int)

        @block.sync
        def _(sp):
            sp.dma_start(Wg[:, :], gnn_W).then_inc(s_par, 16)
            with nc.allow_non_contiguous_dma(reason="256 values once"):
                sp.dma_start(acol[:, :], gnn_a.rearrange("(k o) -> o k", k=2)).then_inc(s_par, 16)
            sp.dma_start(Wr_sb[:, :], Wr).then_inc(s_par, 16)

            def load_x(b, q, half):
                if not (isint(half) and half == 0):
                    sp.wait_ge(s_x[q], 16 * half)
                    alone(sp)
                sp.dma_start(res[:, bass.ds(b * NT, NT), :], x[b].rearrange("(t p) d -> p t d", p=P)).then_inc(s_x[q], 16)

            load_x(0, 0, 0)
            load_x(1, 1, 0)
            n1 = (E + 1) * NC
            sp.dma_start(brow[0:E * NC, :], b1p.rearrange("e (c p) -> (e c) p", p=P)).then_inc(s_brow, 16)
            sp.dma_start(brow[E * NC:n1, :], b1s.rearrange("(c p) -> c p", p=P)).then_inc(s_brow, 16)
            sp.dma_start(brow[n1:n1 + E, :], b2p).then_inc(s_brow, 16)
            sp.dma_start(brow[n1 + E:NBR, :], b2s.rearrange("(a p) -> a p", a=1)).then_inc(s_brow, 16)
            with sp.Fori(1, NB // 2) as h:
                load_x(2 * h, 0, h)
                load_x(2 * h + 1, 1, h)

            def raw_weights(e):
                if e >= 2:
                    sp.wait_ge(s_wlo, e - 1)
                src1, src2 = (W1p[e], W2p[e]) if e < E else (W1s, W2s)
                sp.dma_start(wraw[:, e % 2, 0, :], src1).then_inc(s_wraw[e % 2], 16)
                sp.dma_start(wraw[:, e % 2, 1, :].rearrange("p (c d) -> p c d", c=NC),
                             src2.rearrange("(c p) d -> p c d", p=P)).then_inc(s_wraw[e % 2], 16)

            raw_weights(0)
            for e in range(E + 1):
                if e < E:
                    raw_weights(e + 1)
                sp.wait_ge(s_wlo, e + 1)
                sp.dma_start(wsplit[e], wst[:, e % 2, :, :].bitcast(F32)).then_inc(s_wst[e % 2], 16)

            sp.wait_ge(s_zero, 1)
            for g in range(2):
                r = GBASE[g] + E * REG[g]
                sp.dma_start(xrows[r:r + T, :].rearrange("(k p) d -> p k d", p=P), zrow[:, :, :]).then_inc(s_tail, 16)

            def store_x2(b, q, half):
                sp.wait_ge(s_xn2, b + 1)
                alone(sp)
                if not (isint(half) and half == 0):
                    sp.wait_ge(s_shx[q], 16 * half)
                    alone(sp)
                sp.dma_start(xrows[bass.ds(SHARED + b * N, N), :].rearrange("(t p) d -> p t d", p=P),
                             xn2[:, q, :, :]).then_inc(s_shx[q], 16)

            store_x2(0, 0, 0)
            store_x2(1, 1, 0)
            with sp.Fori(1, NB // 2 - 1) as h:
                store_x2(2 * h, 0, h)
                store_x2(2 * h + 1, 1, h)

            def tails(g):
                sp.wait_ge(s_tab, g + 1)
                for e in range(E):
                    r = sp.value_load(tab_tail[0:1, g, e:e + 1], min_val=0, max_val=ROWS - T)
                    sp.dma_start(xrows[bass.ds(r, T), :].rearrange("(k p) d -> p k d", p=P),
                                 zrow[:, :, :]).then_inc(s_tail, 16)

            def filled(g):
                for q in range(2):
                    sp.wait_ge(s_scat[q], 16 * 2 * NT * sum(GROUPS[:g + 1]) // 2)
                sp.wait_ge(s_tail, 16 * (2 + E * (g + 1)))

            def load_rows(k, r):
                if not (isint(k) and k < 2):
                    sp.wait_ge(s_xT, k - 1)
                    alone(sp)
                row = sp.value_load(tab_x[0:1, bass.ds(k, 1)], min_val=0, max_val=ROWS - T)
                sp.dma_start(xs[:, r, :, :], xrows[bass.ds(row, T), :].rearrange("(k p) d -> p k d", p=P)).then_inc(s_xin[r], 16)

            def load_w1(k, r):
                e = sp.value_load(tab_e[0:1, bass.ds(k, 1)], min_val=0, max_val=E)
                if not (isint(k) and k < 2):
                    sp.wait_ge(s_hp, NC * (k - 1))
                    alone(sp)
                sp.dma_start(w1[:, r, :].bitcast(F32), wsplit[e, :, 0, :]).then_inc(s_w1[r], 16)
                if not (isint(k) and k < 2):
                    sp.wait_ge(s_hf, NC * (k - 1))
                    alone(sp)
                sp.dma_start(b1[:, r, :], b1t[:, e, :]).then_inc(s_w1[r], 16)

            def load_w2(k, r):
                e = sp.value_load(tab_e[0:1, bass.ds(k, 1)], min_val=0, max_val=E)
                if not (isint(k) and k < 2):
                    sp.wait_ge(s_yT, k - 1)
                    alone(sp)
                sp.dma_start(w2[:, r, :].bitcast(F32), wsplit[e, :, 1, :]).then_inc(s_w2[r], 16)
                if not (isint(k) and k < 2):
                    sp.wait_ge(s_yTs, k - 1)
                    alone(sp)
                sp.dma_start(b2[:, r, :], b2t[:, bass.ds(e, 1)]).then_inc(s_w2[r], 16)

            def store_y(k, r, half, part):
                sp.wait_ge(s_ys, k + 1)
                alone(sp)
                if not (isint(half) and half == 0):
                    sp.wait_ge(s_yst[r], 16 * half)
                    alone(sp)
                sp.dma_start(yrows[part][bass.ds((k - PART0[part]) * T, T), :].rearrange("(k p) d -> p k d", p=P),
                             ys[:, r, :, :]).then_inc(s_yst[r], 16)

            def part_of(k):
                return sum(k >= p for p in PART0[1:3])

            def step(k, r):
                h = k // 2 if isint(k) else None
                if isint(k):
                    if k + 1 < NTILES:
                        load_w1(k + 1, 1 - r)
                    if k < NTILES:
                        load_w2(k, r)
                    if k + 2 < NTILES:
                        load_rows(k + 2, r)
                    if k >= 2:
                        store_y(k - 2, r, h - 1, part_of(k - 2))

            def shared_rows(c, stored):
                if not (isint(c) and c == 0):
                    sp.wait_ge(s_oa, c)
                    alone(sp)
                for r in range(2):
                    sp.wait_ge(s_yst[r], 16 * stored)
                    alone(sp)
                sp.dma_start(gsh[:, :, :], yrows[1][bass.ds(c * T, T), :].rearrange("(k p) d -> p k d", p=P)).then_inc(s_gsh, 16)

            def store_out(c):
                sp.wait_ge(s_ot, c + 1)
                alone(sp)
                sp.dma_start(out.rearrange("b n d -> (b n) d")[bass.ds(c * T, T), :].rearrange("(k p) d -> p k d", p=P),
                             ot[:, :, :]).then_inc(s_out, 16)

            tails(0)
            filled(0)
            sp.wait_ge(s_mT, NB * NT)
            sp.wait_ge(s_wst[0], 16 * (E // 2 + 1))
            sp.wait_ge(s_wst[1], 16 * (E // 2))
            sp.wait_ge(s_btab, 1)
            sp.wait_ge(s_tabS, 2)
            load_rows(0, 0)
            load_rows(1, 1)
            load_w1(0, 0)
            step(0, 0)
            step(1, 1)
            store_x2(NB - 2, 0, NB // 2 - 1)
            store_x2(NB - 1, 1, NB // 2 - 1)
            tails(1)

            def pair(m, comb, first):
                if comb:
                    shared_rows(m - COMB_PAIR, m)
                load_w1(2 * m + 3, 1)
                load_w2(2 * m + 2, 0)
                load_rows(2 * m + 4, 0)
                store_y(2 * m, 0, m, part_of(2 * first))
                load_w1(2 * m + 4, 0)
                load_w2(2 * m + 3, 1)
                load_rows(2 * m + 5, 1)
                store_y(2 * m + 1, 1, m, part_of(2 * first + 1))
                if comb and first > COMB_PAIR:
                    store_out(m - COMB_PAIR - 1)

            for q in range(2):
                sp.wait_ge(s_shx[q], 16 * (NB // 2))
            assert COMB_PAIR < B_PAIR < PAIRS
            edges = {0, 1, COMB_PAIR, COMB_PAIR + 1, B_PAIR, PAIRS}
            for p in PART0[1:3]:
                edges |= {p // 2, (p + 1) // 2}
            edges = sorted(edges)
            for lo, hi in zip(edges, edges[1:]):
                if lo == B_PAIR:
                    filled(1)
                if hi - lo == 1:
                    pair(lo, lo >= COMB_PAIR, lo)
                else:
                    with sp.Fori(lo, hi) as m:
                        pair(m, lo >= COMB_PAIR, lo)
            store_out(ROUNDS_A - 1)
            for k in range(NTILES - 2, NTILES + 2):
                step(k, k % 2)
            for c in range(ROUNDS_A, ROUNDS):
                shared_rows(c, NTILES // 2)
                store_out(c)
            sp.wait_ge(s_out, 16 * ROUNDS)


        @block.gpsimd
        def _(pool):
            pool.memset(ident[:, :], 0.0)
            pool.memset(identb[:, :], 0.0)
            pool.memset(before[:, :], 0.0)
            pool.memset(onesb[:, :], 1.0)
            pool.memset(onesf[:, :], 1.0)
            pool.memset(zero_e[:, :], 0.0)
            pool.memset(minus_half[:, :], -0.5)
            pool.memset(coefM[:, 0:1], -1.0)
            pool.memset(coefM[:, 1:2], -SLOPE)
            pool.memset(coefM[:, 2:3], SLOPE - 1.0)
            pool.memset(WhA[:, :, :, D:D + 1], 1.0)
            pool.memset(zrow[:, :, :], 0.0).then_inc(s_zero, 1)
            pool.iota(iota_i[:, :, :], [[0, NT], [1, E]], base=0, channel_multiplier=0)
            for g in range(2):
                pool.iota(base_i[:, g, :], [[REG[g], E]], base=GBASE[g], channel_multiplier=0)
            pool.iota(iota_ti[:, :, :], [[1, GM], [0, E]], base=0, channel_multiplier=0).then_inc(s_iota, 1)
            pool.wait_ge(s_zero, 1)
            pool.wait_ge(s_iota, 1)
            pool.affine_select(out=ident[:, :], in_=ident[:, :], compare_op=ALU.not_equal, fill=1.0,
                               base=0, pattern=[[-1, P]], channel_multiplier=1)
            pool.affine_select(out=identb[:, :], in_=identb[:, :], compare_op=ALU.not_equal, fill=1.0,
                               base=0, pattern=[[-1, P]], channel_multiplier=1)
            pool.affine_select(out=before[:, :], in_=before[:, :], compare_op=ALU.is_ge, fill=1.0,
                               base=0, pattern=[[-1, P]], channel_multiplier=1)
            pool.tensor_copy(iota_e[:, :, :], iota_i[:, :, :])
            pool.tensor_copy(base[:, :, :], base_i[:, :, :])
            pool.tensor_copy(iota_t[:, :, :], iota_ti[:, :, :]).then_inc(s_const, 1)
            s0, s1 = GT[0], GT[0] + ST
            pool.iota(tab_x[:, s0:s1], [[T, ST]], base=SHARED, channel_multiplier=0).then_inc(s_tabS, 1)
            pool.iota(tab_e[:, s0:s1], [[0, ST]], base=E, channel_multiplier=0).then_inc(s_tabS, 1)

            def load_adj(b, q, half):
                if not (isint(b) and b < 2):
                    pool.wait_ge(s_mT, NT * (b - 1))
                    pool.wait_ge(s_adj[q], 32 * half)
                for k in range(2):
                    pool.dma_start(adjm[:, q, k * NT // 2:(k + 1) * NT // 2, :],
                                   adj[b].rearrange("(t p) n -> p t n", p=P)[:, k * NT // 2:(k + 1) * NT // 2, :]
                                   ).then_inc(s_adj[q], 16)

            def rstd(k, b):
                pool.wait_ge(s_var[k], b + 1)
                alone(pool)
                pool.tensor_scalar(lnt[:, k, 6, :], lnt[:, k, 4, :], 1.0 / D, EPS, ALU.mult, ALU.add).then_inc(s_vareps[k], 1)
                pool.wait_ge(s_vareps[k], b + 1)
                pool.tensor_tensor(lnt[:, k, 7, :], lnt[:, k, 6, :], minus_half[:, :], ALU.pow).then_inc(s_rstd[k], 1)

            def batch_max(b):
                pool.wait_ge(s_mx, b + 1)
                if not (isint(b) and b == 0):
                    pool.wait_ge(s_cM, b)
                alone(pool)
                pool.partition_all_reduce(Mb[:, :], mx[:, :], P, RMAX).then_inc(s_M, 1)

            def scatter(b, q):
                pool.wait_ge(s_slot, b + 1)
                pool.wait_ge(s_xn2, b + 1)
                alone(pool)
                for c in range(2):
                    for t in range(NT):
                        pool.indirect_dma_start(xrows, bass.IndirectOffsetOnAxis(ap=sslot[:, q, c, t:t + 1], axis=0),
                                                xn2[:, q, t, :], None).then_inc(s_scat[q], 16)

            def ahead(nxt):
                b, q, half = nxt
                rstd(0, b)
                batch_max(b)

            def attend(cur, fin, nxt):
                if nxt:
                    load_adj(*nxt)
                if fin:
                    rstd(1, fin[0])
                if nxt:
                    rstd(0, nxt[0])
                if nxt:
                    batch_max(nxt[0])
                if fin:
                    scatter(fin[0], fin[1])

            load_adj(0, 0, 0)
            stage1(pool, ahead, attend)

            def gather(c, part):
                for i in range(COMB):
                    if not (isint(c) and c == 0):
                        pool.wait_ge(s_ot, c)
                        pool.wait_ge(s_g[i], 32 * c)
                    alone(pool)
                    for ch in range(2):
                        pool.indirect_dma_start(g12[:, i, ch, :], None, yrows[part],
                                                bass.IndirectOffsetOnAxis(ap=gslot[:, ch, i:i + 1], axis=0)).then_inc(s_g[i], 16)

            def load_slots(c):
                if not (isint(c) and c == 0):
                    for i in range(COMB):
                        pool.wait_ge(s_g[i], 32 * c)
                pool.tensor_copy(gslot[:, :, :], slots[:, :, bass.ds(c * COMB, COMB)]).then_inc(s_gslot, 1)
                pool.wait_ge(s_gslot, c + 1)

            pool.wait_ge(s_yslot, 2)
            for r in range(2):
                pool.wait_ge(s_yst[r], 16 * ((GT[0] + 1 - r) // 2))
            load_slots(0)
            gather(0, 0)
            with pool.Fori(1, ROUNDS_A) as c:
                load_slots(c)
                gather(c, 0)
            for r in range(2):
                pool.wait_ge(s_yst[r], 16 * (NTILES // 2))
            with pool.Fori(ROUNDS_A, ROUNDS) as c:
                load_slots(c)
                gather(c, 2)

        @block.tensor
        def _(pe):
            pe.wait_ge(s_const, 1)
            pe.wait_ge(s_par, 48)
            pe.transpose(tp[0][:, 0:P], Wg[:, :], ident[:, :])
            pe.matmul(ws[:, 0:2], Wg[:, :], acol[:, :], start=True, stop=True).then_inc(s_wt, 1)
            pe.wait_ge(s_brow, 64)
            pe.transpose(tp[1][:, 0:NBR], brow[:, :], ident[0:NBR, 0:NBR]).then_inc(s_bT, 1)
            pe.wait_ge(s_wirep, 1)
            pe.wait_ge(s_btab, 1)

            def project(b, q):
                pe.wait_ge(s_xn, b + 1)
                if not (isint(b) and b == 0):
                    pe.wait_ge(s_E1, 2 * b)
                if not (isint(b) and b < 2):
                    pe.wait_ge(s_x2T, 2 * (b - 1))
                for t in range(NT):
                    i = pe.transpose(tp[t // 4][:, (t % 4) * P:(t % 4 + 1) * P], xn[:, t, :], ident[:, :])
                    if t % 4 == 3:
                        i.then_inc(s_xnt, 1)
                pe.wait_ge(s_xnT, 2 * b + 2)
                for g in range(3):
                    if not (isint(b) and b == 0 and g == 0):
                        pe.wait_ge(s_Whc, 3 * b + g)
                    if g == 0 and not (isint(b) and b < 2):
                        pe.wait_ge(s_carry, b)
                    tiles = range(3 * g, min(3 * g + 3, NT))
                    for t in tiles:
                        i = pe.matmul(whp[:, t % 3, :], xnT[:, t * P:(t + 1) * P], WTa[:, :], start=True, stop=True)
                    i.then_inc(s_Whp, 1)
                    if g < 2:
                        pe.matmul(tp[g][:, :], wirep[:, :], xnT[:, g * H:(g + 1) * H], start=True, stop=True).then_inc(s_ei, 1)

            def mask_T(b, q, jt):
                n = NT * b + jt
                if jt == 0:
                    pe.wait_ge(s_msk, b + 1)
                if not (isint(n) and n < 2):
                    pe.wait_ge(s_PT, n - 1)
                for t in range(NT):
                    i = pe.transpose(mT[jt % 2][:, t * P:(t + 1) * P], adjm[:, q, t, jt * P:(jt + 1) * P], identb[:, :])
                i.then_inc(s_mT, 1)

            def weigh(b, q, jt):
                pe.wait_ge(s_PT, NT * b + jt + 1)
                if jt == 0:
                    pe.wait_ge(s_Whc, 3 * b + 3)
                    if not (isint(b) and b == 0):
                        pe.wait_ge(s_res, b)
                for t in range(NT):
                    i = pe.matmul(at[t // 3][:, t % 3, :], PT[:, jt % 2, t * P:(t + 1) * P], WhA[:, q, jt, :],
                                  start=(jt == 0 and t % 3 == 0), stop=(jt == NT - 1), skip_group_check=True)
                i.then_inc(s_at, 1)

            def x2_T(b, q):
                pe.wait_ge(s_xn2, b + 1)
                if isint(b) and b == NB - 1:
                    pe.wait_ge(s_E1, 2 * NB)
                else:
                    pe.wait_ge(s_E1, 2 * (b + 2))
                for t in range(NT):
                    i = pe.transpose(tp[t // 4][:, (t % 4) * P:(t % 4 + 1) * P], xn2[:, q, t, :], ident[:, :])
                    if t % 4 == 3:
                        i.then_inc(s_xn2t, 1)

            def logits(b):
                pe.wait_ge(s_x2T, 2 * b + 2)
                pe.wait_ge(s_Whc, 3 * NB if isint(b) and b == NB - 1 else 3 * (b + 2))
                if not (isint(b) and b == 0):
                    pe.wait_ge(s_carry, b + 2 if isint(b) and b > GROUPS[0] else b + 1)
                for t in range(NT):
                    i = pe.matmul(lgp[:, t, :], x2T[:, t * P:(t + 1) * P], Wr_sb[:, :], start=True, stop=True)
                i.then_inc(s_lg, 1)

            def ranks(b):
                pe.wait_ge(s_mm, b + 1)
                pe.matmul(lgp[:, :, :], before[:, :], mm[:, :, :], start=True, stop=False, skip_group_check=True)
                for k in range(1, NT):
                    pe.matmul(lgp[:, k:NT, :], onesb[:, :], mm[:, 0:NT - k, :], start=False, stop=(k == NT - 1), skip_group_check=True)
                for t in range(NT):
                    i = pe.matmul(cntp, onesb[:, :], mm[:, t, :], start=(t == 0), stop=(t == NT - 1), skip_group_check=True)
                i.then_inc(s_rank, 1)

            def attend(cur, fin, nxt):
                if cur:
                    b, q, half = cur
                    mask_T(b, q, 0)
                    mask_T(b, q, 1)
                for jt in range(NT):
                    if cur:
                        weigh(b, q, jt)
                        if jt + 2 < NT:
                            mask_T(b, q, jt + 2)
                    if fin and jt == 2:
                        x2_T(fin[0], fin[1])
                    if fin and jt == 3:
                        logits(fin[0])
                    if fin and jt == 5:
                        ranks(fin[0])
                    if nxt and jt == 6:
                        project(nxt[0], nxt[1])

            stage1(pe, lambda nxt: project(nxt[0], nxt[1]), attend)

            def split_product(o, wh, wl, xh_, xl_, start, stop):
                pe.matmul(o, wh, xh_, start=start, stop=False)
                pe.matmul(o, wh, xl_, start=False, stop=False)
                return pe.matmul(o, wl, xh_, start=False, stop=stop)

            def rows_T(k, r):
                pe.wait_ge(s_xin[r], 16 * (k // 2 + 1) if isint(k) else 16 * half_of[0])
                if not (isint(k) and k == 0):
                    pe.wait_ge(s_xl, k)
                for t in range(TB):
                    i = pe.transpose(xTp[:, t * P:(t + 1) * P], xs[:, r, t, :], ident[:, :])
                i.then_inc(s_xT, 1)

            def up(k, r, c):
                if c == 0:
                    pe.wait_ge(s_w1[r], 32 * (k // 2 + 1) if isint(k) else 32 * half_of[1])
                    pe.wait_ge(s_xl, k + 1)
                if not (isint(k) and k == 0):
                    pe.wait_ge(s_hf, NC * (k - 1) + c + 1)
                f = slice(c * P, (c + 1) * P)
                split_product(hps[c][:, :], w1[:, r, f], w1[:, r, F:][:, f], xh[:, r, :], xl[:, r, :], True, True).then_inc(s_hp, 1)

            def down(k, r, c):
                pe.wait_ge(s_hl, NC * k + c + 1)
                if c == 0:
                    pe.wait_ge(s_w2[r], 32 * (k // 2 + 1) if isint(k) else 32 * half_of[2])
                    if not (isint(k) and k < 2):
                        pe.wait_ge(s_yTs, k - 1)
                f = slice(c * P, (c + 1) * P)
                i = split_product(yTp[r][:, :], w2[:, r, f], w2[:, r, F:][:, f], hh[:, r, c, :], hl[:, r, c, :], c == 0, c == NC - 1)
                if c == NC - 1:
                    i.then_inc(s_yT, 1)

            def rows_back(k):
                pe.wait_ge(s_yTs, k + 1)
                if not (isint(k) and k == 0):
                    pe.wait_ge(s_ys, k)
                for t in range(TB):
                    i = pe.transpose(yRp[:, t * P:(t + 1) * P], yTs[:, t * P:(t + 1) * P], ident[:, :])
                i.then_inc(s_yR, 1)

            half_of = [None, None, None]

            def step(k, r):
                static = isint(k)
                for c in range(NC):
                    if not static or k < NTILES:
                        up(k, r, c)
                    if c == 1 and (not static or k + 1 < NTILES):
                        rows_T(k + 1, 1 - r)
                    if c == 2 and (not static or k >= 2):
                        rows_back(k - 2)
                    if not static or 1 <= k <= NTILES:
                        down(k - 1, 1 - r, c)

            def loop():
                with pe.Fori(1, PAIRS) as m:
                    half_of[:] = [m + 2, m + 2, m + 1]
                    step(2 * m + 2, 0)
                    half_of[:] = [m + 3, m + 2, m + 2]
                    step(2 * m + 3, 1)

            pe.wait_ge(s_pos, NB)
            pe.wait_ge(s_carry, NB + 2)
            rows_T(0, 0)
            stage2(step, loop)

        @block.scalar
        def _(act):
            def copy(o, i):
                return act.activation(o, i, ACT.Copy)

            act.wait_ge(s_wt, 1)
            copy(WTa[:, 0:D], tp[0][:, 0:P])
            copy(WTa[:, D:D + 1], ws[:, 1:2])
            copy(wi[:, :], ws[:, 0:1]).then_inc(s_wcopy, 1)
            act.wait_ge(s_bT, 1)
            copy(b1t[:, :, :], tp[1][:, 0:(E + 1) * NC].rearrange("p (e c) -> p e c", c=NC))
            copy(b2t[:, :], tp[1][:, (E + 1) * NC:NBR]).then_inc(s_btab, 1)
            act.wait_ge(s_wcopy, 1)
            act.activation(wirep[:, :], onesf[:, :], ACT.Copy, scale=wi[:, :]).then_inc(s_wirep, 1)

            def project(b, q):
                if not (isint(b) and b == 0):
                    act.wait_ge(s_ei, 2 * b)
                    act.wait_ge(s_Whp, 3 * b)
                for h in range(2):
                    act.wait_ge(s_xnt, 2 * b + h + 1)
                    copy(xnT[:, h * H:(h + 1) * H], tp[h][:, :]).then_inc(s_xnT, 1)
                for g in range(3):
                    act.wait_ge(s_Whp, 3 * b + g + 1)
                    n = min(3, NT - 3 * g)
                    copy(WhA[:, q, 3 * g:3 * g + n, 0:D], whp[:, 0:n, 0:D])
                    copy(ejc[:, q, 3 * g:3 * g + n], whp[:, 0:n, D]).then_inc(s_Whc, 1)

            def factors(b, q):
                act.wait_ge(s_cM, b + 1)
                act.activation(Bc[:, q, :], ejc[:, q, :], ACT.Exp, bias=cM[:, 0:1])
                act.activation(Dc[:, q, :], ejc[:, q, :], ACT.Exp, bias=cM[:, 1:2], scale=SLOPE).then_inc(s_BD, 1)
                for h in range(2):
                    act.wait_ge(s_ei, 2 * b + h + 1)
                    act.activation(crow[:, q, h * H:(h + 1) * H], tp[h][:, :], ACT.Exp, bias=cM[:, 2:3],
                                   scale=SLOPE - 1.0).then_inc(s_E1, 1)

            def over(b, q, jt):
                n = NT * b + jt
                if jt == 0:
                    act.wait_ge(s_crow, b + 1)
                    act.wait_ge(s_nB, b + 1)
                if not (isint(n) and n < 2):
                    act.wait_ge(s_PT, n - 1)
                act.activation(R[:, jt % 2, :], crow[:, q, :], ACT.Relu, bias=nBc[:, q, jt:jt + 1],
                               scale=Dc[:, q, jt:jt + 1]).then_inc(s_R, 1)

            def x2_copy(b):
                if not (isint(b) and b == 0):
                    act.wait_ge(s_lg, b)
                for h in range(2):
                    act.wait_ge(s_xn2t, 2 * b + h + 1)
                    copy(x2T[:, h * H:(h + 1) * H], tp[h][:, :]).then_inc(s_x2T, 1)

            def gate_exp(b):
                act.wait_ge(s_dm, b + 1)
                act.activation(ed[:, :], dm[:, :], ACT.Exp).then_inc(s_ed, 1)

            def split_weights(e):
                act.wait_ge(s_wraw[e % 2], 32 * (e // 2 + 1))
                if e >= 2:
                    act.wait_ge(s_wst[e % 2], 16 * (e // 2))
                    act.wait_ge(s_wlo, e - 1)
                copy(wst[:, e % 2, :, 0:F], wraw[:, e % 2, :, :]).then_inc(s_whi, 1)

            def ahead(nxt):
                project(nxt[0], nxt[1])
                factors(nxt[0], nxt[1])

            def attend(cur, fin, nxt):
                for jt in range(NT):
                    if cur:
                        over(cur[0], cur[1], jt)
                    if fin and jt == 2:
                        x2_copy(fin[0])
                    if fin and jt == 4:
                        gate_exp(fin[0])
                    if nxt and jt == 6:
                        project(nxt[0], nxt[1])
                if nxt:
                    factors(nxt[0], nxt[1])
                if not fin and nxt:
                    for e in range(E + 1):
                        split_weights(e)

            stage1(act, ahead, attend)

            def x_high(k, r):
                act.wait_ge(s_xT, k + 1)
                if not (isint(k) and k < 2):
                    act.wait_ge(s_hp, NC * (k - 1))
                copy(xh[:, r, :], xTp[:, :]).then_inc(s_xh, 1)

            def gelu(k, r, c):
                act.wait_ge(s_hp, NC * k + c + 1)
                if not (isint(k) and NC * k + c < 2):
                    act.wait_ge(s_hl, NC * k + c - 1)
                act.activation(hf[:, c % 2, :], hps[c][:, :], ACT.Gelu, bias=b1[:, r, c:c + 1]).then_inc(s_hf, 1)

            def result(k, r):
                act.wait_ge(s_yT, k + 1)
                if not (isint(k) and k == 0):
                    act.wait_ge(s_yR, k)
                act.activation(yTs[:, :], yTp[r][:, :], ACT.Identity, bias=b2[:, r, :]).then_inc(s_yTs, 1)

            def rows_out(k, r, half):
                act.wait_ge(s_yR, k + 1)
                if not (isint(k) and k < 2):
                    act.wait_ge(s_yst[r], 16 * half)
                copy(ys[:, r, :, :], yRp[:, :].rearrange("p (t d) -> p t d", d=D)).then_inc(s_ys, 1)

            def step(k, r, half):
                static = isint(k)
                if not static or 2 <= k:
                    result(k - 2, r)
                for c in range(NC):
                    if not static or k < NTILES:
                        gelu(k, r, c)
                    if c == 1 and (not static or k + 1 < NTILES):
                        x_high(k + 1, 1 - r)
                    if c == 3 and (not static or k >= 2):
                        rows_out(k - 2, r, half - 1)

            def loop():
                with act.Fori(1, PAIRS) as m:
                    step(2 * m + 2, 0, m + 1)
                    step(2 * m + 3, 1, m + 1)

            x_high(0, 0)
            stage2(lambda k, r: step(k, r, k // 2), loop)

        @block.vector
        def _(dve):
            dve.wait_ge(s_const, 1)
            dve.wait_ge(s_zero, 1)
            dve.tensor_copy(carry[:, :], base[:, 0, :]).then_inc(s_carry, 1)

            def ln_stats(k, b, src):
                L = lnt[:, k]
                alone(dve)
                for t in range(NT):
                    i = dve.bn_stats(stat[:, k, t, :], src(t))
                i.then_inc(s_stat[k], 1)
                dve.wait_ge(s_stat[k], b + 1)
                dve.tensor_tensor(L[:, 0, :], stat[:, k, :, 1], stat[:, k, :, 4], ALU.add)
                dve.tensor_tensor(L[:, 1, :], stat[:, k, :, 1], stat[:, k, :, 4], ALU.subtract)
                dve.tensor_tensor(L[:, 2, :], stat[:, k, :, 2], stat[:, k, :, 5], ALU.add).then_inc(s_lnsum[k], 1)
                dve.wait_ge(s_lnsum[k], b + 1)
                dve.tensor_scalar(L[:, 5, :], L[:, 0, :], 0.5, None, ALU.mult)
                dve.tensor_tensor(L[:, 3, :], L[:, 1, :], L[:, 1, :], ALU.mult).then_inc(s_lnsq[k], 1)
                dve.wait_ge(s_lnsq[k], b + 1)
                dve.scalar_tensor_tensor(L[:, 4, :], L[:, 3, :], D / 4.0, L[:, 2, :], ALU.mult, ALU.add).then_inc(s_var[k], 1)

            def ln_apply(k, b, src, dst, done):
                dve.wait_ge(s_rstd[k], b + 1)
                for t in range(NT):
                    i = dve.tensor_scalar(dst(t), src(t), lnt[:, k, 5, t:t + 1], lnt[:, k, 7, t:t + 1], ALU.subtract, ALU.mult)
                i.then_inc(done, 1)

            def rows(b):
                return lambda t: res[:, b * NT + t, :]

            def norm1_stats(b, q, half):
                dve.wait_ge(s_x[q], 16 * (half + 1))
                ln_stats(0, b, rows(b))

            def norm1(b):
                if not (isint(b) and b == 0):
                    dve.wait_ge(s_xnt, 2 * b)
                ln_apply(0, b, rows(b), lambda t: xn[:, t, :], s_xn)

            def mask(b, q, half):
                dve.wait_ge(s_adj[q], 32 * (half + 1))
                dve.tensor_scalar(adjm[:, q, :, :], adjm[:, q, :, :], 0.0, None, ALU.not_equal).then_inc(s_msk, 1)

            def factors(b, q):
                dve.wait_ge(s_Whc, 3 * b + 3)
                if not (isint(b) and b == 0):
                    dve.wait_ge(s_M, b)
                dve.tensor_reduce(mx[:, :], ejc[:, q, :], AX, ALU.max).then_inc(s_mx, 1)
                dve.wait_ge(s_M, b + 1)
                if not (isint(b) and b == 0):
                    dve.wait_ge(s_E1, 2 * b)
                dve.tensor_scalar(cM[:, :], coefM[:, :], Mb[:, 0:1], None, ALU.mult).then_inc(s_cM, 1)
                dve.wait_ge(s_BD, b + 1)
                dve.tensor_scalar(nBc[:, q, :], Bc[:, q, :], -1.0, None, ALU.mult).then_inc(s_nB, 1)
                dve.wait_ge(s_E1, 2 * b + 2)
                dve.tensor_scalar(crow[:, q, :], crow[:, q, :], 1.0, None, ALU.min).then_inc(s_crow, 1)

            def soft(b, q, jt):
                n = NT * b + jt
                dve.wait_ge(s_R, n + 1)
                dve.wait_ge(s_mT, n + 1)
                if not (isint(n) and n < 2):
                    dve.wait_ge(s_at, n - 1)
                dve.scalar_tensor_tensor(PT[:, jt % 2, :], R[:, jt % 2, :], Bc[:, q, jt:jt + 1], mT[jt % 2], ALU.add, ALU.mult).then_inc(s_PT, 1)

            def residual(b):
                dve.wait_ge(s_at, NT * (b + 1))
                for g in range(3):
                    n = min(3, NT - 3 * g)
                    i = dve.tensor_scalar(dens[:, g, 0:n], at[g][:, 0:n, D], TINY, None, ALU.max)
                i.then_inc(s_den, 1)
                dve.wait_ge(s_den, b + 1)
                for g in range(3):
                    n = min(3, NT - 3 * g)
                    i = dve.reciprocal(rden[:, g, 0:n], dens[:, g, 0:n])
                i.then_inc(s_rden, 1)
                dve.wait_ge(s_rden, b + 1)
                for t in range(NT):
                    i = dve.scalar_tensor_tensor(res[:, b * NT + t, :], at[t // 3][:, t % 3, 0:D], rden[:, t // 3, t % 3:t % 3 + 1],
                                                 res[:, b * NT + t, :], ALU.mult, ALU.add)
                i.then_inc(s_res, 1)

            def norm2_stats(b):
                dve.wait_ge(s_res, b + 1)
                ln_stats(1, b, rows(b))

            def norm2(b, q, half):
                if not (isint(half) and half == 0):
                    dve.wait_ge(s_scat[q], 16 * 2 * NT * half)
                    dve.wait_ge(s_shx[q], 16 * half)
                ln_apply(1, b, rows(b), lambda t: xn2[:, q, t, :], s_xn2)

            def over_e(v):
                return v.rearrange("p (t a) -> p t a", a=1).broadcast_to([P, NT, E])

            def route(b):
                def link(i, n):
                    i.then_inc(s_route, 1)
                    dve.wait_ge(s_route, 10 * b + n)
                dve.wait_ge(s_lg, b + 1)
                if not (isint(b) and b == 0):
                    dve.wait_ge(s_ed, b)
                link(dve.tensor_copy(Ls[:, 0, :, :], lgp), 1)
                for c in range(2):
                    link(dve.tensor_reduce(m12[:, c, :], Ls[:, c, :, :], AX, ALU.max), 5 * c + 2)
                    link(dve.tensor_tensor(eq[:, :, :], Ls[:, c, :, :], over_e(m12[:, c, :]), ALU.is_equal), 5 * c + 3)
                    link(dve.scalar_tensor_tensor(cand[:, :, :], eq[:, :, :], -float(E), iota_e[:, :, :], ALU.mult, ALU.add), 5 * c + 4)
                    link(dve.tensor_reduce(first[:, :], cand[:, :, :], AX, ALU.min), 5 * c + 5)
                    dve.tensor_copy(choice[:, c, bass.ds(b * NT, NT)], first[:, :])
                    if c == 0:
                        dve.tensor_tensor(oh[:, c, :, :], cand[:, :, :], over_e(first[:, :]), ALU.is_equal).then_inc(s_oh, 1)
                        dve.wait_ge(s_oh, 2 * b + 1)
                        link(dve.scalar_tensor_tensor(Ls[:, 1, :, :], oh[:, 0, :, :], -HUGE, Ls[:, 0, :, :], ALU.mult, ALU.add), 6)
                    else:
                        dve.tensor_tensor(oh[:, c, :, :], cand[:, :, :], over_e(first[:, :]), ALU.is_equal).then_inc(s_oh, 1)
                        dve.wait_ge(s_oh, 2 * b + 2)
                dve.tensor_tensor(mm[:, :, :], oh[:, 0, :, :], oh[:, 1, :, :], ALU.add).then_inc(s_mm, 1)
                dve.tensor_tensor(dm[:, :], m12[:, 1, :], m12[:, 0, :], ALU.subtract).then_inc(s_dm, 1)

            def queue(b, q):
                dve.wait_ge(s_ed, b + 1)
                dve.tensor_scalar(ed1[:, :], ed[:, :], 1.0, None, ALU.add).then_inc(s_gate, 1)
                dve.wait_ge(s_gate, 3 * b + 1)
                dve.reciprocal(gates[:, 0, bass.ds(b * NT, NT)], ed1[:, :]).then_inc(s_gate, 1)
                dve.wait_ge(s_gate, 3 * b + 2)
                dve.tensor_tensor(gates[:, 1, bass.ds(b * NT, NT)], ed[:, :], gates[:, 0, bass.ds(b * NT, NT)], ALU.mult).then_inc(s_gate, 1)
                dve.wait_ge(s_rank, b + 1)
                start = carry[:, :].rearrange("p (a e) -> p a e", a=1).broadcast_to([P, NT, E])
                dve.tensor_tensor(pos[:, :, :], lgp, start, ALU.add).then_inc(s_pos, 1)
                dve.wait_ge(s_pos, b + 1)
                dve.tensor_tensor(carry[:, :], carry[:, :], cntp, ALU.add).then_inc(s_carry, 1)
                for c in range(2):
                    i = dve.tensor_tensor(hit[:, c, :, :], oh[:, c, :, :], pos[:, :, :], ALU.mult)
                i.then_inc(s_hit, 1)
                dve.wait_ge(s_hit, 2 * b + 1)
                dve.tensor_reduce(slotf[:, :, :], hit[:, :, :, :], AX, ALU.add).then_inc(s_hit, 1)
                dve.wait_ge(s_hit, 2 * b + 2)
                dve.tensor_copy(sslot[:, q, :, :], slotf[:, :, :])
                dve.tensor_copy(slotall[:, :, bass.ds(b * NT, NT)], slotf[:, :, :]).then_inc(s_slot, 1)

            def tables(g):
                n = GT[g]
                t0 = TILE0[g]
                steps = [(17 + 2 * E) * g]

                def link(i):
                    i.then_inc(s_tstep, 1)
                    steps[0] += 1
                    dve.wait_ge(s_tstep, steps[0])
                dve.wait_ge(s_carry, 1 + sum(GROUPS[:g + 1]) + g)
                rowc = carry[:, :]
                link(dve.tensor_copy(tab_tail[:, g, :], rowc))
                link(dve.tensor_tensor(cnt[:, 0, :], rowc, base[:, g, :], ALU.subtract))
                link(dve.tensor_scalar(nti[:, 0, :], cnt[:, 0, :], float(T - 1), None, ALU.add))
                link(dve.tensor_scalar(nti[:, 1, :], nti[:, 0, :], TSH, None, ALU.arith_shift_right))
                link(dve.tensor_copy(cnt[:, 1, :], nti[:, 1, :]))
                link(dve.tensor_tensor_scan(cnt[:, 2, :], cnt[:, 1, :], zero_e[:, :], 0.0, ALU.add, ALU.add))

                def over_t(v):
                    return v.rearrange("p (a e) -> p a e", a=1).broadcast_to([P, n, E])
                link(dve.tensor_tensor(tge[:, 0, 0:n, :], iota_t[:, 0:n, :], over_t(cnt[:, 2, :]), ALU.is_ge))
                link(dve.tensor_tensor(tge[:, 1, 0:n, :], tge[:, 0, 0:n, :], over_t(cnt[:, 1, :]), ALU.mult))
                link(dve.tensor_reduce(tv[:, 0, 0:n], tge[:, 0, 0:n, :], AX, ALU.add))
                link(dve.tensor_reduce(tv[:, 1, 0:n], tge[:, 1, 0:n, :], AX, ALU.add))
                link(dve.tensor_tensor(tv[:, 2, 0:n], iota_t[:, 0:n, 0], tv[:, 1, 0:n], ALU.subtract))
                link(dve.tensor_scalar(tv[:, 3, 0:n], tv[:, 0, 0:n], float(REG[g]), float(GBASE[g]), ALU.mult, ALU.add))
                link(dve.scalar_tensor_tensor(tv[:, 4, 0:n], tv[:, 2, 0:n], float(T), tv[:, 3, 0:n], ALU.mult, ALU.add))
                link(dve.tensor_scalar(tab_x[:, t0:t0 + n], tv[:, 4, 0:n], float(GBASE[g] + E * REG[g]), None, ALU.min))
                dve.tensor_scalar(tab_e[:, t0:t0 + n], tv[:, 0, 0:n], float(E - 1), None, ALU.min).then_inc(s_tab, 1)
                dve.tensor_copy(carry[:, :], base[:, 1, :]).then_inc(s_carry, 1)
                u0, u1 = (sum(GROUPS[:i]) * NT for i in (g, g + 1))
                link(dve.tensor_tensor(cnt[:, 3, :], cnt[:, 2, :], cnt[:, 1, :], ALU.subtract))
                link(dve.scalar_tensor_tensor(cnt[:, 4, :], cnt[:, 3, :], float(T), base[:, g, :], ALU.mult, ALU.subtract))
                link(dve.tensor_copy(slotmv[:, 0, :, u0:u1], slotall[:, :, u0:u1]))
                for e in range(E):
                    link(dve.tensor_scalar(slotmv[:, 1, :, u0:u1], choice[:, :, u0:u1], float(e - E), cnt[:, 4, e:e + 1], ALU.is_equal, ALU.mult))
                    link(dve.tensor_tensor(slotmv[:, 0, :, u0:u1], slotmv[:, 0, :, u0:u1], slotmv[:, 1, :, u0:u1], ALU.add))
                dve.tensor_copy(slots[:, :, u0:u1], slotmv[:, 0, :, u0:u1]).then_inc(s_yslot, 1)

            def split_weights(e):
                dve.wait_ge(s_whi, e + 1)
                dve.tensor_tensor(wst[:, e % 2, :, F:2 * F], wraw[:, e % 2, :, :], wst[:, e % 2, :, 0:F].bitcast(F32),
                                  ALU.subtract).then_inc(s_wlo, 1)

            def ahead(nxt):
                b, q, half = nxt
                norm1_stats(b, q, half)
                norm1(b)
                factors(b, q)
                mask(b, q, half)

            def attend(cur, fin, nxt):
                if fin:
                    residual(fin[0])
                for jt in range(NT):
                    if cur:
                        soft(cur[0], cur[1], jt)
                    if fin and jt == 0:
                        norm2_stats(fin[0])
                    if fin and jt == 1:
                        norm2(*fin)
                    if not nxt and cur and jt == 2:
                        tables(0)
                    if nxt and jt == 2:
                        norm1_stats(*nxt)
                    if nxt and jt == 3:
                        norm1(nxt[0])
                    if fin and jt == 4:
                        route(fin[0])
                    if nxt and jt == 5:
                        mask(*nxt)
                    if fin and jt == 5:
                        queue(fin[0], fin[1])
                if nxt:
                    factors(nxt[0], nxt[1])
                if not fin and nxt:
                    for e in range(E + 1):
                        split_weights(e)
                if fin and isint(fin[0]):
                    if fin[0] == NB - 1:
                        tables(1)

            stage1(dve, ahead, attend)

            def x_low(k, r):
                dve.wait_ge(s_xh, k + 1)
                if not (isint(k) and k < 2):
                    dve.wait_ge(s_hp, NC * (k - 1))
                dve.tensor_tensor(xl[:, r, :], xTp[:, :], xh[:, r, :].bitcast(F32), ALU.subtract).then_inc(s_xl, 1)

            def h_split(k, r, c):
                dve.wait_ge(s_hf, NC * k + c + 1)
                if c == 0 and not (isint(k) and k < 2):
                    dve.wait_ge(s_yT, k - 1)
                dve.tensor_copy(hh[:, r, c, :], hf[:, c % 2, :]).then_inc(s_hh, 1)
                dve.wait_ge(s_hh, NC * k + c + 1)
                dve.tensor_tensor(hl[:, r, c, :], hf[:, c % 2, :], hh[:, r, c, :].bitcast(F32), ALU.subtract).then_inc(s_hl, 1)

            def step(k, r):
                static = isint(k)
                for c in range(NC):
                    if not static or k < NTILES:
                        h_split(k, r, c)
                    if c == 1 and (not static or k + 1 < NTILES):
                        x_low(k + 1, 1 - r)

            def combine(c):
                dve.wait_ge(s_gsh, 16 * (c + 1))
                dve.tensor_tensor(oa[:, :, :], gsh[:, :, :], res[:, bass.ds(c * COMB, COMB), :], ALU.add).then_inc(s_oa, 1)
                dve.wait_ge(s_oa, c + 1)
                for i in range(COMB):
                    dve.wait_ge(s_g[i], 32 * (c + 1))
                    x = dve.scalar_tensor_tensor(ob[:, i, :], g12[:, i, 0, :], gates[:, 0, bass.ds(c * COMB + i, 1)],
                                                 oa[:, i, :], ALU.mult, ALU.add)
                x.then_inc(s_ob, 1)
                dve.wait_ge(s_ob, c + 1)
                if not (isint(c) and c == 0):
                    dve.wait_ge(s_out, 16 * c)
                for i in range(COMB):
                    x = dve.scalar_tensor_tensor(ot[:, i, :], g12[:, i, 1, :], gates[:, 1, bass.ds(c * COMB + i, 1)],
                                                 ob[:, i, :], ALU.mult, ALU.add)
                x.then_inc(s_ot, 1)

            def loop():
                with dve.Fori(1, COMB_PAIR) as m:
                    step(2 * m + 2, 0)
                    step(2 * m + 3, 1)
                step(2 * COMB_PAIR + 2, 0)
                step(2 * COMB_PAIR + 3, 1)
                combine(0)
                with dve.Fori(COMB_PAIR + 1, PAIRS) as m:
                    step(2 * m + 2, 0)
                    step(2 * m + 3, 1)
                    combine(m - COMB_PAIR)

            x_low(0, 0)
            stage2(step, loop)
            with dve.Fori(ROUNDS_A, ROUNDS) as c:
                combine(c)


_INS = ["x", "adj", "L0_gnn_W", "L0_gnn_a", "L0_ffn_Wr", "L0_ffn_W1s", "L0_ffn_b1s", "L0_ffn_W2s", "L0_ffn_b2s",
        "L0_ffn_W1p", "L0_ffn_b1p", "L0_ffn_W2p", "L0_ffn_b2p"]


def kernel(**inputs):
    import numpy as _np
    import concourse.bacc as _bacc
    from concourse import mybir as _mybir
    from concourse.bass_utils import run_bass_kernel_spmd as _run

    nc = _bacc.Bacc("TRN2", target_bir_lowering=False, num_devices=1)
    arrays, args = {}, []
    for name in _INS:
        a = _np.ascontiguousarray(inputs[name])
        arrays[f"in_{name}_dram"] = a
        args.append(nc.dram_tensor(f"in_{name}_dram", a.shape, _mybir.dt.from_np(a.dtype), kind="ExternalInput").ap())
    args.append(nc.dram_tensor("out_0_dram", inputs["x"].shape, _mybir.dt.float32, kind="ExternalOutput").ap())
    gnn_moe_layer(nc, *args)
    r = _run(nc, [arrays], core_ids=[0])
    return r.results[0]["out_0_dram"]
```

```python
from contextlib import ExitStack

import concourse.bass as bass
from concourse import mybir

F32 = mybir.dt.float32
F32R = mybir.dt.float32r
BF16 = mybir.dt.bfloat16
I32 = mybir.dt.int32
U32 = mybir.dt.uint32
ALU = mybir.AluOpType
ACT = mybir.ActivationFunctionType
AX = mybir.AxisListType.X
RMAX = bass.bass_isa.ReduceOp.max

P = 128
SLOPE = 0.2
EPS = 1e-5
TINY = 1e-30
HUGE = 3.0e38


def gnn_moe_layer(nc, x, adj, gnn_W, gnn_a, Wr, W1s, b1s, W2s, b2s, W1p, b1p, W2p, b2p, out):
    NB, N, D = x.shape
    F = W1s.shape[1]
    E = Wr.shape[1]
    NT = N // P
    NC = F // P
    H = 512
    NH = N // H
    T = 512
    TB = T // P
    TSH = T.bit_length() - 1
    GROUPS = [NB - 2, 2]
    assert D == P and N % H == 0 and sum(GROUPS) == NB and 2 * D + 2 * D <= H

    GT = [(2 * g * N - E) // T + E for g in GROUPS]
    REG = [g * N + T for g in GROUPS]
    GBASE = [0, E * REG[0] + T]
    SHARED = GBASE[1] + E * REG[1] + T
    ROWS = SHARED + NB * N
    ST = NB * N // T
    TILE0 = [0, GT[0] + ST]
    NTILES = GT[0] + ST + GT[1]
    COMB = T // P
    ROUNDS = NB * NT // COMB
    ROUNDS_A = GROUPS[0] * NT // COMB
    PAIRS = NTILES // 2 - 2
    COMB_PAIR = PAIRS - ROUNDS_A
    B_PAIR = (TILE0[1] - 4) // 2
    PART0 = [0, GT[0], TILE0[1], NTILES]
    assert NTILES % 2 == 0 and 2 * COMB_PAIR > GT[0] + 2 and COMB_PAIR < B_PAIR < PAIRS
    edges = {1, COMB_PAIR, COMB_PAIR + 1, B_PAIR, B_PAIR + 1, PAIRS}
    for p in PART0[1:3]:
        edges |= {p // 2, (p + 1) // 2}
    edges = sorted(edges)
    GM = max(GT)

    ctx = ExitStack()
    with ctx:
        def sb(name, shape, dt):
            return ctx.enter_context(nc.sbuf_tensor(name, shape, dt))

        def sem(name):
            return ctx.enter_context(nc.semaphore(name))

        def sems(name, n=2):
            return [sem(f"{name}{i}") for i in range(n)]

        bank = [ctx.enter_context(nc.psum_tensor(f"bank{i}", [P, H], F32)) for i in range(8)]

        wsplit = nc.dram_tensor("wsplit", [E + 1, P, 2, 2 * F], F32, kind="Internal").ap()
        xrows = nc.dram_tensor("xrows", [ROWS, D], F32, kind="Internal").ap()
        yrows = [nc.dram_tensor(f"yrows{i}", [n * T, D], F32, kind="Internal").ap()
                 for i, n in enumerate((GT[0], ST, GT[1]))]

        ident = sb("ident", [P, P], F32)
        identb = sb("identb", [P, P], BF16)
        before = sb("before", [P, P], BF16)
        onesb = sb("onesb", [P, P], BF16)
        onesf = sb("onesf", [P, P], F32)
        coefM = sb("coefM", [P, 3], F32)
        minus_half = sb("minus_half", [P, NT], F32)
        iota_i = sb("iota_i", [P, NT, E], I32)
        iota_e = sb("iota_e", [P, NT, E], F32)
        base_i = sb("base_i", [P, 2, E], I32)
        base = sb("base", [P, 2, E], F32)
        iota_ti = sb("iota_ti", [P, GM, E], I32)
        iota_t = sb("iota_t", [P, GM, E], F32)
        zero_e = sb("zero_e", [P, E], F32)
        zrow = sb("zrow", [P, TB, D], F32)
        Wg = sb("Wg", [P, D], F32)
        acol = sb("acol", [P, 2], F32)
        WTa = sb("WTa", [P, D + 1], F32)
        wi = sb("wi", [P, 1], F32)
        wirep = sb("wirep", [P, P], F32)
        Wr_sb = sb("Wr_sb", [P, E], F32)
        NBR = (E + 1) * (NC + 1)
        brow = sb("brow", [NBR, P], F32)
        b1t = sb("b1t", [P, E + 1, NC], F32)
        b2t = sb("b2t", [P, E + 1], F32)
        wraw = sb("wraw", [P, 2, 2, F], F32)
        wst = sb("wst", [P, 2, 2, 2 * F], F32R)

        res = sb("res", [P, NB * NT, D], F32)
        adjm = sb("adjm", [P, 2, NT, N], BF16)
        stat = sb("stat", [P, 2, NT, 6], F32)
        lnt = sb("lnt", [P, 2, 8, NT], F32)
        xn = sb("xn", [P, NT, D], F32)
        xnT = sb("xnT", [P, N], F32)
        WhA = sb("WhA", [P, 2, NT, D + 1], F32)
        ejc = sb("ejc", [P, 2, NT], F32)
        mx = sb("mx", [P, 1], F32)
        Mb = sb("Mb", [P, 1], F32)
        cM = sb("cM", [P, 3], F32)
        Bc = sb("Bc", [P, 2, NT], F32)
        Dc = sb("Dc", [P, 2, NT], F32)
        nBc = sb("nBc", [P, 2, NT], F32)
        crow = sb("crow", [P, 2, N], F32)
        R = sb("R", [P, 2, N], F32)
        PT = sb("PT", [P, 2, N], F32)
        dens = sb("dens", [P, 3, 3], F32)
        rden = sb("rden", [P, 3, 3], F32)
        xn2 = sb("xn2", [P, 2, NT, D], F32)
        x2T = sb("x2T", [P, N], F32)
        Ls = sb("Ls", [P, 2, NT, E], F32)
        m12 = sb("m12", [P, 2, NT], F32)
        eq = sb("eq", [P, NT, E], F32)
        cand = sb("cand", [P, NT, E], F32)
        first = sb("first", [P, NT], F32)
        oh = sb("oh", [P, 2, NT, E], F32)
        mm = sb("mm", [P, NT, E], BF16)
        dm = sb("dm", [P, NT], F32)
        ed = sb("ed", [P, NT], F32)
        ed1 = sb("ed1", [P, NT], F32)
        gates = sb("gates", [P, 2, NB * NT], F32)
        pos = sb("pos", [P, NT, E], F32)
        hit = sb("hit", [P, 2, NT, E], F32)
        slotf = sb("slotf", [P, 2, NT], F32)
        choice = sb("choice", [P, 2, NB * NT], F32)
        slotall = sb("slotall", [P, 2, NB * NT], F32)
        slotmv = sb("slotmv", [P, 2, 2, NB * NT], F32)
        slots = sb("slots", [P, 2, NB * NT], U32)
        sslot = sb("sslot", [P, 2, 2, NT], U32)
        gslot = sb("gslot", [P, 2, COMB], U32)
        carry = sb("carry", [P, E], F32)

        nti = sb("nti", [P, 2, E], I32)
        cnt = sb("cnt", [P, 5, E], F32)
        tge = sb("tge", [P, 2, GM, E], F32)
        tv = sb("tv", [P, 5, GM], F32)
        tab_x = sb("tab_x", [P, NTILES], I32)
        tab_e = sb("tab_e", [P, NTILES], I32)
        tab_tail = sb("tab_tail", [P, 2, E], I32)

        w1, w2 = wst[:, :, 0, :], wst[:, :, 1, :]
        b1 = sb("b1", [P, 2, NC], F32)
        b2 = sb("b2", [P, 2, 1], F32)
        xh = sb("xh", [P, 2, T], F32R)
        xl = sb("xl", [P, 2, T], F32R)
        spare = adjm[:, :, :, :].rearrange("p q t n -> p (q t n)").bitcast(F32)
        taken = [0]

        def over_masks(*dims):
            size = 1
            for d in dims:
                size *= d
            v = spare[:, taken[0]:taken[0] + size]
            taken[0] += size
            if len(dims) == 2:
                v = v.rearrange("p (a b) -> p a b", a=dims[0])
            if len(dims) == 3:
                v = v.rearrange("p (a b c) -> p a b c", a=dims[0], b=dims[1])
            return v

        xs = over_masks(2, TB, D)
        hf = over_masks(2, T)
        yTs = over_masks(T)
        ys = over_masks(2, TB, D)
        g12 = over_masks(COMB, 2, D)
        gsh, oa, ob, ot = (over_masks(COMB, D) for _ in range(4))
        hh = sb("hh", [P, 2, NC, T], F32R)
        hl = sb("hl", [P, 2, NC, T], F32R)

        mT = [bank[i][:, :].bitcast(BF16) for i in (0, 1)]
        at = [bank[2 + i][:, 0:3 * (D + 1)].rearrange("p (t c) -> p t c", t=3) for i in range(3)]
        tp = [bank[5], bank[6]]
        ws = bank[7]
        whp = [tp[g % 2][:, 0:3 * (D + 1)].rearrange("p (t c) -> p t c", t=3) for g in range(3)]
        lgp = ws[:, 400:400 + NT * E].rearrange("p (t e) -> p t e", e=E)
        cntp = ws[:, 480:480 + E]
        hps = bank[0:4]
        yTp, xTp, yRp = (bank[4], bank[7]), bank[5], bank[6]

        s_zero, s_iota, s_const = sem("s_zero"), sem("s_iota"), sem("s_const")
        s_par, s_wt, s_wcopy, s_wirep = sem("s_par"), sem("s_wt"), sem("s_wcopy"), sem("s_wirep")
        s_brow, s_bT, s_btab = sem("s_brow"), sem("s_bT"), sem("s_btab")
        s_wraw, s_whi, s_wlo, s_wst = sems("s_wraw"), sem("s_whi"), sem("s_wlo"), sems("s_wst")
        s_x, s_adj, s_msk = sems("s_x"), [sems("s_adj_even"), sems("s_adj_odd")], sem("s_msk")
        s_stat, s_lnsum, s_lnsq, s_var = sems("s_stat"), sems("s_lnsum"), sems("s_lnsq"), sems("s_var")
        s_vareps, s_pow, s_rstd = sems("s_vareps"), sems("s_pow"), sems("s_rstd")
        s_xn, s_xnt, s_xnT, s_Whp, s_Whc, s_ei = (sem(n) for n in ("s_xn", "s_xnt", "s_xnT", "s_Whp", "s_Whc", "s_ei"))
        s_mx, s_M, s_cM, s_BD, s_nB, s_E1, s_crow = (sem(n) for n in ("s_mx", "s_M", "s_cM", "s_BD", "s_nB", "s_E1", "s_crow"))
        s_mT, s_R, s_PT, s_at = sem("s_mT"), sem("s_R"), sem("s_PT"), sem("s_at")
        s_den, s_rden, s_res = sem("s_den"), sem("s_rden"), sem("s_res")
        s_xn2, s_xn2t, s_x2T, s_lg, s_route, s_mm = (sem(n) for n in ("s_xn2", "s_xn2t", "s_x2T", "s_lg", "s_route", "s_mm"))
        s_yslot = sem("s_yslot")
        s_oh, s_hit, s_gslot = sem("s_oh"), sem("s_hit"), sems("s_gslot")
        s_dm, s_ed, s_gate, s_rank, s_pos, s_slot = (sem(n) for n in ("s_dm", "s_ed", "s_gate", "s_rank", "s_pos", "s_slot"))
        s_carry, s_scat, s_shx = sem("s_carry"), sems("s_scat"), sems("s_shx")
        s_tstep, s_tab, s_tabS, s_tail = sem("s_tstep"), sem("s_tab"), sem("s_tabS"), sem("s_tail")
        s_xin, s_w1, s_w2 = sems("s_xin"), sems("s_w1"), sems("s_w2")
        s_xT, s_xh, s_xl, s_hp, s_hf, s_hh, s_hl = (sem(n) for n in ("s_xT", "s_xh", "s_xl", "s_hp", "s_hf", "s_hh", "s_hl"))
        s_yT, s_yTs, s_yR, s_ys, s_yst = sem("s_yT"), sem("s_yTs"), sem("s_yR"), sem("s_ys"), sems("s_yst")
        s_g, s_gsh, s_oa, s_ob, s_ot, s_out = sems("s_g"), sem("s_gsh"), sem("s_oa"), sem("s_ob"), sem("s_ot"), sem("s_out")

        s_alone = sem("s_alone")
        block = ctx.enter_context(nc.Block())

        def stage1(eng, ahead, attend):
            def at(b):
                return b, b % 2, b // 2
            ahead(at(0))
            attend(at(0), None, at(1), None)
            attend(at(1), at(0), at(2), None)
            attend(at(2), at(1), at(3), at(0))
            with eng.Fori(1, NB // 2 - 1) as p:
                attend((2 * p + 1, 1, p), (2 * p, 0, p), (2 * p + 2, 0, p + 1), (2 * p - 1, 1, p - 1))
                attend((2 * p + 2, 0, p + 1), (2 * p + 1, 1, p), (2 * p + 3, 1, p + 1), (2 * p, 0, p))
            attend(at(NB - 1), at(NB - 2), None, at(NB - 3))
            attend(None, at(NB - 1), None, at(NB - 2))

        def following(cur, nxt, jt):
            return (cur, jt) if jt < NT else (nxt, jt - NT)

        def stage2(step, loop):
            for k in range(4):
                step(k, k % 2)
            loop()
            for k in range(NTILES - 2, NTILES + 2):
                step(k, k % 2)

        def pairs(eng, body):
            for lo, hi in zip(edges, edges[1:]):
                if hi - lo == 1:
                    body(lo, lo)
                else:
                    with eng.Fori(lo, hi) as m:
                        body(m, lo)

        def part_of(k):
            return sum(k >= p for p in PART0[1:3])

        def alone(eng):
            eng.sem_inc(s_alone, 1)

        def isint(v):
            return isinstance(v, int)

        @block.sync
        def _(sp):
            sp.dma_start(Wg[:, :], gnn_W).then_inc(s_par, 16)
            with nc.allow_non_contiguous_dma(reason="256 values once"):
                sp.dma_start(acol[:, :], gnn_a.rearrange("(k o) -> o k", k=2)).then_inc(s_par, 16)
            sp.dma_start(Wr_sb[:, :], Wr).then_inc(s_par, 16)

            def load_x(b, q, half):
                if not (isint(half) and half == 0):
                    sp.wait_ge(s_x[q], 16 * half)
                    alone(sp)
                sp.dma_start(res[:, bass.ds(b * NT, NT), :], x[b].rearrange("(t p) d -> p t d", p=P)).then_inc(s_x[q], 16)

            load_x(0, 0, 0)
            load_x(1, 1, 0)
            n1 = (E + 1) * NC
            sp.dma_start(brow[0:E * NC, :], b1p.rearrange("e (c p) -> (e c) p", p=P)).then_inc(s_brow, 16)
            sp.dma_start(brow[E * NC:n1, :], b1s.rearrange("(c p) -> c p", p=P)).then_inc(s_brow, 16)
            sp.dma_start(brow[n1:n1 + E, :], b2p).then_inc(s_brow, 16)
            sp.dma_start(brow[n1 + E:NBR, :], b2s.rearrange("(a p) -> a p", a=1)).then_inc(s_brow, 16)
            with sp.Fori(1, NB // 2) as h:
                load_x(2 * h, 0, h)
                load_x(2 * h + 1, 1, h)

            def raw_weights(e):
                if e >= 2:
                    sp.wait_ge(s_wlo, e - 1)
                src1, src2 = (W1p[e], W2p[e]) if e < E else (W1s, W2s)
                sp.dma_start(wraw[:, e % 2, 0, :], src1).then_inc(s_wraw[e % 2], 16)
                sp.dma_start(wraw[:, e % 2, 1, :].rearrange("p (c d) -> p c d", c=NC),
                             src2.rearrange("(c p) d -> p c d", p=P)).then_inc(s_wraw[e % 2], 16)

            raw_weights(0)
            for e in range(E + 1):
                if e < E:
                    raw_weights(e + 1)
                sp.wait_ge(s_wlo, e + 1)
                sp.dma_start(wsplit[e], wst[:, e % 2, :, :].bitcast(F32)).then_inc(s_wst[e % 2], 16)

            sp.wait_ge(s_zero, 1)
            for g in range(2):
                r = GBASE[g] + E * REG[g]
                sp.dma_start(xrows[r:r + T, :].rearrange("(k p) d -> p k d", p=P), zrow[:, :, :]).then_inc(s_tail, 16)

            def store_x2(b, q, half):
                sp.wait_ge(s_xn2, b + 1)
                alone(sp)
                if not (isint(half) and half == 0):
                    sp.wait_ge(s_shx[q], 16 * half)
                    alone(sp)
                sp.dma_start(xrows[bass.ds(SHARED + b * N, N), :].rearrange("(t p) d -> p t d", p=P),
                             xn2[:, q, :, :]).then_inc(s_shx[q], 16)

            store_x2(0, 0, 0)
            store_x2(1, 1, 0)
            with sp.Fori(1, NB // 2 - 1) as h:
                store_x2(2 * h, 0, h)
                store_x2(2 * h + 1, 1, h)

            def tails(g):
                sp.wait_ge(s_tab, g + 1)
                for e in range(E):
                    r = sp.value_load(tab_tail[0:1, g, e:e + 1], min_val=0, max_val=ROWS - T)
                    sp.dma_start(xrows[bass.ds(r, T), :].rearrange("(k p) d -> p k d", p=P),
                                 zrow[:, :, :]).then_inc(s_tail, 16)

            def filled(g):
                for q in range(2):
                    sp.wait_ge(s_scat[q], 16 * 2 * NT * sum(GROUPS[:g + 1]) // 2)
                sp.wait_ge(s_tail, 16 * (2 + E * (g + 1)))

            def load_rows(k, r):
                if not (isint(k) and k < 2):
                    sp.wait_ge(s_xT, k - 1)
                    alone(sp)
                row = sp.value_load(tab_x[0:1, bass.ds(k, 1)], min_val=0, max_val=ROWS - T)
                sp.dma_start(xs[:, r, :, :], xrows[bass.ds(row, T), :].rearrange("(k p) d -> p k d", p=P)).then_inc(s_xin[r], 16)

            def load_w1(k, r):
                e = sp.value_load(tab_e[0:1, bass.ds(k, 1)], min_val=0, max_val=E)
                if not (isint(k) and k < 2):
                    sp.wait_ge(s_hp, NC * (k - 1))
                    alone(sp)
                sp.dma_start(w1[:, r, :].bitcast(F32), wsplit[e, :, 0, :]).then_inc(s_w1[r], 16)
                if not (isint(k) and k < 2):
                    sp.wait_ge(s_hf, NC * (k - 1))
                    alone(sp)
                sp.dma_start(b1[:, r, :], b1t[:, e, :]).then_inc(s_w1[r], 16)

            def load_w2(k, r):
                e = sp.value_load(tab_e[0:1, bass.ds(k, 1)], min_val=0, max_val=E)
                if not (isint(k) and k < 2):
                    sp.wait_ge(s_yT, k - 1)
                    alone(sp)
                sp.dma_start(w2[:, r, :].bitcast(F32), wsplit[e, :, 1, :]).then_inc(s_w2[r], 16)
                if not (isint(k) and k < 2):
                    sp.wait_ge(s_yTs, k - 1)
                    alone(sp)
                sp.dma_start(b2[:, r, :], b2t[:, bass.ds(e, 1)]).then_inc(s_w2[r], 16)

            def step(k, r):
                if k + 1 < NTILES:
                    load_w1(k + 1, 1 - r)
                if k < NTILES:
                    load_w2(k, r)
                if k + 2 < NTILES:
                    load_rows(k + 2, r)

            def shared_rows(c, stored):
                if not (isint(c) and c == 0):
                    sp.wait_ge(s_oa, c)
                    alone(sp)
                for r in range(2):
                    sp.wait_ge(s_yst[r], 16 * stored)
                    alone(sp)
                sp.dma_start(gsh[:, :, :], yrows[1][bass.ds(c * T, T), :].rearrange("(k p) d -> p k d", p=P)).then_inc(s_gsh, 16)

            def store_out(c):
                sp.wait_ge(s_ot, c + 1)
                alone(sp)
                sp.dma_start(out.rearrange("b n d -> (b n) d")[bass.ds(c * T, T), :].rearrange("(k p) d -> p k d", p=P),
                             ot[:, :, :]).then_inc(s_out, 16)

            tails(0)
            filled(0)
            sp.wait_ge(s_mT, NB * NT)
            sp.wait_ge(s_wst[0], 16 * (E // 2 + 1))
            sp.wait_ge(s_wst[1], 16 * (E // 2))
            sp.wait_ge(s_btab, 1)
            sp.wait_ge(s_tabS, 2)
            load_rows(0, 0)
            load_rows(1, 1)
            load_w1(0, 0)
            step(0, 0)
            step(1, 1)
            store_x2(NB - 2, 0, NB // 2 - 1)
            store_x2(NB - 1, 1, NB // 2 - 1)
            tails(1)

            def pair(m, first):
                if first == B_PAIR and isint(m):
                    filled(1)
                load_w1(2 * m + 3, 1)
                load_w2(2 * m + 2, 0)
                load_rows(2 * m + 4, 0)
                if first > COMB_PAIR:
                    store_out(m - COMB_PAIR - 1)
                load_w1(2 * m + 4, 0)
                load_w2(2 * m + 3, 1)
                load_rows(2 * m + 5, 1)
                if first == COMB_PAIR:
                    shared_rows(0, m)
                if first >= COMB_PAIR:
                    shared_rows(m - COMB_PAIR + 1, m)

            for q in range(2):
                sp.wait_ge(s_shx[q], 16 * (NB // 2))
            step(2, 0)
            step(3, 1)
            pairs(sp, pair)
            for k in range(NTILES - 2, NTILES):
                step(k, k % 2)
            store_out(ROUNDS_A - 1)
            for c in range(ROUNDS_A, ROUNDS):
                store_out(c)
                if c + 1 < ROUNDS:
                    shared_rows(c + 1, NTILES // 2)
            sp.wait_ge(s_out, 16 * ROUNDS)


        @block.gpsimd
        def _(pool):
            pool.memset(ident[:, :], 0.0)
            pool.memset(identb[:, :], 0.0)
            pool.memset(before[:, :], 0.0)
            pool.memset(onesb[:, :], 1.0)
            pool.memset(onesf[:, :], 1.0)
            pool.memset(zero_e[:, :], 0.0)
            pool.memset(minus_half[:, :], -0.5)
            pool.memset(coefM[:, 0:1], -1.0)
            pool.memset(coefM[:, 1:2], -SLOPE)
            pool.memset(coefM[:, 2:3], SLOPE - 1.0)
            pool.memset(WhA[:, :, :, D:D + 1], 1.0)
            pool.memset(zrow[:, :, :], 0.0).then_inc(s_zero, 1)
            pool.iota(iota_i[:, :, :], [[0, NT], [1, E]], base=0, channel_multiplier=0)
            for g in range(2):
                pool.iota(base_i[:, g, :], [[REG[g], E]], base=GBASE[g], channel_multiplier=0)
            pool.iota(iota_ti[:, :, :], [[1, GM], [0, E]], base=0, channel_multiplier=0).then_inc(s_iota, 1)
            pool.wait_ge(s_zero, 1)
            pool.wait_ge(s_iota, 1)
            pool.affine_select(out=ident[:, :], in_=ident[:, :], compare_op=ALU.not_equal, fill=1.0,
                               base=0, pattern=[[-1, P]], channel_multiplier=1)
            pool.affine_select(out=identb[:, :], in_=identb[:, :], compare_op=ALU.not_equal, fill=1.0,
                               base=0, pattern=[[-1, P]], channel_multiplier=1)
            pool.affine_select(out=before[:, :], in_=before[:, :], compare_op=ALU.is_ge, fill=1.0,
                               base=0, pattern=[[-1, P]], channel_multiplier=1)
            pool.tensor_copy(iota_e[:, :, :], iota_i[:, :, :])
            pool.tensor_copy(base[:, :, :], base_i[:, :, :])
            pool.tensor_copy(iota_t[:, :, :], iota_ti[:, :, :]).then_inc(s_const, 1)
            s0, s1 = GT[0], GT[0] + ST
            pool.iota(tab_x[:, s0:s1], [[T, ST]], base=SHARED, channel_multiplier=0).then_inc(s_tabS, 1)
            pool.iota(tab_e[:, s0:s1], [[0, ST]], base=E, channel_multiplier=0).then_inc(s_tabS, 1)

            def load_adj(b, q, half):
                if not (isint(b) and b < 2):
                    pool.wait_ge(s_mT, NT * (b - 1))
                for k in range(2):
                    if not (isint(b) and b < 2):
                        pool.wait_ge(s_adj[q][k], 16 * half)
                    pool.dma_start(adjm[:, q, k * NT // 2:(k + 1) * NT // 2, :],
                                   adj[b].rearrange("(t p) n -> p t n", p=P)[:, k * NT // 2:(k + 1) * NT // 2, :]
                                   ).then_inc(s_adj[q][k], 16)

            def rstd(k, b):
                pool.wait_ge(s_var[k], b + 1)
                alone(pool)
                pool.tensor_scalar(lnt[:, k, 6, :], lnt[:, k, 4, :], 1.0 / D, EPS, ALU.mult, ALU.add).then_inc(s_vareps[k], 1)
                pool.wait_ge(s_vareps[k], b + 1)
                pool.tensor_tensor(lnt[:, k, 7, :], lnt[:, k, 6, :], minus_half[:, :], ALU.pow).then_inc(s_pow[k], 1)
                pool.wait_ge(s_pow[k], b + 1)
                pool.tensor_tensor(lnt[:, k, 3, :], lnt[:, k, 5, :], lnt[:, k, 7, :], ALU.mult).then_inc(s_rstd[k], 1)

            def batch_max(b):
                pool.wait_ge(s_mx, b + 1)
                if not (isint(b) and b == 0):
                    pool.wait_ge(s_cM, b)
                alone(pool)
                pool.partition_all_reduce(Mb[:, :], mx[:, :], P, RMAX).then_inc(s_M, 1)

            def scatter(b, q, lo, hi):
                if lo == 0:
                    pool.wait_ge(s_slot, b + 1)
                    pool.wait_ge(s_xn2, b + 1)
                    alone(pool)
                for i in range(lo, hi):
                    c, t = i // NT, i % NT
                    pool.indirect_dma_start(xrows, bass.IndirectOffsetOnAxis(ap=sslot[:, q, c, t:t + 1], axis=0),
                                            xn2[:, q, t, :], None).then_inc(s_scat[q], 16)

            def ahead(nxt):
                b, q, half = nxt
                rstd(0, b)
                batch_max(b)

            def attend(cur, fin, nxt, old):
                if nxt:
                    load_adj(*nxt)
                    rstd(0, nxt[0])
                if old:
                    scatter(old[0], old[1], 0, 3)
                if fin:
                    rstd(1, fin[0])
                if old:
                    scatter(old[0], old[1], 3, 6)
                if nxt:
                    batch_max(nxt[0])
                if old:
                    scatter(old[0], old[1], 6, 2 * NT)

            load_adj(0, 0, 0)
            stage1(pool, ahead, attend)
            scatter(NB - 1, (NB - 1) % 2, 0, 2 * NT)

            def gather(c, part):
                for ch in range(2):
                    if not (isint(c) and c == 0):
                        pool.wait_ge((s_ob, s_ot)[ch], c)
                        pool.wait_ge(s_g[ch], 16 * COMB * c)
                    pool.tensor_copy(gslot[:, ch, :], slots[:, ch, bass.ds(c * COMB, COMB)]).then_inc(s_gslot[ch], 1)
                    pool.wait_ge(s_gslot[ch], c + 1)
                    alone(pool)
                    for i in range(COMB):
                        pool.indirect_dma_start(g12[:, i, ch, :], None, yrows[part],
                                                bass.IndirectOffsetOnAxis(ap=gslot[:, ch, i:i + 1], axis=0)).then_inc(s_g[ch], 16)

            pool.wait_ge(s_yslot, 2)
            for r in range(2):
                pool.wait_ge(s_yst[r], 16 * ((GT[0] + 1 - r) // 2))
            gather(0, 0)
            with pool.Fori(1, ROUNDS_A) as c:
                gather(c, 0)
            for r in range(2):
                pool.wait_ge(s_yst[r], 16 * (NTILES // 2))
            with pool.Fori(ROUNDS_A, ROUNDS) as c:
                gather(c, 2)

        @block.tensor
        def _(pe):
            pe.wait_ge(s_const, 1)
            pe.wait_ge(s_par, 48)
            pe.transpose(tp[0][:, 0:P], Wg[:, :], ident[:, :])
            pe.matmul(ws[:, 0:2], Wg[:, :], acol[:, :], start=True, stop=True).then_inc(s_wt, 1)
            pe.wait_ge(s_brow, 64)
            pe.transpose(tp[1][:, 0:NBR], brow[:, :], ident[0:NBR, 0:NBR]).then_inc(s_bT, 1)
            pe.wait_ge(s_wirep, 1)
            pe.wait_ge(s_btab, 1)

            def xn_T(b):
                pe.wait_ge(s_xn, b + 1)
                if not (isint(b) and b == 0):
                    pe.wait_ge(s_E1, 2 * b)
                for t in range(NT):
                    i = pe.transpose(tp[t // 4][:, (t % 4) * P:(t % 4 + 1) * P], xn[:, t, :], ident[:, :])
                    if t % 4 == 3:
                        i.then_inc(s_xnt, 1)

            def project(b):
                for g in range(3):
                    pe.wait_ge(s_xnT, 2 * b + min(g, 1) + 1)
                    if g == 2:
                        pe.wait_ge(s_Whc, 3 * b + 1)
                    for t in range(3 * g, min(3 * g + 3, NT)):
                        i = pe.matmul(whp[g][:, t % 3, :], xnT[:, t * P:(t + 1) * P], WTa[:, :], start=True, stop=True)
                    i.then_inc(s_Whp, 1)

            def ei_rows(b):
                pe.wait_ge(s_Whc, 3 * b + 3)
                if not (isint(b) and b < 2):
                    pe.wait_ge(s_x2T, 2 * (b - 1))
                for h in range(NH):
                    pe.matmul(tp[h][:, :], wirep[:, :], xnT[:, h * H:(h + 1) * H], start=True, stop=True).then_inc(s_ei, 1)

            def mask_T(batch, jt):
                b, q, half = batch
                n = NT * b + jt
                if jt == 0:
                    pe.wait_ge(s_msk, 2 * b + 2)
                if not (isint(n) and n < 2):
                    pe.wait_ge(s_PT, n - 1)
                for t in range(NT):
                    i = pe.transpose(mT[jt % 2][:, t * P:(t + 1) * P], adjm[:, q, t, jt * P:(jt + 1) * P], identb[:, :])
                i.then_inc(s_mT, 1)

            def weigh(b, q, jt):
                pe.wait_ge(s_PT, NT * b + jt + 1)
                if jt == 0:
                    pe.wait_ge(s_Whc, 3 * b + 3)
                for t in range(NT):
                    if jt == 0 and t % 3 == 0 and not (isint(b) and b == 0):
                        pe.wait_ge(s_res, 3 * b - 2 + t // 3)
                    i = pe.matmul(at[t // 3][:, t % 3, :], PT[:, jt % 2, t * P:(t + 1) * P], WhA[:, q, jt, :],
                                  start=(jt == 0 and t % 3 == 0), stop=(jt == NT - 1), skip_group_check=True)
                i.then_inc(s_at, 1)

            def x2_T(b, q):
                pe.wait_ge(s_xn2, b + 1)
                if isint(b) and b == NB - 1:
                    pe.wait_ge(s_x2T, 2 * b)
                elif isint(b) and b == NB - 2:
                    pe.wait_ge(s_E1, 2 * NB)
                else:
                    pe.wait_ge(s_Whc, 3 * (b + 3))
                for t in range(NT):
                    i = pe.transpose(tp[t // 4][:, (t % 4) * P:(t % 4 + 1) * P], xn2[:, q, t, :], ident[:, :])
                    if t % 4 == 3:
                        i.then_inc(s_xn2t, 1)

            def logits(b):
                pe.wait_ge(s_x2T, 2 * b + 2)
                if not (isint(b) and b == 0):
                    pe.wait_ge(s_carry, b + 2 if isint(b) and b > GROUPS[0] else b + 1)
                for t in range(NT):
                    i = pe.matmul(lgp[:, t, :], x2T[:, t * P:(t + 1) * P], Wr_sb[:, :], start=True, stop=True)
                i.then_inc(s_lg, 1)

            def ranks(b):
                pe.wait_ge(s_mm, b + 1)
                pe.matmul(lgp[:, :, :], before[:, :], mm[:, :, :], start=True, stop=False, skip_group_check=True)
                for k in range(1, NT):
                    pe.matmul(lgp[:, k:NT, :], onesb[:, :], mm[:, 0:NT - k, :], start=False, stop=(k == NT - 1), skip_group_check=True)
                for t in range(NT):
                    i = pe.matmul(cntp, onesb[:, :], mm[:, t, :], start=(t == 0), stop=(t == NT - 1), skip_group_check=True)
                i.then_inc(s_rank, 1)

            def ahead(nxt):
                xn_T(nxt[0])
                project(nxt[0])
                ei_rows(nxt[0])
                mask_T(nxt, 0)
                mask_T(nxt, 1)

            def attend(cur, fin, nxt, old):
                for jt in range(NT):
                    if cur:
                        weigh(cur[0], cur[1], jt)
                    batch, tile = following(cur, nxt, jt + 2)
                    if batch:
                        mask_T(batch, tile)
                    if nxt and jt == 2:
                        xn_T(nxt[0])
                    if nxt and jt == 3:
                        project(nxt[0])
                    if fin and jt == 4:
                        x2_T(fin[0], fin[1])
                    if fin and jt == 5:
                        logits(fin[0])
                    if nxt and jt == 5:
                        ei_rows(nxt[0])
                    if fin and jt == 6:
                        ranks(fin[0])

            stage1(pe, ahead, attend)

            def split_product(o, wh, wl, xh_, xl_, start, stop):
                pe.matmul(o, wh, xh_, start=start, stop=False)
                pe.matmul(o, wh, xl_, start=False, stop=False)
                return pe.matmul(o, wl, xh_, start=False, stop=stop)

            def rows_T(k, r):
                pe.wait_ge(s_xin[r], 16 * (k // 2 + 1) if isint(k) else 16 * half_of[0])
                if not (isint(k) and k == 0):
                    pe.wait_ge(s_xl, k)
                for t in range(TB):
                    i = pe.transpose(xTp[:, t * P:(t + 1) * P], xs[:, r, t, :], ident[:, :])
                i.then_inc(s_xT, 1)

            def up(k, r, c):
                if c == 0:
                    pe.wait_ge(s_w1[r], 32 * (k // 2 + 1) if isint(k) else 32 * half_of[1])
                    pe.wait_ge(s_xl, k + 1)
                if not (isint(k) and k == 0):
                    pe.wait_ge(s_hf, NC * (k - 1) + c + 1)
                f = slice(c * P, (c + 1) * P)
                split_product(hps[c][:, :], w1[:, r, f], w1[:, r, F:][:, f], xh[:, r, :], xl[:, r, :], True, True).then_inc(s_hp, 1)

            def down(k, r, c):
                pe.wait_ge(s_hl, NC * k + c + 1)
                if c == 0:
                    pe.wait_ge(s_w2[r], 32 * (k // 2 + 1) if isint(k) else 32 * half_of[2])
                    if not (isint(k) and k < 2):
                        pe.wait_ge(s_yTs, k - 1)
                f = slice(c * P, (c + 1) * P)
                i = split_product(yTp[r][:, :], w2[:, r, f], w2[:, r, F:][:, f], hh[:, r, c, :], hl[:, r, c, :], c == 0, c == NC - 1)
                if c == NC - 1:
                    i.then_inc(s_yT, 1)

            def rows_back(k):
                pe.wait_ge(s_yTs, k + 1)
                if not (isint(k) and k == 0):
                    pe.wait_ge(s_ys, k)
                for t in range(TB):
                    i = pe.transpose(yRp[:, t * P:(t + 1) * P], yTs[:, t * P:(t + 1) * P], ident[:, :])
                i.then_inc(s_yR, 1)

            half_of = [None, None, None]

            def step(k, r):
                static = isint(k)
                for c in range(NC):
                    if not static or k < NTILES:
                        up(k, r, c)
                    if c == 1 and (not static or k + 1 < NTILES):
                        rows_T(k + 1, 1 - r)
                    if c == 2 and (not static or k >= 2):
                        rows_back(k - 2)
                    if not static or 1 <= k <= NTILES:
                        down(k - 1, 1 - r, c)

            def loop():
                with pe.Fori(1, PAIRS) as m:
                    half_of[:] = [m + 2, m + 2, m + 1]
                    step(2 * m + 2, 0)
                    half_of[:] = [m + 3, m + 2, m + 2]
                    step(2 * m + 3, 1)

            pe.wait_ge(s_pos, NB)
            pe.wait_ge(s_carry, NB + 2)
            rows_T(0, 0)
            stage2(step, loop)

        @block.scalar
        def _(act):
            def copy(o, i):
                return act.activation(o, i, ACT.Copy)

            act.wait_ge(s_wt, 1)
            copy(WTa[:, 0:D], tp[0][:, 0:P])
            copy(WTa[:, D:D + 1], ws[:, 1:2])
            copy(wi[:, :], ws[:, 0:1]).then_inc(s_wcopy, 1)
            act.wait_ge(s_bT, 1)
            copy(b1t[:, :, :], tp[1][:, 0:(E + 1) * NC].rearrange("p (e c) -> p e c", c=NC))
            copy(b2t[:, :], tp[1][:, (E + 1) * NC:NBR]).then_inc(s_btab, 1)
            act.wait_ge(s_wcopy, 1)
            act.activation(wirep[:, :], onesf[:, :], ACT.Copy, scale=wi[:, :]).then_inc(s_wirep, 1)

            def normalize(k, b, dst, done):
                act.wait_ge(s_rstd[k], b + 1)
                alone(act)
                for t in range(NT):
                    i = act.activation(dst(t), res[:, b * NT + t, :], ACT.Identity, bias=lnt[:, k, 3, t:t + 1], scale=lnt[:, k, 7, t:t + 1])
                i.then_inc(done, 1)

            def norm1(b):
                if not (isint(b) and b == 0):
                    act.wait_ge(s_xnt, 2 * b)
                normalize(0, b, lambda t: xn[:, t, :], s_xn)

            def norm2(b, q, half):
                if not (isint(half) and half == 0):
                    act.wait_ge(s_scat[q], 16 * 2 * NT * half)
                    act.wait_ge(s_shx[q], 16 * half)
                normalize(1, b, lambda t: xn2[:, q, t, :], s_xn2)

            def xn_copy(b):
                if not (isint(b) and b == 0):
                    act.wait_ge(s_ei, 2 * b)
                for h in range(2):
                    act.wait_ge(s_xnt, 2 * b + h + 1)
                    copy(xnT[:, h * H:(h + 1) * H], tp[h][:, :]).then_inc(s_xnT, 1)

            def wh_copy(b, q):
                if not (isint(b) and b < 2):
                    act.wait_ge(s_at, NT * (b - 1))
                for g in range(3):
                    act.wait_ge(s_Whp, 3 * b + g + 1)
                    n = min(3, NT - 3 * g)
                    copy(WhA[:, q, 3 * g:3 * g + n, 0:D], whp[g][:, 0:n, 0:D])
                    copy(ejc[:, q, 3 * g:3 * g + n], whp[g][:, 0:n, D]).then_inc(s_Whc, 1)

            def factors(b, q):
                act.wait_ge(s_cM, b + 1)
                if not (isint(b) and b < 2):
                    act.wait_ge(s_PT, NT * (b - 1))
                act.activation(Bc[:, q, :], ejc[:, q, :], ACT.Exp, bias=cM[:, 0:1])
                act.activation(Dc[:, q, :], ejc[:, q, :], ACT.Exp, bias=cM[:, 1:2], scale=SLOPE).then_inc(s_BD, 1)

            def row_factor(b, q):
                for h in range(2):
                    act.wait_ge(s_ei, 2 * b + h + 1)
                    act.activation(crow[:, q, h * H:(h + 1) * H], tp[h][:, :], ACT.Exp, bias=cM[:, 2:3],
                                   scale=SLOPE - 1.0).then_inc(s_E1, 1)

            def over(batch, jt):
                b, q, half = batch
                n = NT * b + jt
                if jt == 0:
                    act.wait_ge(s_crow, b + 1)
                    act.wait_ge(s_nB, b + 1)
                if not (isint(n) and n < 2):
                    act.wait_ge(s_PT, n - 1)
                act.activation(R[:, jt % 2, :], crow[:, q, :], ACT.Relu, bias=nBc[:, q, jt:jt + 1],
                               scale=Dc[:, q, jt:jt + 1]).then_inc(s_R, 1)

            def x2_copy(b):
                if not (isint(b) and b == 0):
                    act.wait_ge(s_lg, b)
                for h in range(2):
                    act.wait_ge(s_xn2t, 2 * b + h + 1)
                    copy(x2T[:, h * H:(h + 1) * H], tp[h][:, :]).then_inc(s_x2T, 1)

            def gate_exp(b):
                act.wait_ge(s_dm, b + 1)
                act.activation(ed[:, :], dm[:, :], ACT.Exp).then_inc(s_ed, 1)

            def split_weights(e):
                act.wait_ge(s_wraw[e % 2], 32 * (e // 2 + 1))
                if e >= 2:
                    act.wait_ge(s_wst[e % 2], 16 * (e // 2))
                    act.wait_ge(s_wlo, e - 1)
                copy(wst[:, e % 2, :, 0:F], wraw[:, e % 2, :, :]).then_inc(s_whi, 1)

            def ahead(nxt):
                b, q, half = nxt
                norm1(b)
                xn_copy(b)
                wh_copy(b, q)
                factors(b, q)
                row_factor(b, q)
                over(nxt, 0)
                over(nxt, 1)

            def attend(cur, fin, nxt, old):
                for jt in range(NT):
                    batch, tile = following(cur, nxt, jt + 2)
                    if batch:
                        over(batch, tile)
                    if nxt and jt == 1:
                        norm1(nxt[0])
                    if nxt and jt == 2:
                        xn_copy(nxt[0])
                    if fin and jt == 3:
                        norm2(*fin)
                    if nxt and jt == 3:
                        wh_copy(nxt[0], nxt[1])
                    if fin and jt == 4:
                        x2_copy(fin[0])
                    if nxt and jt == 5:
                        factors(nxt[0], nxt[1])
                        row_factor(nxt[0], nxt[1])
                    if fin and jt == 6:
                        gate_exp(fin[0])
                    if not fin:
                        split_weights(jt)
                if not fin:
                    split_weights(E)

            stage1(act, ahead, attend)

            def x_high(k, r):
                act.wait_ge(s_xT, k + 1)
                if not (isint(k) and k < 2):
                    act.wait_ge(s_hp, NC * (k - 1))
                copy(xh[:, r, :], xTp[:, :]).then_inc(s_xh, 1)

            def gelu(k, r, c):
                act.wait_ge(s_hp, NC * k + c + 1)
                if not (isint(k) and NC * k + c < 2):
                    act.wait_ge(s_hl, NC * k + c - 1)
                act.activation(hf[:, c % 2, :], hps[c][:, :], ACT.Gelu, bias=b1[:, r, c:c + 1]).then_inc(s_hf, 1)

            def result(k, r):
                act.wait_ge(s_yT, k + 1)
                if not (isint(k) and k == 0):
                    act.wait_ge(s_yR, k)
                act.activation(yTs[:, :], yTp[r][:, :], ACT.Identity, bias=b2[:, r, :]).then_inc(s_yTs, 1)

            def rows_out(k, r, half, part):
                act.wait_ge(s_yR, k + 1)
                if not (isint(k) and k < 2):
                    act.wait_ge(s_yst[r], 16 * half)
                copy(ys[:, r, :, :], yRp[:, :].rearrange("p (t d) -> p t d", d=D)).then_inc(s_ys, 1)
                act.wait_ge(s_ys, k + 1)
                alone(act)
                act.dma_start(yrows[part][bass.ds((k - PART0[part]) * T, T), :].rearrange("(k p) d -> p k d", p=P),
                              ys[:, r, :, :]).then_inc(s_yst[r], 16)

            def step(k, r, half, part=None):
                static = isint(k)
                if not static or 2 <= k:
                    result(k - 2, r)
                for c in range(NC):
                    if not static or k < NTILES:
                        gelu(k, r, c)
                    if c == 1 and (not static or k + 1 < NTILES):
                        x_high(k + 1, 1 - r)
                    if c == 3 and (not static or k >= 2):
                        rows_out(k - 2, r, half - 1, part_of(k - 2) if static else part)

            def pair(m, first):
                step(2 * m + 2, 0, m + 1, part_of(2 * first))
                step(2 * m + 3, 1, m + 1, part_of(2 * first + 1))

            x_high(0, 0)
            stage2(lambda k, r: step(k, r, k // 2), lambda: pairs(act, pair))

        @block.vector
        def _(dve):
            dve.wait_ge(s_const, 1)
            dve.wait_ge(s_zero, 1)
            dve.tensor_copy(carry[:, :], base[:, 0, :]).then_inc(s_carry, 1)

            def ln_stats(k, b, src):
                L = lnt[:, k]
                alone(dve)
                for t in range(NT):
                    i = dve.bn_stats(stat[:, k, t, :], src(t))
                i.then_inc(s_stat[k], 1)
                dve.wait_ge(s_stat[k], b + 1)
                dve.tensor_tensor(L[:, 0, :], stat[:, k, :, 1], stat[:, k, :, 4], ALU.add)
                dve.tensor_tensor(L[:, 1, :], stat[:, k, :, 1], stat[:, k, :, 4], ALU.subtract)
                dve.tensor_tensor(L[:, 2, :], stat[:, k, :, 2], stat[:, k, :, 5], ALU.add).then_inc(s_lnsum[k], 1)
                dve.wait_ge(s_lnsum[k], b + 1)
                dve.tensor_scalar(L[:, 5, :], L[:, 0, :], -0.5, None, ALU.mult)
                dve.tensor_tensor(L[:, 3, :], L[:, 1, :], L[:, 1, :], ALU.mult).then_inc(s_lnsq[k], 1)
                dve.wait_ge(s_lnsq[k], b + 1)
                dve.scalar_tensor_tensor(L[:, 4, :], L[:, 3, :], D / 4.0, L[:, 2, :], ALU.mult, ALU.add).then_inc(s_var[k], 1)

            def rows(b):
                return lambda t: res[:, b * NT + t, :]

            def norm1_stats(b, q, half):
                dve.wait_ge(s_x[q], 16 * (half + 1))
                ln_stats(0, b, rows(b))

            def mask(b, q, half, k):
                dve.wait_ge(s_adj[q][k], 16 * (half + 1))
                part = adjm[:, q, k * NT // 2:(k + 1) * NT // 2, :]
                dve.tensor_scalar(part, part, 0.0, None, ALU.not_equal).then_inc(s_msk, 1)

            def largest(b, q):
                dve.wait_ge(s_Whc, 3 * b + 3)
                if not (isint(b) and b == 0):
                    dve.wait_ge(s_M, b)
                dve.tensor_reduce(mx[:, :], ejc[:, q, :], AX, ALU.max).then_inc(s_mx, 1)

            def offsets(b):
                dve.wait_ge(s_M, b + 1)
                if not (isint(b) and b == 0):
                    dve.wait_ge(s_E1, 2 * b)
                dve.tensor_scalar(cM[:, :], coefM[:, :], Mb[:, 0:1], None, ALU.mult).then_inc(s_cM, 1)

            def factors(b, q):
                dve.wait_ge(s_BD, b + 1)
                dve.tensor_scalar(nBc[:, q, :], Bc[:, q, :], -1.0, None, ALU.mult).then_inc(s_nB, 1)
                dve.wait_ge(s_E1, 2 * b + 2)
                dve.tensor_scalar(crow[:, q, :], crow[:, q, :], 1.0, None, ALU.min).then_inc(s_crow, 1)

            def soft(batch, jt):
                b, q, half = batch
                n = NT * b + jt
                dve.wait_ge(s_R, n + 1)
                dve.wait_ge(s_mT, n + 1)
                if not (isint(n) and n < 2):
                    dve.wait_ge(s_at, n - 1)
                dve.scalar_tensor_tensor(PT[:, jt % 2, :], R[:, jt % 2, :], Bc[:, q, jt:jt + 1], mT[jt % 2], ALU.add, ALU.mult).then_inc(s_PT, 1)

            def residual(b):
                dve.wait_ge(s_at, NT * (b + 1))
                for g in range(3):
                    n = min(3, NT - 3 * g)
                    i = dve.tensor_scalar(dens[:, g, 0:n], at[g][:, 0:n, D], TINY, None, ALU.max)
                i.then_inc(s_den, 1)
                dve.wait_ge(s_den, b + 1)
                for g in range(3):
                    n = min(3, NT - 3 * g)
                    i = dve.reciprocal(rden[:, g, 0:n], dens[:, g, 0:n])
                i.then_inc(s_rden, 1)
                dve.wait_ge(s_rden, b + 1)
                for t in range(NT):
                    i = dve.scalar_tensor_tensor(res[:, b * NT + t, :], at[t // 3][:, t % 3, 0:D], rden[:, t // 3, t % 3:t % 3 + 1],
                                                 res[:, b * NT + t, :], ALU.mult, ALU.add)
                    if t % 3 == 2 or t == NT - 1:
                        i.then_inc(s_res, 1)

            def norm2_stats(b):
                dve.wait_ge(s_res, 3 * b + 3)
                ln_stats(1, b, rows(b))

            def over_e(v):
                return v.rearrange("p (t a) -> p t a", a=1).broadcast_to([P, NT, E])

            def route(b, choices):
                def link(i, n):
                    i.then_inc(s_route, 1)
                    dve.wait_ge(s_route, 10 * b + n)
                if choices[0] == 0:
                    dve.wait_ge(s_lg, b + 1)
                    link(dve.tensor_copy(Ls[:, 0, :, :], lgp), 1)
                for c in choices:
                    link(dve.tensor_reduce(m12[:, c, :], Ls[:, c, :, :], AX, ALU.max), 5 * c + 2)
                    link(dve.tensor_tensor(eq[:, :, :], Ls[:, c, :, :], over_e(m12[:, c, :]), ALU.is_equal), 5 * c + 3)
                    link(dve.scalar_tensor_tensor(cand[:, :, :], eq[:, :, :], -float(E), iota_e[:, :, :], ALU.mult, ALU.add), 5 * c + 4)
                    link(dve.tensor_reduce(first[:, :], cand[:, :, :], AX, ALU.min), 5 * c + 5)
                    dve.tensor_copy(choice[:, c, bass.ds(b * NT, NT)], first[:, :])
                    if c == 0:
                        dve.tensor_tensor(oh[:, c, :, :], cand[:, :, :], over_e(first[:, :]), ALU.is_equal).then_inc(s_oh, 1)
                        dve.wait_ge(s_oh, 2 * b + 1)
                        link(dve.scalar_tensor_tensor(Ls[:, 1, :, :], oh[:, 0, :, :], -HUGE, Ls[:, 0, :, :], ALU.mult, ALU.add), 6)
                    else:
                        dve.tensor_tensor(oh[:, c, :, :], cand[:, :, :], over_e(first[:, :]), ALU.is_equal).then_inc(s_oh, 1)
                        dve.wait_ge(s_oh, 2 * b + 2)
                        dve.tensor_tensor(mm[:, :, :], oh[:, 0, :, :], oh[:, 1, :, :], ALU.add).then_inc(s_mm, 1)
                        if not (isint(b) and b == 0):
                            dve.wait_ge(s_ed, b)
                        dve.tensor_tensor(dm[:, :], m12[:, 1, :], m12[:, 0, :], ALU.subtract).then_inc(s_dm, 1)

            def queue(b, q):
                dve.wait_ge(s_ed, b + 1)
                dve.tensor_scalar(ed1[:, :], ed[:, :], 1.0, None, ALU.add).then_inc(s_gate, 1)
                dve.wait_ge(s_gate, 3 * b + 1)
                dve.reciprocal(gates[:, 0, bass.ds(b * NT, NT)], ed1[:, :]).then_inc(s_gate, 1)
                dve.wait_ge(s_gate, 3 * b + 2)
                dve.tensor_tensor(gates[:, 1, bass.ds(b * NT, NT)], ed[:, :], gates[:, 0, bass.ds(b * NT, NT)], ALU.mult).then_inc(s_gate, 1)
                dve.wait_ge(s_rank, b + 1)
                start = carry[:, :].rearrange("p (a e) -> p a e", a=1).broadcast_to([P, NT, E])
                dve.tensor_tensor(pos[:, :, :], lgp, start, ALU.add).then_inc(s_pos, 1)
                dve.wait_ge(s_pos, b + 1)
                dve.tensor_tensor(carry[:, :], carry[:, :], cntp, ALU.add).then_inc(s_carry, 1)
                for c in range(2):
                    i = dve.tensor_tensor(hit[:, c, :, :], oh[:, c, :, :], pos[:, :, :], ALU.mult)
                i.then_inc(s_hit, 1)
                dve.wait_ge(s_hit, 2 * b + 1)
                dve.tensor_reduce(slotf[:, :, :], hit[:, :, :, :], AX, ALU.add).then_inc(s_hit, 1)
                dve.wait_ge(s_hit, 2 * b + 2)
                dve.tensor_copy(sslot[:, q, :, :], slotf[:, :, :])
                dve.tensor_copy(slotall[:, :, bass.ds(b * NT, NT)], slotf[:, :, :]).then_inc(s_slot, 1)

            def tables(g):
                n = GT[g]
                t0 = TILE0[g]
                steps = [(17 + 2 * E) * g]

                def link(i):
                    i.then_inc(s_tstep, 1)
                    steps[0] += 1
                    dve.wait_ge(s_tstep, steps[0])
                dve.wait_ge(s_carry, 1 + sum(GROUPS[:g + 1]) + g)
                rowc = carry[:, :]
                link(dve.tensor_copy(tab_tail[:, g, :], rowc))
                link(dve.tensor_tensor(cnt[:, 0, :], rowc, base[:, g, :], ALU.subtract))
                link(dve.tensor_scalar(nti[:, 0, :], cnt[:, 0, :], float(T - 1), None, ALU.add))
                link(dve.tensor_scalar(nti[:, 1, :], nti[:, 0, :], TSH, None, ALU.arith_shift_right))
                link(dve.tensor_copy(cnt[:, 1, :], nti[:, 1, :]))
                link(dve.tensor_tensor_scan(cnt[:, 2, :], cnt[:, 1, :], zero_e[:, :], 0.0, ALU.add, ALU.add))

                def over_t(v):
                    return v.rearrange("p (a e) -> p a e", a=1).broadcast_to([P, n, E])
                link(dve.tensor_tensor(tge[:, 0, 0:n, :], iota_t[:, 0:n, :], over_t(cnt[:, 2, :]), ALU.is_ge))
                link(dve.tensor_tensor(tge[:, 1, 0:n, :], tge[:, 0, 0:n, :], over_t(cnt[:, 1, :]), ALU.mult))
                link(dve.tensor_reduce(tv[:, 0, 0:n], tge[:, 0, 0:n, :], AX, ALU.add))
                link(dve.tensor_reduce(tv[:, 1, 0:n], tge[:, 1, 0:n, :], AX, ALU.add))
                link(dve.tensor_tensor(tv[:, 2, 0:n], iota_t[:, 0:n, 0], tv[:, 1, 0:n], ALU.subtract))
                link(dve.tensor_scalar(tv[:, 3, 0:n], tv[:, 0, 0:n], float(REG[g]), float(GBASE[g]), ALU.mult, ALU.add))
                link(dve.scalar_tensor_tensor(tv[:, 4, 0:n], tv[:, 2, 0:n], float(T), tv[:, 3, 0:n], ALU.mult, ALU.add))
                link(dve.tensor_scalar(tab_x[:, t0:t0 + n], tv[:, 4, 0:n], float(GBASE[g] + E * REG[g]), None, ALU.min))
                dve.tensor_scalar(tab_e[:, t0:t0 + n], tv[:, 0, 0:n], float(E - 1), None, ALU.min).then_inc(s_tab, 1)
                dve.tensor_copy(carry[:, :], base[:, 1, :]).then_inc(s_carry, 1)
                u0, u1 = (sum(GROUPS[:i]) * NT for i in (g, g + 1))
                link(dve.tensor_tensor(cnt[:, 3, :], cnt[:, 2, :], cnt[:, 1, :], ALU.subtract))
                link(dve.scalar_tensor_tensor(cnt[:, 4, :], cnt[:, 3, :], float(T), base[:, g, :], ALU.mult, ALU.subtract))
                link(dve.tensor_copy(slotmv[:, 0, :, u0:u1], slotall[:, :, u0:u1]))
                for e in range(E):
                    link(dve.tensor_scalar(slotmv[:, 1, :, u0:u1], choice[:, :, u0:u1], float(e - E), cnt[:, 4, e:e + 1], ALU.is_equal, ALU.mult))
                    link(dve.tensor_tensor(slotmv[:, 0, :, u0:u1], slotmv[:, 0, :, u0:u1], slotmv[:, 1, :, u0:u1], ALU.add))
                dve.tensor_copy(slots[:, :, u0:u1], slotmv[:, 0, :, u0:u1]).then_inc(s_yslot, 1)

            def split_weights(e):
                dve.wait_ge(s_whi, e + 1)
                dve.tensor_tensor(wst[:, e % 2, :, F:2 * F], wraw[:, e % 2, :, :], wst[:, e % 2, :, 0:F].bitcast(F32),
                                  ALU.subtract).then_inc(s_wlo, 1)

            def ahead(nxt):
                b, q, half = nxt
                norm1_stats(b, q, half)
                largest(b, q)
                offsets(b)
                factors(b, q)
                for k in range(2):
                    mask(b, q, half, k)
                soft(nxt, 0)

            def attend(cur, fin, nxt, old):
                if nxt:
                    norm1_stats(*nxt)
                if fin:
                    residual(fin[0])
                for jt in range(NT):
                    batch, tile = following(cur, nxt, jt + 1)
                    if batch:
                        soft(batch, tile)
                    if fin and jt == 1:
                        norm2_stats(fin[0])
                    if not nxt and cur and jt == 2:
                        tables(0)
                    if nxt and jt == 3:
                        mask(*nxt, 0)
                    if nxt and jt == 4:
                        largest(nxt[0], nxt[1])
                        mask(*nxt, 1)
                    if nxt and jt == 5:
                        offsets(nxt[0])
                    if fin and jt == 5:
                        route(fin[0], [0])
                    if nxt and jt == 6:
                        factors(nxt[0], nxt[1])
                    if fin and jt == 6:
                        route(fin[0], [1])
                    if fin and jt == 7:
                        queue(fin[0], fin[1])
                    if not fin:
                        split_weights(jt)
                if not fin:
                    split_weights(E)
                if not cur:
                    tables(1)

            stage1(dve, ahead, attend)

            def x_low(k, r):
                dve.wait_ge(s_xh, k + 1)
                if not (isint(k) and k < 2):
                    dve.wait_ge(s_hp, NC * (k - 1))
                dve.tensor_tensor(xl[:, r, :], xTp[:, :], xh[:, r, :].bitcast(F32), ALU.subtract).then_inc(s_xl, 1)

            def h_split(k, r, c):
                dve.wait_ge(s_hf, NC * k + c + 1)
                if c == 0 and not (isint(k) and k < 2):
                    dve.wait_ge(s_yT, k - 1)
                dve.tensor_copy(hh[:, r, c, :], hf[:, c % 2, :]).then_inc(s_hh, 1)
                dve.wait_ge(s_hh, NC * k + c + 1)
                dve.tensor_tensor(hl[:, r, c, :], hf[:, c % 2, :], hh[:, r, c, :].bitcast(F32), ALU.subtract).then_inc(s_hl, 1)

            def step(k, r):
                static = isint(k)
                for c in range(NC):
                    if not static or k < NTILES:
                        h_split(k, r, c)
                    if c == 1 and (not static or k + 1 < NTILES):
                        x_low(k + 1, 1 - r)

            def combine_first(c):
                dve.wait_ge(s_gsh, 16 * (c + 1))
                dve.tensor_tensor(oa[:, :, :], gsh[:, :, :], res[:, bass.ds(c * COMB, COMB), :], ALU.add).then_inc(s_oa, 1)
                dve.wait_ge(s_oa, c + 1)
                dve.wait_ge(s_g[0], 16 * COMB * (c + 1))
                for i in range(COMB):
                    x = dve.scalar_tensor_tensor(ob[:, i, :], g12[:, i, 0, :], gates[:, 0, bass.ds(c * COMB + i, 1)],
                                                 oa[:, i, :], ALU.mult, ALU.add)
                x.then_inc(s_ob, 1)

            def combine_second(c):
                dve.wait_ge(s_ob, c + 1)
                dve.wait_ge(s_g[1], 16 * COMB * (c + 1))
                if not (isint(c) and c == 0):
                    dve.wait_ge(s_out, 16 * c)
                for i in range(COMB):
                    x = dve.scalar_tensor_tensor(ot[:, i, :], g12[:, i, 1, :], gates[:, 1, bass.ds(c * COMB + i, 1)],
                                                 ob[:, i, :], ALU.mult, ALU.add)
                x.then_inc(s_ot, 1)

            def pair(m, combine):
                step(2 * m + 2, 0)
                if combine:
                    combine_first(m - COMB_PAIR)
                step(2 * m + 3, 1)
                if combine:
                    combine_second(m - COMB_PAIR)

            def loop():
                with dve.Fori(1, COMB_PAIR) as m:
                    pair(m, False)
                pair(COMB_PAIR, True)
                with dve.Fori(COMB_PAIR + 1, PAIRS) as m:
                    pair(m, True)

            x_low(0, 0)
            stage2(step, loop)
            with dve.Fori(ROUNDS_A, ROUNDS) as c:
                combine_first(c)
                combine_second(c)


_INS = ["x", "adj", "L0_gnn_W", "L0_gnn_a", "L0_ffn_Wr", "L0_ffn_W1s", "L0_ffn_b1s", "L0_ffn_W2s", "L0_ffn_b2s",
        "L0_ffn_W1p", "L0_ffn_b1p", "L0_ffn_W2p", "L0_ffn_b2p"]


def kernel(**inputs):
    import numpy as _np
    import concourse.bacc as _bacc
    from concourse import mybir as _mybir
    from concourse.bass_utils import run_bass_kernel_spmd as _run

    nc = _bacc.Bacc("TRN2", target_bir_lowering=False, num_devices=1)
    arrays, args = {}, []
    for name in _INS:
        a = _np.ascontiguousarray(inputs[name])
        arrays[f"in_{name}_dram"] = a
        args.append(nc.dram_tensor(f"in_{name}_dram", a.shape, _mybir.dt.from_np(a.dtype), kind="ExternalInput").ap())
    args.append(nc.dram_tensor("out_0_dram", inputs["x"].shape, _mybir.dt.float32, kind="ExternalOutput").ap())
    gnn_moe_layer(nc, *args)
    r = _run(nc, [arrays], core_ids=[0])
    return r.results[0]["out_0_dram"]
```

```python
from contextlib import ExitStack

import concourse.bass as bass
from concourse import mybir

F32 = mybir.dt.float32
F32R = mybir.dt.float32r
BF16 = mybir.dt.bfloat16
I32 = mybir.dt.int32
U32 = mybir.dt.uint32
ALU = mybir.AluOpType
ACT = mybir.ActivationFunctionType
AX = mybir.AxisListType.X
RMAX = bass.bass_isa.ReduceOp.max

P = 128
SLOPE = 0.2
EPS = 1e-5
TINY = 1e-30
HUGE = 3.0e38


def gnn_moe_layer(nc, x, adj, gnn_W, gnn_a, Wr, W1s, b1s, W2s, b2s, W1p, b1p, W2p, b2p, out):
    NB, N, D = x.shape
    F = W1s.shape[1]
    E = Wr.shape[1]
    NT = N // P
    NC = F // P
    H = 512
    NH = N // H
    T = 512
    TB = T // P
    TSH = T.bit_length() - 1
    GROUPS = [NB - 2, 2]
    assert D == P and NT == 8 and NC == 4 and N == 2 * T and sum(GROUPS) == NB

    GT = [(2 * g * N - E) // T + E for g in GROUPS]
    REG = [g * N + T for g in GROUPS]
    GBASE = [0, E * REG[0] + T]
    ROWS = GBASE[1] + E * REG[1] + T
    ST = NB * N // T
    PART0 = [0, GT[0], sum(GT)]
    NTILES = sum(GT) + ST
    COMB = T // P
    ROUNDS = NB * NT // COMB
    ROUNDS_A = GROUPS[0] * NT // COMB
    PAIRS = NTILES // 2 - 2
    B_PAIR = (GT[0] - 4) // 2
    COMB_PAIR = (GT[0] + 2) // 2
    SHARED_PAIR = PART0[2] // 2
    SHARED_LAST = PAIRS - COMB_PAIR
    assert NTILES % 2 == 0 and PART0[2] % 2 == 0
    assert all(c + COMB_PAIR < (PART0[2] + c) // 2 for c in range(SHARED_LAST))
    assert COMB_PAIR + ROUNDS_A > SHARED_PAIR and SHARED_LAST == ROUNDS - 3
    STORED = [sum(k % 2 == r for k in range(PART0[2] + SHARED_LAST)) for r in range(2)]
    LOADED = PART0[2] + 2
    COLS_CUTS = [PART0[2] // 2 - 2, PART0[2] // 2 - 1]
    EARLY = ROUNDS - 2
    GM = max(GT)

    ctx = ExitStack()
    with ctx:
        def sb(name, shape, dt):
            return ctx.enter_context(nc.sbuf_tensor(name, shape, dt))

        def sem(name):
            return ctx.enter_context(nc.semaphore(name))

        def sems(name, n=2):
            return [sem(f"{name}{i}") for i in range(n)]

        bank = [ctx.enter_context(nc.psum_tensor(f"bank{i}", [P, H], F32)) for i in range(8)]

        wsplit = nc.dram_tensor("wsplit", [E + 1, P, 2, 2 * F], F32, kind="Internal").ap()
        xrows = nc.dram_tensor("xrows", [ROWS, D], F32, kind="Internal").ap()
        xcols = nc.dram_tensor("xcols", [NB, D, N], F32, kind="Internal").ap()
        yrows = [nc.dram_tensor(f"yrows{i}", [n * T, D], F32, kind="Internal").ap()
                 for i, n in enumerate(GT)]

        ident = sb("ident", [P, P], F32)
        identb = sb("identb", [P, P], BF16)
        before = sb("before", [P, P], BF16)
        onesb = sb("onesb", [P, P], BF16)
        onesf = sb("onesf", [P, P], F32)
        coefM = sb("coefM", [P, 3], F32)
        minus_half = sb("minus_half", [P, NB * NT], F32)
        iota_i = sb("iota_i", [P, NT, E], I32)
        iota_e = sb("iota_e", [P, NT, E], F32)
        base_i = sb("base_i", [P, 2, E], I32)
        base = sb("base", [P, 2, E], F32)
        iota_ti = sb("iota_ti", [P, GM, E], I32)
        iota_t = sb("iota_t", [P, GM, E], F32)
        zero_e = sb("zero_e", [P, E], F32)
        zrow = sb("zrow", [P, TB, D], F32)
        Wg = sb("Wg", [P, D], F32)
        acol = sb("acol", [P, 2], F32)
        WTa = sb("WTa", [P, D + 1], F32)
        wi = sb("wi", [P, 1], F32)
        wirep = sb("wirep", [P, P], F32)
        Wr_sb = sb("Wr_sb", [P, E], F32)
        NBR = (E + 1) * (NC + 1)
        brow = sb("brow", [NBR, P], F32)
        b1t = sb("b1t", [P, E + 1, NC], F32)
        b2t = sb("b2t", [P, E + 1], F32)
        wraw = sb("wraw", [P, 2, 2, F], F32)
        wst = sb("wst", [P, 2, 2, 2 * F], F32R)

        res = sb("res", [P, NB * NT, D], F32)
        adjm = sb("adjm", [P, 2, NT, N], BF16)
        stat1 = sb("stat1", [P, NB * NT, 6], F32)
        ln1 = sb("ln1", [P, 8, NB * NT], F32)
        stat2 = sb("stat2", [P, NT, 6], F32)
        ln2 = sb("ln2", [P, 8, NT], F32)
        xn = sb("xn", [P, NT, D], F32)
        xnT = sb("xnT", [P, N], F32)
        WhA = sb("WhA", [P, 2, NT, D + 1], F32)
        ejc = sb("ejc", [P, 2, NT], F32)
        mx = sb("mx", [P, 1], F32)
        Mb = sb("Mb", [P, 1], F32)
        cM = sb("cM", [P, 3], F32)
        Bc = sb("Bc", [P, 2, NT], F32)
        Dc = sb("Dc", [P, 2, NT], F32)
        nBc = sb("nBc", [P, 2, NT], F32)
        crow = sb("crow", [P, 2, N], F32)
        R = sb("R", [P, 2, N], F32)
        PT = sb("PT", [P, 2, N], F32)
        dens = sb("dens", [P, 3, 3], F32)
        rden = sb("rden", [P, 3, 3], F32)
        xn2 = sb("xn2", [P, 2, NT, D], F32)
        x2T = sb("x2T", [P, N], F32)
        Ls = sb("Ls", [P, 2, NT, E], F32)
        m12 = sb("m12", [P, 2, NT], F32)
        eq = sb("eq", [P, NT, E], F32)
        cand = sb("cand", [P, NT, E], F32)
        first = sb("first", [P, NT], F32)
        oh = sb("oh", [P, 2, NT, E], F32)
        mm = sb("mm", [P, NT, E], BF16)
        dm = sb("dm", [P, NB * NT], F32)
        ed = sb("ed", [P, NB * NT], F32)
        ed1 = sb("ed1", [P, NB * NT], F32)
        gates = sb("gates", [P, 2, NB * NT], F32)
        pos = sb("pos", [P, NT, E], F32)
        hit = sb("hit", [P, 2, NT, E], F32)
        slotf = sb("slotf", [P, 2, NT], F32)
        choice = sb("choice", [P, 2, NB * NT], F32)
        slotall = sb("slotall", [P, 2, NB * NT], F32)
        slotmv = sb("slotmv", [P, 2, 2, NB * NT], F32)
        slots = sb("slots", [P, 2, NB * NT], U32)
        sslot = sb("sslot", [P, 2, 2, NT], U32)
        gslot = sb("gslot", [P, 2, COMB], U32)
        gslot_early = sb("gslot_early", [P, 2, COMB], U32)
        carry = sb("carry", [P, E], F32)

        nti = sb("nti", [P, 2, E], I32)
        cnt = sb("cnt", [P, 2, 5, E], F32)
        tge = sb("tge", [P, 2, GM, E], F32)
        tv = sb("tv", [P, 5, GM], F32)
        tab_x = sb("tab_x", [P, NTILES], I32)
        tab_e = sb("tab_e", [P, NTILES], I32)
        tab_tail = sb("tab_tail", [P, 2, E], I32)

        w1, w2 = wst[:, :, 0, :], wst[:, :, 1, :]
        b1 = sb("b1", [P, 2, NC], F32)
        b2 = sb("b2", [P, 2, 1], F32)
        xh = sb("xh", [P, 2, T], F32R)
        xl = sb("xl", [P, 2, T], F32R)
        spare = adjm[:, :, :, :].rearrange("p q t n -> p (q t n)").bitcast(F32)
        taken = [0]

        def over_masks(*dims):
            size = 1
            for d in dims:
                size *= d
            v = spare[:, taken[0]:taken[0] + size]
            taken[0] += size
            if len(dims) == 2:
                v = v.rearrange("p (a b) -> p a b", a=dims[0])
            if len(dims) == 3:
                v = v.rearrange("p (a b c) -> p a b c", a=dims[0], b=dims[1])
            return v

        xs = over_masks(2, TB, D)
        hf = over_masks(NC, T)
        yTs = over_masks(T)
        ys = over_masks(2, TB, D)
        g12 = over_masks(COMB, 2, D)
        g12_early = over_masks(COMB, 2, D)
        ot = over_masks((ROUNDS - SHARED_LAST) * COMB, D)
        hh = sb("hh", [P, 2, NC, T], F32R)
        hl = sb("hl", [P, 2, NC, T], F32R)

        mT = [bank[i][:, :].bitcast(BF16) for i in (0, 1)]
        at = [bank[2 + i][:, 0:3 * (D + 1)].rearrange("p (t c) -> p t c", t=3) for i in range(3)]
        tp = [bank[5], bank[6]]
        ws = bank[7]
        whp = [tp[g % 2][:, 0:3 * (D + 1)].rearrange("p (t c) -> p t c", t=3) for g in range(3)]
        lgp = ws[:, 400:400 + NT * E].rearrange("p (t e) -> p t e", e=E)
        cntp = ws[:, 480:480 + E]
        hps = bank[0:4]
        yTp, xTp, yRp = (bank[4], bank[7]), bank[5], bank[6]

        s_zero, s_iota, s_const = sem("s_zero"), sem("s_iota"), sem("s_const")
        s_par, s_wt, s_wcopy, s_wirep = sem("s_par"), sem("s_wt"), sem("s_wcopy"), sem("s_wirep")
        s_brow, s_bT, s_btab = sem("s_brow"), sem("s_bT"), sem("s_btab")
        s_wraw, s_whi, s_wlo, s_wst = sems("s_wraw"), sem("s_whi"), sem("s_wlo"), sems("s_wst")
        s_x, s_adj, s_msk = sems("s_x"), [sems("s_adj_even"), sems("s_adj_odd")], sem("s_msk")
        s_stat, s_lnsum, s_lnsq, s_var = sems("s_stat"), sems("s_lnsum"), sems("s_lnsq"), sems("s_var")
        s_vareps, s_pow, s_rstd = sems("s_vareps"), sems("s_pow"), sems("s_rstd")
        s_xn, s_xnt, s_xnT, s_Whp, s_Whc, s_ei = (sem(n) for n in ("s_xn", "s_xnt", "s_xnT", "s_Whp", "s_Whc", "s_ei"))
        s_mx, s_M, s_cM, s_B, s_nB, s_E1, s_crow = (sem(n) for n in ("s_mx", "s_M", "s_cM", "s_B", "s_nB", "s_E1", "s_crow"))
        s_mT, s_R, s_PT, s_at = sem("s_mT"), sem("s_R"), sem("s_PT"), sem("s_at")
        s_bank, s_den, s_rden, s_res = sem("s_bank"), sem("s_den"), sem("s_rden"), sem("s_res")
        s_xn2t, s_x2T, s_lg, s_route, s_mm = (sem(n) for n in ("s_xn2t", "s_x2T", "s_lg", "s_route", "s_mm"))
        s_xn2 = sems("s_xn2_half")
        s_yslot = sem("s_yslot")
        s_oh, s_hit, s_gslot = sem("s_oh"), sem("s_hit"), sems("s_gslot")
        s_dm, s_ed, s_gate, s_rank, s_pos, s_slot = (sem(n) for n in ("s_dm", "s_ed", "s_gate", "s_rank", "s_pos", "s_slot"))
        s_carry, s_scat, s_shx = sem("s_carry"), sems("s_scat"), sems("s_shx")
        s_tstep, s_rstep, s_tab, s_tabS, s_tail = sem("s_tstep"), sem("s_rstep"), sem("s_tab"), sem("s_tabS"), sems("s_tail")
        s_xin, s_w1, s_w2 = sems("s_xin"), sems("s_w1"), sems("s_w2")
        s_xT, s_xh, s_xl, s_hp, s_hf, s_hh, s_hh1, s_hl = (sem(n) for n in ("s_xT", "s_xh", "s_xl", "s_hp", "s_hf", "s_hh", "s_hh1", "s_hl"))
        s_yT, s_yTs, s_yR, s_ys, s_yst = sem("s_yT"), sem("s_yTs"), sem("s_yR"), sem("s_ys"), sems("s_yst")
        s_g, s_g_early, s_gslot_early, s_ob, s_ot, s_rsum, s_out = sems("s_g"), sems("s_g_early"), sem("s_gslot_early"), sem("s_ob"), sem("s_ot"), sem("s_rsum"), sem("s_out")

        s_alone = sem("s_alone")
        block = ctx.enter_context(nc.Block())

        def stage1(eng, ahead, attend):
            def at(b):
                return b, b % 2, b // 2
            ahead(at(0))
            attend(at(0), None, at(1), None)
            attend(at(1), at(0), at(2), None)
            attend(at(2), at(1), at(3), at(0))
            with eng.Fori(1, NB // 2 - 1) as p:
                attend((2 * p + 1, 1, p), (2 * p, 0, p), (2 * p + 2, 0, p + 1), (2 * p - 1, 1, p - 1))
                attend((2 * p + 2, 0, p + 1), (2 * p + 1, 1, p), (2 * p + 3, 1, p + 1), (2 * p, 0, p))
            attend(at(NB - 1), at(NB - 2), None, at(NB - 3))

        LN1 = [(0, 1), (1, 2), (2, 5), (5, NB)]

        def following(cur, nxt, jt):
            return (cur, jt) if jt < NT else (nxt, jt - NT)

        def stage2(step, loop, beside=None):
            for k in range(4):
                step(k, k % 2)
            loop()
            for k in range(NTILES - 2, NTILES + 2):
                step(k, k % 2)
                if beside:
                    beside(k)

        def pairs(eng, body, cuts):
            edges = sorted({1, PAIRS} | set(cuts))
            for lo, hi in zip(edges, edges[1:]):
                if hi - lo == 1:
                    body(lo, lo)
                else:
                    with eng.Fori(lo, hi) as m:
                        body(m, lo)

        def part_of(k):
            return sum(k >= p for p in PART0[1:3])

        def tails(eng, g):
            eng.wait_ge(s_tab, g + 1)
            for e in range(E):
                r = eng.value_load(tab_tail[0:1, g, e:e + 1], min_val=0, max_val=ROWS - T)
                eng.dma_start(xrows[bass.ds(r, T), :].rearrange("(k p) d -> p k d", p=P), zrow[:, :, :]).then_inc(s_tail[g], 16)

        def alone(eng):
            eng.sem_inc(s_alone, 1)

        def isint(v):
            return isinstance(v, int)

        @block.sync
        def _(sp):
            def load_x(b, q, half):
                if not (isint(half) and half == 0):
                    sp.wait_ge(s_x[q], 16 * half)
                    alone(sp)
                sp.dma_start(res[:, bass.ds(b * NT, NT), :], x[b].rearrange("(t p) d -> p t d", p=P)).then_inc(s_x[q], 16)

            load_x(0, 0, 0)
            sp.dma_start(Wg[:, :], gnn_W).then_inc(s_par, 16)
            with nc.allow_non_contiguous_dma(reason="256 values once"):
                sp.dma_start(acol[:, :], gnn_a.rearrange("(k o) -> o k", k=2)).then_inc(s_par, 16)
            sp.dma_start(Wr_sb[:, :], Wr).then_inc(s_par, 16)
            load_x(1, 1, 0)
            n1 = (E + 1) * NC
            sp.dma_start(brow[0:E * NC, :], b1p.rearrange("e (c p) -> (e c) p", p=P)).then_inc(s_brow, 16)
            sp.dma_start(brow[E * NC:n1, :], b1s.rearrange("(c p) -> c p", p=P)).then_inc(s_brow, 16)
            sp.dma_start(brow[n1:n1 + E, :], b2p).then_inc(s_brow, 16)
            sp.dma_start(brow[n1 + E:NBR, :], b2s.rearrange("(a p) -> a p", a=1)).then_inc(s_brow, 16)
            with sp.Fori(1, NB // 2) as h:
                load_x(2 * h, 0, h)
                load_x(2 * h + 1, 1, h)

            def store_x2(b, q, half):
                sp.wait_ge(s_x2T, 2 * b + 2)
                alone(sp)
                if not (isint(half) and half == 0):
                    sp.wait_ge(s_shx[q], 16 * half)
                    alone(sp)
                sp.dma_start(xcols[b], x2T[:, :]).then_inc(s_shx[q], 16)

            def raw_weights(e):
                if e >= 2:
                    sp.wait_ge(s_wlo, e - 1)
                src1, src2 = (W1p[e], W2p[e]) if e < E else (W1s, W2s)
                sp.dma_start(wraw[:, e % 2, 0, :], src1).then_inc(s_wraw[e % 2], 16)
                sp.dma_start(wraw[:, e % 2, 1, :].rearrange("p (c d) -> p c d", c=NC),
                             src2.rearrange("(c p) d -> p c d", p=P)).then_inc(s_wraw[e % 2], 16)

            raw_weights(0)
            for e in range(E + 1):
                if e < E:
                    raw_weights(e + 1)
                if e == 5:
                    store_x2(0, 0, 0)
                sp.wait_ge(s_wlo, e + 1)
                sp.dma_start(wsplit[e], wst[:, e % 2, :, :].bitcast(F32)).then_inc(s_wst[e % 2], 16)

            sp.wait_ge(s_zero, 1)
            for g in range(2):
                r = GBASE[g] + E * REG[g]
                sp.dma_start(xrows[r:r + T, :].rearrange("(k p) d -> p k d", p=P), zrow[:, :, :]).then_inc(s_tail[0], 16)

            store_x2(1, 1, 0)
            with sp.Fori(1, NB // 2 - 1) as h:
                store_x2(2 * h, 0, h)
                store_x2(2 * h + 1, 1, h)

            def filled(g):
                for q in range(2):
                    sp.wait_ge(s_scat[q], 16 * 2 * NT * sum(GROUPS[:g + 1]) // 2)
                for i in range(g + 1):
                    sp.wait_ge(s_tail[i], 16 * (E + 2 * (1 - i)))

            def load_cols(k, r, b):
                sp.wait_ge(*((s_xT, k - 1) if isint(k) and k < PART0[2] + 2 else (s_xl, k - 1)))
                alone(sp)
                sp.dma_start(xs[:, r, :, :].rearrange("p k d -> p (k d)"), xcols[b, :, r * T:(r + 1) * T]).then_inc(s_xin[r], 16)

            def load_rows(k, r):
                if not (isint(k) and k < 2):
                    sp.wait_ge(s_xT, k - 1)
                    alone(sp)
                row = sp.value_load(tab_x[0:1, bass.ds(k, 1)], min_val=0, max_val=ROWS - T)
                sp.dma_start(xs[:, r, :, :], xrows[bass.ds(row, T), :].rearrange("(k p) d -> p k d", p=P)).then_inc(s_xin[r], 16)

            def load_w1(k, r):
                e = sp.value_load(tab_e[0:1, bass.ds(k, 1)], min_val=0, max_val=E)
                if not (isint(k) and k < 2):
                    sp.wait_ge(s_hp, NC * (k - 1))
                    alone(sp)
                sp.dma_start(w1[:, r, :].bitcast(F32), wsplit[e, :, 0, :]).then_inc(s_w1[r], 16)
                if not (isint(k) and k < 2):
                    sp.wait_ge(s_hf, NC * (k - 1))
                    alone(sp)
                sp.dma_start(b1[:, r, :], b1t[:, e, :]).then_inc(s_w1[r], 16)
                return e

            def load_w2(k, r, e=None):
                e = e if e is not None else sp.value_load(tab_e[0:1, bass.ds(k, 1)], min_val=0, max_val=E)
                if not (isint(k) and k < 2):
                    sp.wait_ge(s_yT, k - 1)
                    alone(sp)
                sp.dma_start(w2[:, r, :].bitcast(F32), wsplit[e, :, 1, :]).then_inc(s_w2[r], 16)
                if not (isint(k) and k < 2):
                    sp.wait_ge(s_yTs, k - 1)
                    alone(sp)
                sp.dma_start(b2[:, r, :], b2t[:, bass.ds(e, 1)]).then_inc(s_w2[r], 16)

            def store_rows(k, r, part):
                sp.wait_ge(s_ys, k + 1)
                alone(sp)
                rows = out.rearrange("b n d -> (b n) d") if part == 2 else yrows[part]
                sp.dma_start(rows[bass.ds((k - PART0[part]) * T, T), :].rearrange("(k p) d -> p k d", p=P),
                             ys[:, r, :, :]).then_inc(s_yst[r], 16)

            def step(k, r):
                if k + 1 < LOADED:
                    load_w1(k + 1, 1 - r)
                if k < LOADED:
                    load_w2(k, r)
                if k + 2 < PART0[2]:
                    load_rows(k + 2, r)
                elif k + 2 < NTILES:
                    load_cols(k + 2, r, (k + 2 - PART0[2]) // 2)
                if 3 <= k < PART0[2] + SHARED_LAST + 3:
                    store_rows(k - 3, 1 - r, part_of(k - 3))

            tails(sp, 0)
            store_x2(NB - 2, 0, NB // 2 - 1)
            filled(0)
            sp.wait_ge(s_mT, NB * NT)
            sp.wait_ge(s_wst[0], 16 * (E // 2 + 1))
            sp.wait_ge(s_wst[1], 16 * (E // 2))
            sp.wait_ge(s_btab, 1)
            sp.wait_ge(s_tabS, 1)
            load_rows(0, 0)
            load_rows(1, 1)
            load_w1(0, 0)
            step(0, 0)
            step(1, 1)
            store_x2(NB - 1, 1, NB // 2 - 1)

            def pair(m, first):
                def load(k, r, m):
                    if 2 * first + 4 < PART0[2]:
                        load_rows(k, r)
                    else:
                        load_cols(k, r, m + 2 - PART0[2] // 2)
                if first == B_PAIR:
                    filled(1)
                    for q in range(2):
                        sp.wait_ge(s_shx[q], 16 * (NB // 2))
                if 2 * first + 3 < LOADED:
                    e = load_w1(2 * m + 3, 1)
                    load_w2(2 * m + 2, 0)
                load(2 * m + 4, 0, m)
                store_rows(2 * m - 1, 1, part_of(2 * first - 1))
                if 2 * first + 4 < LOADED:
                    load_w1(2 * m + 4, 0)
                if 2 * first + 3 < LOADED:
                    load_w2(2 * m + 3, 1, e)
                load(2 * m + 5, 1, m)
                store_rows(2 * m, 0, part_of(2 * first))

            step(2, 0)
            step(3, 1)
            pairs(sp, pair, COLS_CUTS + [B_PAIR, B_PAIR + 1, LOADED // 2 - 2, LOADED // 2 - 1] + [c for p in PART0[1:3] for c in ((p + 1) // 2, p // 2 + 1)])
            for k in range(NTILES - 2, NTILES):
                step(k, k % 2)
            for i, c in enumerate(range(SHARED_LAST, ROUNDS)):
                sp.wait_ge(s_ot, c + 1)
                sp.dma_start(out.rearrange("b n d -> (b n) d")[c * T:(c + 1) * T, :].rearrange("(k p) d -> p k d", p=P),
                             ot[:, i * COMB:(i + 1) * COMB, :]).then_inc(s_out, 16)
            sp.wait_ge(s_out, 16 * (ROUNDS - SHARED_LAST))
            for r in range(2):
                sp.wait_ge(s_yst[r], 16 * STORED[r])

        @block.gpsimd
        def _(pool):
            pool.memset(ident[:, :], 0.0)
            pool.memset(identb[:, :], 0.0)
            pool.memset(before[:, :], 0.0)
            pool.memset(onesb[:, :], 1.0)
            pool.memset(onesf[:, :], 1.0)
            pool.memset(zero_e[:, :], 0.0)
            pool.memset(minus_half[:, :], -0.5)
            pool.memset(coefM[:, 0:1], -1.0)
            pool.memset(coefM[:, 1:2], -SLOPE)
            pool.memset(coefM[:, 2:3], 1.0 - SLOPE)
            pool.memset(WhA[:, :, :, D:D + 1], 1.0)
            pool.memset(zrow[:, :, :], 0.0).then_inc(s_zero, 1)
            pool.iota(iota_i[:, :, :], [[0, NT], [1, E]], base=0, channel_multiplier=0)
            for g in range(2):
                pool.iota(base_i[:, g, :], [[REG[g], E]], base=GBASE[g], channel_multiplier=0)
            pool.iota(iota_ti[:, :, :], [[1, GM], [0, E]], base=0, channel_multiplier=0).then_inc(s_iota, 1)
            pool.wait_ge(s_zero, 1)
            pool.wait_ge(s_iota, 1)
            pool.affine_select(out=ident[:, :], in_=ident[:, :], compare_op=ALU.not_equal, fill=1.0,
                               base=0, pattern=[[-1, P]], channel_multiplier=1)
            pool.affine_select(out=identb[:, :], in_=identb[:, :], compare_op=ALU.not_equal, fill=1.0,
                               base=0, pattern=[[-1, P]], channel_multiplier=1)
            pool.affine_select(out=before[:, :], in_=before[:, :], compare_op=ALU.is_ge, fill=1.0,
                               base=0, pattern=[[-1, P]], channel_multiplier=1)
            pool.tensor_copy(iota_e[:, :, :], iota_i[:, :, :])
            pool.tensor_copy(base[:, :, :], base_i[:, :, :])
            pool.tensor_copy(iota_t[:, :, :], iota_ti[:, :, :]).then_inc(s_const, 1)
            s0, s1 = PART0[2], NTILES
            pool.iota(tab_e[:, s0:s1], [[0, ST]], base=E, channel_multiplier=0).then_inc(s_tabS, 1)

            def load_adj(b, q, half):
                if not (isint(b) and b < 2):
                    pool.wait_ge(s_mT, NT * (b - 1))
                for k in range(2):
                    if not (isint(b) and b < 2):
                        pool.wait_ge(s_adj[q][k], 16 * half)
                    pool.dma_start(adjm[:, q, k * NT // 2:(k + 1) * NT // 2, :],
                                   adj[b].rearrange("(t p) n -> p t n", p=P)[:, k * NT // 2:(k + 1) * NT // 2, :]
                                   ).then_inc(s_adj[q][k], 16)

            def rstd(k, n, L):
                pool.wait_ge(s_var[k], n + 1)
                alone(pool)
                pool.tensor_scalar(L(6), L(4), 1.0 / D, EPS, ALU.mult, ALU.add).then_inc(s_vareps[k], 1)
                pool.wait_ge(s_vareps[k], n + 1)
                half = minus_half[:, 0:L(6).shape[1]]
                pool.tensor_tensor(L(7), L(6), half, ALU.pow).then_inc(s_pow[k], 1)
                pool.wait_ge(s_pow[k], n + 1)
                pool.tensor_tensor(L(3), L(5), L(7), ALU.mult).then_inc(s_rstd[k], 1)

            def rstd1(group):
                lo, hi = (b * NT for b in LN1[group])
                rstd(0, group, lambda i: ln1[:, i, lo:hi])

            def batch_max(b):
                pool.wait_ge(s_mx, b + 1)
                if not (isint(b) and b == 0):
                    pool.wait_ge(s_cM, b)
                alone(pool)
                pool.partition_all_reduce(Mb[:, :], mx[:, :], P, RMAX).then_inc(s_M, 1)

            def scatter(b, q, lo, hi):
                if lo == 0:
                    pool.wait_ge(s_slot, b + 1)
                    for h in range(2):
                        pool.wait_ge(s_xn2[h], b + 1)
                    alone(pool)
                for i in range(lo, hi):
                    c, t = i // NT, i % NT
                    pool.indirect_dma_start(xrows, bass.IndirectOffsetOnAxis(ap=sslot[:, q, c, t:t + 1], axis=0),
                                            xn2[:, q, t, :], None).then_inc(s_scat[q], 16)

            def split_weights(e):
                pool.wait_ge(s_whi, e + 1)
                pool.tensor_tensor(wst[:, e % 2, :, F:2 * F], wraw[:, e % 2, :, :], wst[:, e % 2, :, 0:F].bitcast(F32),
                                   ALU.subtract).then_inc(s_wlo, 1)

            def ahead(nxt):
                rstd1(0)
                batch_max(nxt[0])

            def attend(cur, fin, nxt, old):
                if nxt:
                    load_adj(*nxt)
                first, second = not fin, bool(fin and not old)
                third = bool(nxt and isint(nxt[0]) and nxt[0] == 3)
                if first:
                    rstd1(1)
                    split_weights(0)
                if fin:
                    rstd(1, fin[0], lambda i: ln2[:, i, :])
                if third:
                    split_weights(E - 1)
                if old:
                    scatter(old[0], old[1], 0, 6)
                if nxt:
                    batch_max(nxt[0])
                if first:
                    rstd1(2)
                    for e in range(1, 4):
                        split_weights(e)
                if second:
                    split_weights(4)
                    rstd1(3)
                    for e in range(5, E - 1):
                        split_weights(e)
                if third:
                    split_weights(E)
                if old:
                    scatter(old[0], old[1], 6, 2 * NT)

            steps = [0]

            def result_rows(g):
                def link(i):
                    i.then_inc(s_rstep, 1)
                    steps[0] += 1
                    pool.wait_ge(s_rstep, steps[0])
                pool.wait_ge(s_tab, g + 1)
                u0, u1 = (sum(GROUPS[:i]) * NT for i in (g, g + 1))
                link(pool.tensor_tensor(cnt[:, g, 3, :], cnt[:, g, 2, :], cnt[:, g, 1, :], ALU.subtract))
                link(pool.tensor_scalar(cnt[:, g, 0, :], cnt[:, g, 3, :], float(T), None, ALU.mult))
                link(pool.tensor_tensor(cnt[:, g, 4, :], cnt[:, g, 0, :], base[:, g, :], ALU.subtract))
                link(pool.tensor_copy(slotmv[:, 0, :, u0:u1], slotall[:, :, u0:u1]))
                for e in range(E):
                    link(pool.tensor_scalar(slotmv[:, 1, :, u0:u1], choice[:, :, u0:u1], float(e - E), cnt[:, g, 4, e:e + 1], ALU.is_equal, ALU.mult))
                    link(pool.tensor_tensor(slotmv[:, 0, :, u0:u1], slotmv[:, 0, :, u0:u1], slotmv[:, 1, :, u0:u1], ALU.add))
                pool.tensor_copy(slots[:, :, u0:u1], slotmv[:, 0, :, u0:u1]).then_inc(s_yslot, 1)

            load_adj(0, 0, 0)
            stage1(pool, ahead, attend)
            attend(None, (NB - 1, (NB - 1) % 2, NB // 2 - 1), None, (NB - 2, NB % 2, NB // 2 - 1))
            scatter(NB - 1, (NB - 1) % 2, 0, 2 * NT)
            result_rows(0)
            tails(pool, 1)
            result_rows(1)


            def gather(c, part):
                n = c - 1 if isint(c) and c > EARLY else c
                for ch in range(2):
                    if not (isint(c) and c == 0):
                        pool.wait_ge((s_ob, s_ot)[ch], n)
                        pool.wait_ge(s_g[ch], 16 * COMB * n)
                    pool.tensor_copy(gslot[:, ch, :], slots[:, ch, bass.ds(c * COMB, COMB)]).then_inc(s_gslot[ch], 1)
                    pool.wait_ge(s_gslot[ch], n + 1)
                    alone(pool)
                    for i in range(COMB):
                        pool.indirect_dma_start(g12[:, i, ch, :], None, yrows[part],
                                                bass.IndirectOffsetOnAxis(ap=gslot[:, ch, i:i + 1], axis=0)).then_inc(s_g[ch], 16)

            def gather_early(ch):
                pool.tensor_copy(gslot_early[:, ch, :], slots[:, ch, EARLY * COMB:(EARLY + 1) * COMB]).then_inc(s_gslot_early, 1)
                pool.wait_ge(s_gslot_early, ch + 1)
                for i in range(COMB):
                    pool.indirect_dma_start(g12_early[:, i, ch, :], None, yrows[1],
                                            bass.IndirectOffsetOnAxis(ap=gslot_early[:, ch, i:i + 1], axis=0)).then_inc(s_g_early[ch], 16)

            pool.wait_ge(s_yslot, 2)
            for r in range(2):
                pool.wait_ge(s_yst[r], 16 * ((GT[0] + 1 - r) // 2))
            gather(0, 0)
            with pool.Fori(1, ROUNDS_A) as c:
                gather(c, 0)
            for r in range(2):
                pool.wait_ge(s_yst[r], 16 * (PART0[2] // 2))
            for c in range(ROUNDS_A, ROUNDS):
                if c != EARLY:
                    gather(c, 1)
                if c < ROUNDS_A + 2:
                    gather_early(c - ROUNDS_A)

        @block.tensor
        def _(pe):
            pe.wait_ge(s_const, 1)
            pe.wait_ge(s_par, 48)
            pe.transpose(tp[0][:, 0:P], Wg[:, :], ident[:, :])
            pe.matmul(ws[:, 0:2], Wg[:, :], acol[:, :], start=True, stop=True).then_inc(s_wt, 1)
            pe.wait_ge(s_brow, 64)
            pe.transpose(tp[1][:, 0:NBR], brow[:, :], ident[0:NBR, 0:NBR]).then_inc(s_bT, 1)
            pe.wait_ge(s_wirep, 1)
            pe.wait_ge(s_btab, 1)

            def xn_T(b):
                if not (isint(b) and b == 0):
                    pe.wait_ge(s_E1, 2 * b)
                for t in range(NT):
                    if t % 4 == 0:
                        pe.wait_ge(s_xn, 2 * b + t // 4 + 1)
                    i = pe.transpose(tp[t // 4][:, (t % 4) * P:(t % 4 + 1) * P], xn[:, t, :], ident[:, :])
                    if t % 4 == 3:
                        i.then_inc(s_xnt, 1)

            def project(b):
                for g in range(3):
                    pe.wait_ge(s_xnT, 2 * b + min(g, 1) + 1)
                    if g == 2:
                        pe.wait_ge(s_Whc, 3 * b + 1)
                    for t in range(3 * g, min(3 * g + 3, NT)):
                        i = pe.matmul(whp[g][:, t % 3, :], xnT[:, t * P:(t + 1) * P], WTa[:, :], start=True, stop=True)
                    i.then_inc(s_Whp, 1)

            def ei_rows(b):
                pe.wait_ge(s_Whc, 3 * b + 3)
                if not (isint(b) and b < 2):
                    pe.wait_ge(s_x2T, 2 * (b - 1))
                for h in range(NH):
                    pe.matmul(tp[h][:, :], wirep[:, :], xnT[:, h * H:(h + 1) * H], start=True, stop=True).then_inc(s_ei, 1)

            def mask_T(batch, jt):
                b, q, half = batch
                n = NT * b + jt
                if jt == 0:
                    pe.wait_ge(s_msk, 2 * b + 2)
                if not (isint(n) and n < 2):
                    pe.wait_ge(s_PT, n - 1)
                for t in range(NT):
                    i = pe.transpose(mT[jt % 2][:, t * P:(t + 1) * P], adjm[:, q, t, jt * P:(jt + 1) * P], identb[:, :])
                i.then_inc(s_mT, 1)

            def weigh(b, q, jt):
                pe.wait_ge(s_PT, NT * b + jt + 1)
                if jt == 0:
                    pe.wait_ge(s_Whc, 3 * b + 3)
                for t in range(NT):
                    if jt == 0 and t % 3 == 0 and not (isint(b) and b == 0):
                        pe.wait_ge(s_res, 3 * b - 2 + t // 3)
                    i = pe.matmul(at[t // 3][:, t % 3, :], PT[:, jt % 2, t * P:(t + 1) * P], WhA[:, q, jt, :],
                                  start=(jt == 0 and t % 3 == 0), stop=(jt == NT - 1), skip_group_check=True)
                    if jt == NT - 1 and t in (2, 5):
                        i.then_inc(s_bank, 1)
                i.then_inc(s_at, 1)

            def x2_T(b, q):
                if isint(b) and b == NB - 1:
                    pe.wait_ge(s_x2T, 2 * b)
                elif isint(b) and b == NB - 2:
                    pe.wait_ge(s_E1, 2 * NB)
                else:
                    pe.wait_ge(s_Whc, 3 * (b + 3))
                last = isint(b) and b == NB - 1
                for t in range(NT):
                    if t % 4 == 0:
                        pe.wait_ge(s_xn2[t // 4], b + 1)
                    if last and t == 4:
                        pe.wait_ge(s_x2T, 2 * b + 1)
                    i = pe.transpose(tp[1 if last else t // 4][:, (t % 4) * P:(t % 4 + 1) * P], xn2[:, q, t, :], ident[:, :])
                    if t % 4 == 3:
                        i.then_inc(s_xn2t, 1)

            def logits(b):
                pe.wait_ge(s_x2T, 2 * b + 2)
                if not (isint(b) and b == 0):
                    pe.wait_ge(s_carry, b + 2 if isint(b) and b > GROUPS[0] else b + 1)
                for t in range(NT):
                    i = pe.matmul(lgp[:, t, :], x2T[:, t * P:(t + 1) * P], Wr_sb[:, :], start=True, stop=True)
                i.then_inc(s_lg, 1)

            def ranks(b):
                pe.wait_ge(s_mm, b + 1)
                pe.matmul(lgp[:, :, :], before[:, :], mm[:, :, :], start=True, stop=False, skip_group_check=True)
                for k in range(1, NT):
                    pe.matmul(lgp[:, k:NT, :], onesb[:, :], mm[:, 0:NT - k, :], start=False, stop=(k == NT - 1), skip_group_check=True)
                for t in range(NT):
                    i = pe.matmul(cntp, onesb[:, :], mm[:, t, :], start=(t == 0), stop=(t == NT - 1), skip_group_check=True)
                i.then_inc(s_rank, 1)

            def ahead(nxt):
                xn_T(nxt[0])
                project(nxt[0])
                ei_rows(nxt[0])
                mask_T(nxt, 0)
                mask_T(nxt, 1)

            def attend(cur, fin, nxt, old):
                for jt in range(NT):
                    if cur:
                        weigh(cur[0], cur[1], jt)
                    batch, tile = following(cur, nxt, jt + 2)
                    if batch:
                        mask_T(batch, tile)
                    if nxt and jt == 1:
                        xn_T(nxt[0])
                    if nxt and jt == 2:
                        project(nxt[0])
                    if fin and jt == 3:
                        x2_T(fin[0], fin[1])
                    if fin and jt == 4:
                        logits(fin[0])
                    if nxt and jt == 4:
                        ei_rows(nxt[0])
                    if fin and jt == 6:
                        ranks(fin[0])

            stage1(pe, ahead, attend)

            def split_product(o, wh, wl, xh_, xl_, start, stop):
                pe.matmul(o, wh, xh_, start=start, stop=False)
                pe.matmul(o, wh, xl_, start=False, stop=False)
                return pe.matmul(o, wl, xh_, start=False, stop=stop)

            def rows_T(k, r):
                pe.wait_ge(s_xin[r], 16 * (k // 2 + 1) if isint(k) else 16 * half_of[0])
                if not (isint(k) and k == 0):
                    pe.wait_ge(s_xl, k)
                for t in range(TB):
                    i = pe.transpose(xTp[:, t * P:(t + 1) * P], xs[:, r, t, :], ident[:, :])
                i.then_inc(s_xT, 1)

            def up(k, r, c):
                if c == 0:
                    pe.wait_ge(s_w1[r], 32 * min(k // 2 + 1, LOADED // 2) if isint(k) else 32 * half_of[1])
                    pe.wait_ge(s_xl, k + 1)
                if not (isint(k) and k == 0):
                    pe.wait_ge(s_hf, NC * (k - 1) + c + 1)
                f = slice(c * P, (c + 1) * P)
                split_product(hps[c][:, :], w1[:, r, f], w1[:, r, F:][:, f], xh[:, r, :], xl[:, r, :], True, True).then_inc(s_hp, 1)

            def down(k, r, c):
                pe.wait_ge(s_hl, NC * k + c + 1)
                if c == 0:
                    pe.wait_ge(s_w2[r], 32 * min(k // 2 + 1, LOADED // 2) if isint(k) else 32 * half_of[2])
                    if not (isint(k) and k < 2):
                        pe.wait_ge(s_yTs, k - 1)
                f = slice(c * P, (c + 1) * P)
                i = split_product(yTp[r][:, :], w2[:, r, f], w2[:, r, F:][:, f], hh[:, r, c, :], hl[:, r, c, :], c == 0, c == NC - 1)
                if c == NC - 1:
                    i.then_inc(s_yT, 1)

            def rows_back(k):
                pe.wait_ge(s_yTs, k + 1)
                if not (isint(k) and k == 0):
                    pe.wait_ge(s_ys, k)
                for t in range(TB):
                    i = pe.transpose(yRp[:, t * P:(t + 1) * P], yTs[:, t * P:(t + 1) * P], ident[:, :])
                i.then_inc(s_yR, 1)

            half_of = [None, None, None]

            def step(k, r, shared=None):
                static = isint(k)
                if static and k == 2:
                    pe.wait_ge(s_carry, NB + 2)
                for c in range(NC):
                    if not static or k < NTILES:
                        up(k, r, c)
                    if c == 1 and (k + 1 < PART0[2] if static else not shared):
                        rows_T(k + 1, 1 - r)
                    if c == 2 and (not static or k >= 2):
                        rows_back(k - 2)
                    if not static or 1 <= k <= NTILES:
                        down(k - 1, 1 - r, c)
                    if static and k < 2:
                        last_batch(k, c)

            def last_batch(k, c):
                if k == 0 and c == 3:
                    x2_T(NB - 1, (NB - 1) % 2)
                if k == 1 and c == 0:
                    logits(NB - 1)
                if k == 1 and c == 2:
                    ranks(NB - 1)

            def pair(m, first):
                loaded = LOADED // 2
                all_there = 2 * first + 2 >= LOADED
                half_of[:] = [m + 2] + ([loaded] * 2 if all_there else [m + 2, m + 1])
                step(2 * m + 2, 0, 2 * first + 3 >= PART0[2])
                half_of[:] = [m + 3] + ([loaded] * 2 if all_there else [m + 2, m + 2])
                step(2 * m + 3, 1, 2 * first + 4 >= PART0[2])

            pe.wait_ge(s_E1, 2 * NB)
            pe.wait_ge(s_x2T, 2 * (NB - 1))
            rows_T(0, 0)
            pe.wait_ge(s_PT, NB * NT)
            pe.wait_ge(s_res, 3 * NB)
            stage2(step, lambda: pairs(pe, pair, [LOADED // 2 - 1] + COLS_CUTS))

        @block.scalar
        def _(act):
            def copy(o, i):
                return act.activation(o, i, ACT.Copy)

            act.wait_ge(s_wt, 1)
            copy(WTa[:, 0:D], tp[0][:, 0:P])
            copy(WTa[:, D:D + 1], ws[:, 1:2])
            copy(wi[:, :], ws[:, 0:1]).then_inc(s_wcopy, 1)
            act.wait_ge(s_bT, 1)
            copy(b1t[:, :, :], tp[1][:, 0:(E + 1) * NC].rearrange("p (e c) -> p e c", c=NC))
            copy(b2t[:, :], tp[1][:, (E + 1) * NC:NBR]).then_inc(s_btab, 1)
            act.wait_ge(s_wcopy, 1)
            act.activation(wirep[:, :], onesf[:, :], ACT.Copy, scale=wi[:, :]).then_inc(s_wirep, 1)

            def normalize(src, dst, L, tiles):
                alone(act)
                for t in tiles:
                    i = act.activation(dst(t), src(t), ACT.Identity, bias=L(3, t), scale=L(7, t))
                return i

            def norm1(b, h):
                act.wait_ge(s_rstd[0], b + 1 if isint(b) and b < 3 else len(LN1))
                if not (isint(b) and b == 0):
                    act.wait_ge(s_xnt, 2 * b)
                normalize(lambda t: res[:, b * NT + t, :], lambda t: xn[:, t, :], lambda i, t: ln1[:, i, bass.ds(b * NT + t, 1)],
                          range(h * NT // 2, (h + 1) * NT // 2)).then_inc(s_xn, 1)

            def norm2(b, q, half):
                act.wait_ge(s_rstd[1], b + 1)
                if not (isint(half) and half == 0):
                    act.wait_ge(s_scat[q], 16 * 2 * NT * half)
                normalize(lambda t: res[:, b * NT + t, :], lambda t: xn2[:, q, t, :], lambda i, t: ln2[:, i, t:t + 1],
                          range(NT // 2, NT)).then_inc(s_xn2[1], 1)

            def xn_copy(b):
                if not (isint(b) and b == 0):
                    act.wait_ge(s_ei, 2 * b)
                for h in range(2):
                    act.wait_ge(s_xnt, 2 * b + h + 1)
                    copy(xnT[:, h * H:(h + 1) * H], tp[h][:, :]).then_inc(s_xnT, 1)

            def wh_copy(b, q):
                if not (isint(b) and b < 2):
                    act.wait_ge(s_at, NT * (b - 1))
                for g in range(3):
                    act.wait_ge(s_Whp, 3 * b + g + 1)
                    n = min(3, NT - 3 * g)
                    copy(WhA[:, q, 3 * g:3 * g + n, 0:D], whp[g][:, 0:n, 0:D])
                    copy(ejc[:, q, 3 * g:3 * g + n], whp[g][:, 0:n, D]).then_inc(s_Whc, 1)

            def factors(b, q):
                act.wait_ge(s_M, b + 1)
                act.activation(cM[:, :], coefM[:, :], ACT.Copy, scale=Mb[:, 0:1]).then_inc(s_cM, 1)
                act.wait_ge(s_cM, b + 1)
                if not (isint(b) and b < 2):
                    act.wait_ge(s_PT, NT * (b - 1))
                act.activation(Bc[:, q, :], ejc[:, q, :], ACT.Exp, bias=cM[:, 0:1]).then_inc(s_B, 1)
                act.activation(Dc[:, q, :], ejc[:, q, :], ACT.Exp, bias=cM[:, 1:2], scale=SLOPE)
                act.wait_ge(s_B, b + 1)
                act.activation(nBc[:, q, :], Bc[:, q, :], ACT.Copy, scale=-1.0).then_inc(s_nB, 1)

            def row_factor(b, q):
                for h in range(2):
                    act.wait_ge(s_ei, 2 * b + h + 1)
                    act.activation(crow[:, q, h * H:(h + 1) * H], tp[h][:, :], ACT.Relu, bias=cM[:, 2:3],
                                   scale=1.0 - SLOPE).then_inc(s_E1, 1)
                act.wait_ge(s_E1, 2 * b + 2)
                act.activation(crow[:, q, :], crow[:, q, :], ACT.Exp, scale=-1.0).then_inc(s_crow, 1)

            def over(batch, jt):
                b, q, half = batch
                n = NT * b + jt
                if jt == 0:
                    act.wait_ge(s_crow, b + 1)
                    act.wait_ge(s_nB, b + 1)
                if not (isint(n) and n < 2):
                    act.wait_ge(s_PT, n - 1)
                act.activation(R[:, jt % 2, :], crow[:, q, :], ACT.Relu, bias=nBc[:, q, jt:jt + 1],
                               scale=Dc[:, q, jt:jt + 1]).then_inc(s_R, 1)

            def x2_copy(b, q, half):
                if not (isint(b) and b == 0):
                    act.wait_ge(s_lg, b)
                    act.wait_ge(s_shx[1 - q], 16 * (half + q))
                for h in range(2):
                    act.wait_ge(s_xn2t, 2 * b + h + 1)
                    last = isint(b) and b == NB - 1
                    copy(x2T[:, h * H:(h + 1) * H], tp[1 if last else h][:, :]).then_inc(s_x2T, 1)

            def gate_exp():
                act.wait_ge(s_dm, NB)
                act.activation(ed[:, :], dm[:, :], ACT.Exp).then_inc(s_ed, 1)

            def split_weights(e):
                act.wait_ge(s_wraw[e % 2], 32 * (e // 2 + 1))
                if e >= 2:
                    act.wait_ge(s_wst[e % 2], 16 * (e // 2))
                copy(wst[:, e % 2, :, 0:F], wraw[:, e % 2, :, :]).then_inc(s_whi, 1)

            SPLITS = [(0, 1), (0, 3), (0, 5), (0, 7), (1, 3), (1, 5), (1, 7), (2, 1), (2, 3)]
            assert len(SPLITS) == E + 1

            def ahead(nxt):
                b, q, half = nxt
                norm1(b, 0)
                norm1(b, 1)
                xn_copy(b)
                wh_copy(b, q)
                factors(b, q)
                row_factor(b, q)
                over(nxt, 0)
                over(nxt, 1)

            def attend(cur, fin, nxt, old):
                for jt in range(NT):
                    batch, tile = following(cur, nxt, jt + 2)
                    if batch:
                        over(batch, tile)
                    if nxt and jt < 2:
                        norm1(nxt[0], jt)
                    if nxt and jt == 2:
                        xn_copy(nxt[0])
                    if nxt and jt == 3:
                        wh_copy(nxt[0], nxt[1])
                    if fin and jt == 3:
                        norm2(*fin)
                    if fin and jt == 4:
                        x2_copy(*fin)
                    if nxt and jt == 4:
                        factors(nxt[0], nxt[1])
                    if nxt and jt == 5:
                        row_factor(nxt[0], nxt[1])
                    if isint(cur[0]) and (cur[0], jt) in SPLITS:
                        split_weights(SPLITS.index((cur[0], jt)))

            stage1(act, ahead, attend)

            def x_high(k, r, loads, shared=False):
                if shared:
                    act.wait_ge(s_xin[r], 16 * loads)
                    alone(act)
                else:
                    act.wait_ge(s_xT, k + 1)
                if not (isint(k) and k < 2):
                    act.wait_ge(s_hp, NC * (k - 1))
                copy(xh[:, r, :], xs[:, r, :, :].rearrange("p k d -> p (k d)") if shared else xTp[:, :]).then_inc(s_xh, 1)

            def gelu(k, r, c):
                act.wait_ge(s_hp, NC * k + c + 1)
                if not (isint(k) and k == 0):
                    act.wait_ge(s_hl, NC * (k - 1) + c + 1)
                act.activation(hf[:, c, :], hps[c][:, :], ACT.Gelu, bias=b1[:, r, c:c + 1]).then_inc(s_hf, 1)

            def h_high(k, r, c):
                act.wait_ge(s_hf, NC * k + c + 1)
                if c == 1 and not (isint(k) and k < 2):
                    act.wait_ge(s_yT, k - 1)
                copy(hh[:, r, c, :], hf[:, c, :]).then_inc(s_hh1, 1)

            def result(k, r):
                act.wait_ge(s_yT, k + 1)
                if not (isint(k) and k == 0):
                    act.wait_ge(s_yR, k)
                act.activation(yTs[:, :], yTp[r][:, :], ACT.Identity, bias=b2[:, r, :]).then_inc(s_yTs, 1)

            def rows_out(k, r, half, part):
                if part < 2:
                    act.wait_ge(s_yR, k + 1)
                    if not (isint(k) and k < 2):
                        act.wait_ge(s_yst[r], 16 * half)
                    copy(ys[:, r, :, :], yRp[:, :].rearrange("p (t d) -> p t d", d=D)).then_inc(s_ys, 1)

            def step(k, r, half, part=None, shared=None):
                static = isint(k)
                if not static or 2 <= k:
                    result(k - 2, r)
                for c in range(NC):
                    if not static or k < NTILES:
                        gelu(k, r, c)
                    if c % 2 == 1 and (not static or k < NTILES):
                        h_high(k, r, c)
                    if c == 1 and (not static or k + 1 < NTILES):
                        x_high(k + 1, 1 - r, (k + 1) // 2 + 1 if static else half + 1 + r, k + 1 >= PART0[2] if static else shared)
                    if c == 3 and (not static or k >= 2):
                        rows_out(k - 2, r, half - 1, part_of(k - 2) if static else part)
                    if static and k < 2:
                        last_batch(k, c)

            def last_batch(k, c):
                if k == 0 and c == 1:
                    norm2(NB - 1, (NB - 1) % 2, NB // 2 - 1)
                if k == 0 and c == 3:
                    x2_copy(NB - 1, (NB - 1) % 2, NB // 2 - 1)
                if k == 1 and c == 2:
                    gate_exp()

            def pair(m, first):
                for r in range(2):
                    step(2 * m + 2 + r, r, m + 1, part_of(2 * first + r), 2 * first + 3 + r >= PART0[2])

            x_high(0, 0, 1)
            stage2(lambda k, r: step(k, r, k // 2), lambda: pairs(act, pair, [GT[0] // 2, (GT[0] + 1) // 2, SHARED_PAIR] + COLS_CUTS))

        @block.vector
        def _(dve):

            def ln_sums(k, n, S, L):
                dve.wait_ge(s_stat[k], n + 1)
                dve.tensor_tensor(L(0), S(1), S(4), ALU.add)
                dve.tensor_tensor(L(1), S(1), S(4), ALU.subtract)
                dve.tensor_tensor(L(2), S(2), S(5), ALU.add).then_inc(s_lnsum[k], 1)
                dve.wait_ge(s_lnsum[k], n + 1)
                dve.tensor_scalar(L(5), L(0), -0.5, None, ALU.mult)
                dve.tensor_tensor(L(3), L(1), L(1), ALU.mult).then_inc(s_lnsq[k], 1)
                dve.wait_ge(s_lnsq[k], n + 1)
                dve.scalar_tensor_tensor(L(4), L(3), D / 4.0, L(2), ALU.mult, ALU.add).then_inc(s_var[k], 1)

            def norm1_stats(group, part=0, parts=1):
                lo, hi = (b * NT for b in LN1[group])
                n = (hi - lo) // parts
                for t in range(lo + part * n, lo + (part + 1) * n):
                    if t % NT == 0 or t == lo + part * n:
                        b = t // NT
                        dve.wait_ge(s_x[b % 2], 16 * (b // 2 + 1))
                    i = dve.bn_stats(stat1[:, t, :], res[:, t, :])
                if part == parts - 1:
                    i.then_inc(s_stat[0], 1)
                    ln_sums(0, group, lambda i: stat1[:, lo:hi, i], lambda i: ln1[:, i, lo:hi])

            def mask(b, q, half, k):
                dve.wait_ge(s_adj[q][k], 16 * (half + 1))
                part = adjm[:, q, k * NT // 2:(k + 1) * NT // 2, :]
                dve.tensor_scalar(part, part, 0.0, None, ALU.not_equal).then_inc(s_msk, 1)

            def largest(b, q):
                dve.wait_ge(s_Whc, 3 * b + 3)
                if not (isint(b) and b == 0):
                    dve.wait_ge(s_M, b)
                dve.tensor_reduce(mx[:, :], ejc[:, q, :], AX, ALU.max).then_inc(s_mx, 1)

            def soft(batch, jt):
                b, q, half = batch
                n = NT * b + jt
                dve.wait_ge(s_R, n + 1)
                dve.wait_ge(s_mT, n + 1)
                if not (isint(n) and n < 2):
                    dve.wait_ge(s_at, n - 1)
                dve.scalar_tensor_tensor(PT[:, jt % 2, :], R[:, jt % 2, :], Bc[:, q, jt:jt + 1], mT[jt % 2], ALU.add, ALU.mult).then_inc(s_PT, 1)

            def residual(b):
                for g in range(3):
                    if g < 2:
                        dve.wait_ge(s_bank, 2 * b + g + 1)
                    else:
                        dve.wait_ge(s_at, NT * (b + 1))
                    n = min(3, NT - 3 * g)
                    dve.tensor_scalar(dens[:, g, 0:n], at[g][:, 0:n, D], TINY, None, ALU.max).then_inc(s_den, 1)
                    dve.wait_ge(s_den, 3 * b + g + 1)
                    dve.reciprocal(rden[:, g, 0:n], dens[:, g, 0:n]).then_inc(s_rden, 1)
                    dve.wait_ge(s_rden, 3 * b + g + 1)
                    for t in range(3 * g, 3 * g + n):
                        i = dve.scalar_tensor_tensor(res[:, b * NT + t, :], at[g][:, t % 3, 0:D], rden[:, g, t % 3:t % 3 + 1],
                                                     res[:, b * NT + t, :], ALU.mult, ALU.add)
                    i.then_inc(s_res, 1)

            def norm2_stats(b):
                dve.wait_ge(s_res, 3 * b + 3)
                alone(dve)
                for t in range(NT):
                    i = dve.bn_stats(stat2[:, t, :], res[:, b * NT + t, :])
                i.then_inc(s_stat[1], 1)
                ln_sums(1, b, lambda i: stat2[:, :, i], lambda i: ln2[:, i, :])

            def norm2(b, q, half):
                dve.wait_ge(s_rstd[1], b + 1)
                if not (isint(half) and half == 0):
                    dve.wait_ge(s_scat[q], 16 * 2 * NT * half)
                for t in range(NT // 2):
                    i = dve.tensor_scalar(xn2[:, q, t, :], res[:, b * NT + t, :], ln2[:, 5, t:t + 1], ln2[:, 7, t:t + 1], ALU.add, ALU.mult)
                i.then_inc(s_xn2[0], 1)

            def over_e(v):
                return v.rearrange("p (t a) -> p t a", a=1).broadcast_to([P, NT, E])

            def route(b, choices):
                def link(i, n):
                    i.then_inc(s_route, 1)
                    dve.wait_ge(s_route, 10 * b + n)
                if choices[0] == 0:
                    dve.wait_ge(s_lg, b + 1)
                    link(dve.tensor_copy(Ls[:, 0, :, :], lgp), 1)
                for c in choices:
                    link(dve.tensor_reduce(m12[:, c, :], Ls[:, c, :, :], AX, ALU.max), 5 * c + 2)
                    link(dve.tensor_tensor(eq[:, :, :], Ls[:, c, :, :], over_e(m12[:, c, :]), ALU.is_equal), 5 * c + 3)
                    link(dve.scalar_tensor_tensor(cand[:, :, :], eq[:, :, :], -float(E), iota_e[:, :, :], ALU.mult, ALU.add), 5 * c + 4)
                    link(dve.tensor_reduce(first[:, :], cand[:, :, :], AX, ALU.min), 5 * c + 5)
                    dve.tensor_copy(choice[:, c, bass.ds(b * NT, NT)], first[:, :])
                    if c == 0:
                        dve.tensor_tensor(oh[:, c, :, :], cand[:, :, :], over_e(first[:, :]), ALU.is_equal).then_inc(s_oh, 1)
                        dve.wait_ge(s_oh, 2 * b + 1)
                        link(dve.scalar_tensor_tensor(Ls[:, 1, :, :], oh[:, 0, :, :], -HUGE, Ls[:, 0, :, :], ALU.mult, ALU.add), 6)
                    else:
                        dve.tensor_tensor(oh[:, c, :, :], cand[:, :, :], over_e(first[:, :]), ALU.is_equal).then_inc(s_oh, 1)
                        dve.wait_ge(s_oh, 2 * b + 2)
                        dve.tensor_tensor(mm[:, :, :], oh[:, 0, :, :], oh[:, 1, :, :], ALU.add).then_inc(s_mm, 1)
                        dve.tensor_tensor(dm[:, bass.ds(b * NT, NT)], m12[:, 1, :], m12[:, 0, :], ALU.subtract).then_inc(s_dm, 1)

            def queue(b, q):
                dve.wait_ge(s_rank, b + 1)
                start = carry[:, :].rearrange("p (a e) -> p a e", a=1).broadcast_to([P, NT, E])
                dve.tensor_tensor(pos[:, :, :], lgp, start, ALU.add).then_inc(s_pos, 1)
                dve.wait_ge(s_pos, b + 1)
                dve.tensor_tensor(carry[:, :], carry[:, :], cntp, ALU.add).then_inc(s_carry, 1)
                for c in range(2):
                    i = dve.tensor_tensor(hit[:, c, :, :], oh[:, c, :, :], pos[:, :, :], ALU.mult)
                i.then_inc(s_hit, 1)
                dve.wait_ge(s_hit, 2 * b + 1)
                dve.tensor_reduce(slotf[:, :, :], hit[:, :, :, :], AX, ALU.add).then_inc(s_hit, 1)
                dve.wait_ge(s_hit, 2 * b + 2)
                dve.tensor_copy(sslot[:, q, :, :], slotf[:, :, :])
                dve.tensor_copy(slotall[:, :, bass.ds(b * NT, NT)], slotf[:, :, :]).then_inc(s_slot, 1)

            def weights():
                dve.wait_ge(s_ed, 1)
                dve.tensor_scalar(ed1[:, :], ed[:, :], 1.0, None, ALU.add).then_inc(s_gate, 1)
                dve.wait_ge(s_gate, 1)
                dve.reciprocal(gates[:, 0, :], ed1[:, :]).then_inc(s_gate, 1)
                dve.wait_ge(s_gate, 2)
                dve.tensor_tensor(gates[:, 1, :], ed[:, :], gates[:, 0, :], ALU.mult).then_inc(s_gate, 1)

            steps = [0]

            def link(i):
                i.then_inc(s_tstep, 1)
                steps[0] += 1
                dve.wait_ge(s_tstep, steps[0])

            def counts(g):
                dve.wait_ge(s_carry, 1 + sum(GROUPS[:g + 1]) + g)
                rowc = carry[:, :]
                link(dve.tensor_copy(tab_tail[:, g, :], rowc))
                link(dve.tensor_tensor(cnt[:, g, 0, :], rowc, base[:, g, :], ALU.subtract))
                link(dve.tensor_scalar(nti[:, 0, :], cnt[:, g, 0, :], float(T - 1), None, ALU.add))
                link(dve.tensor_scalar(nti[:, 1, :], nti[:, 0, :], TSH, None, ALU.arith_shift_right))
                link(dve.tensor_copy(cnt[:, g, 1, :], nti[:, 1, :]))
                link(dve.tensor_tensor_scan(cnt[:, g, 2, :], cnt[:, g, 1, :], zero_e[:, :], 0.0, ALU.add, ALU.add))

            def tables(g):
                n = GT[g]
                t0 = PART0[g]

                def over_t(v):
                    return v.rearrange("p (a e) -> p a e", a=1).broadcast_to([P, n, E])
                link(dve.tensor_tensor(tge[:, 0, 0:n, :], iota_t[:, 0:n, :], over_t(cnt[:, g, 2, :]), ALU.is_ge))
                link(dve.tensor_tensor(tge[:, 1, 0:n, :], tge[:, 0, 0:n, :], over_t(cnt[:, g, 1, :]), ALU.mult))
                link(dve.tensor_reduce(tv[:, 0, 0:n], tge[:, 0, 0:n, :], AX, ALU.add))
                link(dve.tensor_reduce(tv[:, 1, 0:n], tge[:, 1, 0:n, :], AX, ALU.add))
                link(dve.tensor_tensor(tv[:, 2, 0:n], iota_t[:, 0:n, 0], tv[:, 1, 0:n], ALU.subtract))
                link(dve.tensor_scalar(tv[:, 3, 0:n], tv[:, 0, 0:n], float(REG[g]), float(GBASE[g]), ALU.mult, ALU.add))
                link(dve.scalar_tensor_tensor(tv[:, 4, 0:n], tv[:, 2, 0:n], float(T), tv[:, 3, 0:n], ALU.mult, ALU.add))
                link(dve.tensor_scalar(tab_x[:, t0:t0 + n], tv[:, 4, 0:n], float(GBASE[g] + E * REG[g]), None, ALU.min))
                dve.tensor_scalar(tab_e[:, t0:t0 + n], tv[:, 0, 0:n], float(E - 1), None, ALU.min).then_inc(s_tab, 1)
                dve.tensor_copy(carry[:, :], base[:, 1, :]).then_inc(s_carry, 1)

            def ahead(nxt):
                b, q, half = nxt
                norm1_stats(0)
                dve.wait_ge(s_const, 1)
                dve.tensor_copy(carry[:, :], base[:, 0, :]).then_inc(s_carry, 1)
                for k in range(2):
                    mask(b, q, half, k)
                largest(b, q)
                soft(nxt, 0)

            def attend(cur, fin, nxt, old):
                if fin:
                    residual(fin[0])
                for jt in range(NT):
                    batch, tile = following(cur, nxt, jt + 1)
                    if batch:
                        soft(batch, tile)
                    if fin and jt == 0:
                        norm2_stats(fin[0])
                    if fin and jt == 2:
                        norm2(*fin)
                    if not nxt and jt == 2:
                        tables(0)
                    if old and jt == 1:
                        queue(old[0], old[1])
                    if not nxt and jt == 1:
                        counts(0)
                    if nxt and jt == 3:
                        mask(*nxt, 0)
                        largest(nxt[0], nxt[1])
                    if nxt and jt == 4:
                        mask(*nxt, 1)
                    if fin and jt == 4:
                        route(fin[0], [0])
                    if fin and jt == 5:
                        route(fin[0], [1])
                    if not fin:
                        if jt == 0:
                            norm1_stats(1)
                        elif jt < 7:
                            norm1_stats(2 + jt // 4, (jt - 1) % 3, 3)

            stage1(dve, ahead, attend)

            def x_low(k, r, shared=False):
                dve.wait_ge(s_xh, k + 1)
                if not (isint(k) and k < 2):
                    dve.wait_ge(s_hp, NC * (k - 1))
                dve.tensor_tensor(xl[:, r, :], xs[:, r, :, :].rearrange("p k d -> p (k d)") if shared else xTp[:, :], xh[:, r, :].bitcast(F32), ALU.subtract).then_inc(s_xl, 1)

            def h_split(k, r, c):
                dve.wait_ge(s_hf, NC * k + c + 1)
                if c == 0 and not (isint(k) and k < 2):
                    dve.wait_ge(s_yT, k - 1)
                if c % 2 == 1:
                    dve.wait_ge(s_hh1, NC // 2 * k + c // 2 + 1)
                else:
                    dve.tensor_copy(hh[:, r, c, :], hf[:, c, :]).then_inc(s_hh, 1)
                    dve.wait_ge(s_hh, NC // 2 * k + c // 2 + 1)
                dve.tensor_tensor(hl[:, r, c, :], hf[:, c, :], hh[:, r, c, :].bitcast(F32), ALU.subtract).then_inc(s_hl, 1)

            def shared_out(k, r, half):
                c = k - PART0[2]
                dve.wait_ge(s_yR, k + 1)
                y = yRp[:, :].rearrange("p (t d) -> p t d", d=D)
                nodes = res[:, bass.ds(c * COMB, COMB), :]
                if isint(k) and c >= SHARED_LAST:
                    if c == SHARED_LAST:
                        dve.wait_ge(s_ob, c + 1)
                    dve.tensor_tensor(nodes, y, nodes, ALU.add).then_inc(s_rsum, 1)
                    dve.wait_ge(s_rsum, c - SHARED_LAST + 1)
                    dve.sem_inc(s_ys, 1)
                else:
                    dve.wait_ge(s_ot, c + 1)
                    dve.wait_ge(s_yst[r], 16 * half)
                    alone(dve)
                    dve.tensor_tensor(ys[:, r, :, :], y, nodes, ALU.add).then_inc(s_ys, 1)

            def step(k, r, half=None, part=None, shared=None):
                static = isint(k)
                if static:
                    half, part, shared = k // 2, part_of(k - 2), k + 1 >= PART0[2]
                for c in range(NC):
                    if not static or k < NTILES:
                        h_split(k, r, c)
                    if c == 1 and (not static or k + 1 < NTILES):
                        x_low(k + 1, 1 - r, shared)
                    if c == 2 and part == 2:
                        shared_out(k - 2, r, half - 1)
                    if static and k < 4:
                        last_batch(k, c)

            def last_batch(k, c):
                b, q = NB - 1, (NB - 1) % 2
                if k == 0 and c == 0:
                    norm2(b, q, NB // 2 - 1)
                if k == 0 and c == 1:
                    queue(b - 1, 1 - q)
                if k == 1 and c < 2:
                    route(b, [c])
                if k == 1 and c == 2:
                    queue(b, q)
                if k == 2 and c == 0:
                    counts(1)
                if k == 2 and c == 2:
                    tables(1)
                if k == 3 and c == 1:
                    weights()

            def combine_first(c):
                dve.wait_ge(s_gate, 3)
                if isint(c) and c == EARLY:
                    rows = g12_early
                    dve.wait_ge(s_g_early[0], 16 * COMB)
                else:
                    rows = g12
                    dve.wait_ge(s_g[0], 16 * COMB * (c if isint(c) and c > EARLY else c + 1))
                if isint(c) and c > SHARED_LAST:
                    dve.wait_ge(s_rsum, c - SHARED_LAST + 1)
                alone(dve)
                for i in range(COMB):
                    x = dve.scalar_tensor_tensor(res[:, c * COMB + i, :], rows[:, i, 0, :], gates[:, 0, bass.ds(c * COMB + i, 1)],
                                                 res[:, c * COMB + i, :], ALU.mult, ALU.add)
                x.then_inc(s_ob, 1)

            def combine_second(c):
                dve.wait_ge(s_ob, c + 1)
                if isint(c) and c == EARLY:
                    rows = g12_early
                    dve.wait_ge(s_g_early[1], 16 * COMB)
                else:
                    rows = g12
                    dve.wait_ge(s_g[1], 16 * COMB * (c if isint(c) and c > EARLY else c + 1))
                last = isint(c) and c >= SHARED_LAST
                if last:
                    dve.wait_ge(s_rsum, c - SHARED_LAST + 1)
                alone(dve)
                for i in range(COMB):
                    x = dve.scalar_tensor_tensor(ot[:, (c - SHARED_LAST) * COMB + i, :] if last else res[:, c * COMB + i, :],
                                                 rows[:, i, 1, :], gates[:, 1, bass.ds(c * COMB + i, 1)],
                                                 res[:, c * COMB + i, :], ALU.mult, ALU.add)
                x.then_inc(s_ot, 1)

            def pair(m, first):
                for r in range(2):
                    step(2 * m + 2 + r, r, m + 1, part_of(2 * first + r), 2 * first + 3 + r >= PART0[2])
                    if first >= COMB_PAIR:
                        (combine_first, combine_second)[r](m - COMB_PAIR)

            def loop():
                pairs(dve, pair, [COMB_PAIR, COMB_PAIR + 1, SHARED_PAIR] + COLS_CUTS)

            residual(NB - 1)
            norm2_stats(NB - 1)
            x_low(0, 0)

            def beside(k):
                i = k - (NTILES - 2)
                if i < 3:
                    (combine_first, combine_second)[i % 2](SHARED_LAST + i // 2)

            stage2(step, loop, beside)
            for c in range(ROUNDS - 2, ROUNDS):
                if c == ROUNDS - 1:
                    combine_first(c)
                combine_second(c)


_INS = ["x", "adj", "L0_gnn_W", "L0_gnn_a", "L0_ffn_Wr", "L0_ffn_W1s", "L0_ffn_b1s", "L0_ffn_W2s", "L0_ffn_b2s",
        "L0_ffn_W1p", "L0_ffn_b1p", "L0_ffn_W2p", "L0_ffn_b2p"]


def kernel(**inputs):
    import numpy as _np
    import concourse.bacc as _bacc
    from concourse import mybir as _mybir
    from concourse.bass_utils import run_bass_kernel_spmd as _run

    nc = _bacc.Bacc("TRN2", target_bir_lowering=False, num_devices=1)
    arrays, args = {}, []
    for name in _INS:
        a = _np.ascontiguousarray(inputs[name])
        arrays[f"in_{name}_dram"] = a
        args.append(nc.dram_tensor(f"in_{name}_dram", a.shape, _mybir.dt.from_np(a.dtype), kind="ExternalInput").ap())
    args.append(nc.dram_tensor("out_0_dram", inputs["x"].shape, _mybir.dt.float32, kind="ExternalOutput").ap())
    gnn_moe_layer(nc, *args)
    r = _run(nc, [arrays], core_ids=[0])
    return r.results[0]["out_0_dram"]
```
